# Optimizing a Trainium2 kernel written in Bass

```python
import numpy as np
import jax
import jax.numpy as jnp

def _softmax(x, axis=-1):
    return jax.nn.softmax(x, axis=axis)

def _gelu(x):
    return jax.nn.gelu(x, approximate=True)

def _silu(x):
    return jax.nn.silu(x)

def _sigmoid(x):
    return jax.nn.sigmoid(x)

def _layernorm(x, axis=-1, eps=1e-05):
    m = jnp.mean(x, axis=axis, keepdims=True)
    v = jnp.var(x, axis=axis, keepdims=True)
    return (x - m) / jnp.sqrt(v + eps)

def _scatter_add(tgt, idx, src, axis=0):
    return tgt.at[idx].add(src)

def _segment_sum(src, seg, n):
    return jax.ops.segment_sum(src, seg, n)
kernel_name = 'mk_decoder_preln_d1_seqx_r8_f275de'

def setup_inputs(seed: int=0):
    np.random.seed(seed)
    _w = jnp.asarray

    def _rec_inputs():
        import jax
        import jax.numpy as jnp
        _rk = jax.random.key(seed)
        x = 7.22e-05 + 1 * jax.random.normal(jax.random.fold_in(_rk, 1), (32, 64, 256), jnp.float32)
        _lenS = 64 - jax.random.randint(jax.random.fold_in(_rk, 7), (32,), 0, max(1, 64 // 4) + 1, jnp.int32)
        _lenS2 = 64 - jax.random.randint(jax.random.fold_in(_rk, 8), (32,), 0, max(1, 64 // 4) + 1, jnp.int32)
        _ctx_2048P = jax.random.normal(jax.random.fold_in(_rk, 11), (32, 16, 256), jnp.float32)
        _ctx_2048c = jax.random.dirichlet(jax.random.fold_in(_rk, 511), 0.3 * jnp.ones((16,), jnp.float32), (32, 64))
        _ctx_2048t = jnp.einsum('bsk,bkd->bsd', _ctx_2048c, _ctx_2048P)
        _ctx_2048t = _ctx_2048t * jax.lax.rsqrt(jnp.mean(jnp.square(_ctx_2048t)) + 1e-12) * 0.953939
        ctx_2048 = 4.13588e-05 + 0.999923 * (_ctx_2048t + 0.3 * jax.random.normal(jax.random.fold_in(_rk, 611), (32, 64, 256), jnp.float32))
        _validS = jnp.arange(64)[None, :] < _lenS[:, None]
        _validS2 = jnp.arange(64)[None, :] < _lenS2[:, None]
        _causal = jnp.tril(jnp.ones((64, 64), dtype=bool))
        mask_BxS2_bf1 = jnp.ones((32, 64), dtype=bool)
        return (x, ctx_2048, mask_BxS2_bf1)
    x, ctx_2048, mask_BxS2_bf1 = _rec_inputs()

    def _L0_attn_setup():
        import jax, jax.numpy as jnp
        import numpy as np
        D_MODEL = 256
        NUM_HEADS = 16
        D_K = D_MODEL // NUM_HEADS

        def _heads(t, B, S):
            return t.reshape(B, S, NUM_HEADS, D_K).transpose(0, 2, 1, 3)
        key = jax.random.key(seed)
        ks = jax.random.split(key, 9)
        s = 1.0 / np.sqrt(D_MODEL)
        x = jax.random.normal(ks[0], (4, 512, D_MODEL), dtype=jnp.float32)
        wq = jax.random.uniform(ks[1], (D_MODEL, D_MODEL), jnp.float32, -s, s)
        bq = jax.random.uniform(ks[2], (D_MODEL,), jnp.float32, -s, s)
        wk = jax.random.uniform(ks[3], (D_MODEL, D_MODEL), jnp.float32, -s, s)
        bk = jax.random.uniform(ks[4], (D_MODEL,), jnp.float32, -s, s)
        wv = jax.random.uniform(ks[5], (D_MODEL, D_MODEL), jnp.float32, -s, s)
        bv = jax.random.uniform(ks[6], (D_MODEL,), jnp.float32, -s, s)
        wo = jax.random.uniform(ks[7], (D_MODEL, D_MODEL), jnp.float32, -s, s)
        bo = jax.random.uniform(ks[8], (D_MODEL,), jnp.float32, -s, s)
        return {'x': x, 'wq': wq, 'bq': bq, 'wk': wk, 'bk': bk, 'wv': wv, 'bv': bv, 'wo': wo, 'bo': bo}
    _L0_attn_all = _L0_attn_setup()
    _L0_attn_in = {k: v for k, v in _L0_attn_all.items() if k in ('wq', 'bq', 'wk', 'bk', 'wv', 'bv', 'wo', 'bo')}
    del _L0_attn_all

    def _L0_xattn_setup():
        import jax, jax.numpy as jnp
        import numpy as np
        import math
        D_MODEL = 256
        N_Q_HEADS = 16
        N_KV_HEADS = 4
        HEAD_DIM = D_MODEL // N_Q_HEADS
        B = 4
        S = 128

        def _alibi_slopes(num_heads):
            n = 2 ** int(math.floor(math.log2(num_heads)))
            m0 = 2.0 ** (-8.0 / n)
            return m0 ** jnp.arange(1, n + 1, dtype=jnp.float32)
        key = jax.random.key(seed)
        ks = jax.random.split(key, 8)
        xavier = lambda k, fi, fo: jax.random.normal(k, (fi, fo), jnp.float32) * math.sqrt(2.0 / (fi + fo))
        return {'query': jax.random.normal(ks[0], (B, S, D_MODEL), jnp.float32), 'key': jax.random.normal(ks[1], (B, S, D_MODEL), jnp.float32), 'value': jax.random.normal(ks[2], (B, S, D_MODEL), jnp.float32), 'mask': jnp.ones((B, S), dtype=bool), 'Wq': xavier(ks[3], D_MODEL, N_Q_HEADS * HEAD_DIM), 'Wk': xavier(ks[4], D_MODEL, N_KV_HEADS * HEAD_DIM), 'Wv': xavier(ks[5], D_MODEL, N_KV_HEADS * HEAD_DIM), 'Wo': xavier(ks[6], D_MODEL, D_MODEL)}
    _L0_xattn_all = _L0_xattn_setup()
    _L0_xattn_in = {k: v for k, v in _L0_xattn_all.items() if k in ('Wq', 'Wk', 'Wv', 'Wo')}
    del _L0_xattn_all

    def _L0_ffn_setup():
        import jax, jax.numpy as jnp
        import numpy as np
        B, L, D = (2, 128, 256)
        E, K = (8, 2)
        H, HS = (176, 352)
        key = jax.random.key(seed)
        ks = jax.random.split(key, 9)
        s = 0.02
        return {'x': jax.random.normal(ks[0], (B, L, D), dtype=jnp.float32), 'gate_w': jax.random.normal(ks[1], (E, D), dtype=jnp.float32) * s, 'w_gate': jax.random.normal(ks[2], (E, D, H), dtype=jnp.float32) * s, 'w_up': jax.random.normal(ks[3], (E, D, H), dtype=jnp.float32) * s, 'w_down': jax.random.normal(ks[4], (E, H, D), dtype=jnp.float32) * s, 'shgate_w': jax.random.normal(ks[5], (D,), dtype=jnp.float32) * s, 'shw_gate': jax.random.normal(ks[6], (D, HS), dtype=jnp.float32) * s, 'shw_up': jax.random.normal(ks[7], (D, HS), dtype=jnp.float32) * s, 'shw_down': jax.random.normal(ks[8], (HS, D), dtype=jnp.float32) * s}
    _L0_ffn_all = _L0_ffn_setup()
    _L0_ffn_in = {k: v for k, v in _L0_ffn_all.items() if k in ('gate_w', 'w_gate', 'w_up', 'w_down', 'shgate_w', 'shw_gate', 'shw_up', 'shw_down')}
    del _L0_ffn_all
    return {'x': x, 'ctx_2048': ctx_2048, 'mask_BxS2_bf1': mask_BxS2_bf1, 'L0_attn_wq': _L0_attn_in['wq'], 'L0_attn_bq': _L0_attn_in['bq'], 'L0_attn_wk': _L0_attn_in['wk'], 'L0_attn_bk': _L0_attn_in['bk'], 'L0_attn_wv': _L0_attn_in['wv'], 'L0_attn_bv': _L0_attn_in['bv'], 'L0_attn_wo': _L0_attn_in['wo'], 'L0_attn_bo': _L0_attn_in['bo'], 'L0_xattn_Wq': _L0_xattn_in['Wq'], 'L0_xattn_Wk': _L0_xattn_in['Wk'], 'L0_xattn_Wv': _L0_xattn_in['Wv'], 'L0_xattn_Wo': _L0_xattn_in['Wo'], 'L0_ffn_gate_w': _L0_ffn_in['gate_w'], 'L0_ffn_w_gate': _L0_ffn_in['w_gate'], 'L0_ffn_w_up': _L0_ffn_in['w_up'], 'L0_ffn_w_down': _L0_ffn_in['w_down'], 'L0_ffn_shgate_w': _L0_ffn_in['shgate_w'], 'L0_ffn_shw_gate': _L0_ffn_in['shw_gate'], 'L0_ffn_shw_up': _L0_ffn_in['shw_up'], 'L0_ffn_shw_down': _L0_ffn_in['shw_down']}

def reference(x, ctx_2048, mask_BxS2_bf1, L0_attn_wq, L0_attn_bq, L0_attn_wk, L0_attn_bk, L0_attn_wv, L0_attn_bv, L0_attn_wo, L0_attn_bo, L0_xattn_Wq, L0_xattn_Wk, L0_xattn_Wv, L0_xattn_Wo, L0_ffn_gate_w, L0_ffn_w_gate, L0_ffn_w_up, L0_ffn_w_down, L0_ffn_shgate_w, L0_ffn_shw_gate, L0_ffn_shw_up, L0_ffn_shw_down):
    import jax
    import jax.numpy as jnp

    def _L0_attn_ref(x, wq, bq, wk, bk, wv, bv, wo, bo):
        import jax, jax.numpy as jnp
        import numpy as np
        D_MODEL = 256
        NUM_HEADS = 16
        D_K = D_MODEL // NUM_HEADS

        def _heads(t, B, S):
            return t.reshape(B, S, NUM_HEADS, D_K).transpose(0, 2, 1, 3)
        B, S, _ = x.shape
        Q = _heads(x @ wq.T + bq, B, S)
        K = _heads(x @ wk.T + bk, B, S)
        V = _heads(x @ wv.T + bv, B, S)
        Q = jax.nn.elu(Q) + 1.0
        K = jax.nn.elu(K) + 1.0
        KV = jnp.einsum('bhsd,bhse->bhde', K, V)
        QKV = jnp.einsum('bhsd,bhde->bhse', Q, KV)
        K_sum = jnp.sum(K, axis=-2)
        QK_sum = jnp.einsum('bhsd,bhd->bhs', Q, K_sum)
        out = QKV / (QK_sum[..., None] + 1e-08)
        out = out.transpose(0, 2, 1, 3).reshape(B, S, D_MODEL)
        return out @ wo.T + bo

    def _L0_xattn_ref(query, key, value, mask, Wq, Wk, Wv, Wo):
        import jax, jax.numpy as jnp
        import numpy as np
        import math
        D_MODEL = 256
        N_Q_HEADS = 16
        N_KV_HEADS = 4
        HEAD_DIM = D_MODEL // N_Q_HEADS
        B = 4
        S = 128

        def _alibi_slopes(num_heads):
            n = 2 ** int(math.floor(math.log2(num_heads)))
            m0 = 2.0 ** (-8.0 / n)
            return m0 ** jnp.arange(1, n + 1, dtype=jnp.float32)
        b, q_len, d = query.shape
        kv_len = key.shape[1]
        G = N_KV_HEADS
        Hpg = N_Q_HEADS // G
        dh = HEAD_DIM
        Q = (query @ Wq).reshape(b, q_len, G, Hpg, dh)
        K = (key @ Wk).reshape(b, kv_len, G, dh)
        V = (value @ Wv).reshape(b, kv_len, G, dh)
        Q = Q / math.sqrt(dh)
        scores = jnp.einsum('bqghd,bkgd->bghqk', Q, K)
        rel = jnp.arange(kv_len, dtype=jnp.float32)[None, :] - jnp.arange(q_len, dtype=jnp.float32)[:, None]
        m = _alibi_slopes(N_Q_HEADS).reshape(1, G, Hpg, 1, 1)
        scores = scores + m * rel[None, None, None]
        neg = jnp.finfo(scores.dtype).min
        scores = jnp.where(mask[:, None, None, None, :], scores, neg)
        w = jax.nn.softmax(scores, axis=-1)
        out = jnp.einsum('bghqk,bkgd->bqghd', w, V)
        out = out.reshape(b, q_len, G * Hpg * dh)
        return out @ Wo

    def _L0_ffn_ref(x, gate_w, w_gate, w_up, w_down, shgate_w, shw_gate, shw_up, shw_down):
        import jax, jax.numpy as jnp
        import numpy as np
        B, L, D = (2, 128, 256)
        E, K = (8, 2)
        H, HS = (176, 352)
        b, l, d = x.shape
        xf = x.reshape(-1, d)
        logits = jnp.einsum('td,ed->te', xf.astype(jnp.float32), gate_w)
        probs = jax.nn.softmax(logits.astype(jnp.float32), axis=-1)
        weights, indices = jax.lax.top_k(probs, K)
        weights = (weights / weights.sum(-1, keepdims=True)).astype(x.dtype)
        onehot = jax.nn.one_hot(indices, E, dtype=x.dtype)
        combine = jnp.einsum('tk,tke->te', weights, onehot)
        g = jnp.einsum('td,edh->teh', xf, w_gate)
        u = jnp.einsum('td,edh->teh', xf, w_up)
        h = jax.nn.silu(g) * u
        out = jnp.einsum('teh,ehd,te->td', h.astype(jnp.float32), w_down.astype(jnp.float32), combine.astype(jnp.float32))
        sgate = jax.nn.sigmoid(xf @ shgate_w)[:, None]
        sh = jax.nn.silu(xf @ shw_gate) * (xf @ shw_up) @ shw_down
        out = out + (sgate * sh).astype(jnp.float32)
        return out.astype(x.dtype).reshape(b, l, d)
    x = x + _L0_attn_ref(_layernorm(x, axis=-1), L0_attn_wq, L0_attn_bq, L0_attn_wk, L0_attn_bk, L0_attn_wv, L0_attn_bv, L0_attn_wo, L0_attn_bo)
    x = x + _L0_xattn_ref(_layernorm(x, axis=-1), ctx_2048, ctx_2048, mask_BxS2_bf1, L0_xattn_Wq, L0_xattn_Wk, L0_xattn_Wv, L0_xattn_Wo)
    x = x + _L0_ffn_ref(_layernorm(x, axis=-1), L0_ffn_gate_w, L0_ffn_w_gate, L0_ffn_w_up, L0_ffn_w_down, L0_ffn_shgate_w, L0_ffn_shw_gate, L0_ffn_shw_up, L0_ffn_shw_down)
    return x

_drawn_inputs = setup_inputs


def setup_inputs(seed=0):
    import zlib

    import numpy as np

    out = dict(_drawn_inputs(seed))
    spreads = {}
    factors = {'L0_attn_wq': 8.0,
     'L0_attn_bq': 64.0,
     'L0_attn_wk': 8.0,
     'L0_attn_bk': 168.439,
     'L0_attn_bv': 3.341,
     'L0_ffn_gate_w': 8.0,
     'L0_ffn_w_gate': 7.495,
     'L0_ffn_w_up': 7.4,
     'L0_ffn_w_down': 7.37,
     'L0_ffn_shgate_w': 8.0,
     'L0_ffn_shw_gate': 7.408,
     'L0_ffn_shw_up': 7.393,
     'L0_ffn_shw_down': 7.323}
    for name, (base, spread) in spreads.items():
        noise = np.random.default_rng([zlib.crc32(name.encode()), seed]).standard_normal(out[name].shape)
        drawn = base * np.exp(spread * noise) if base else spread * noise
        out[name] = jnp.asarray(drawn.astype(out[name].dtype))
    for name, factor in factors.items():
        out[name] = (out[name] * factor).astype(out[name].dtype)
    return out
```

```python
from contextlib import ExitStack

import numpy as np

import concourse.bass as bass
from concourse import mybir

F32 = mybir.dt.float32
U32 = mybir.dt.uint32
U8 = mybir.dt.uint8
ALU = mybir.AluOpType
ACT = mybir.ActivationFunctionType
AX = mybir.AxisListType

P = 128
B, S, D = 32, 64, 256
TILES = B * S // P
KC = D // P
HEADS, DH = 16, 16
GROUPS = 4
SEQS = P // S
HALF = HEADS // 2
NE, H = 8, 176
HC = H // 2
HS = 352
HS_LAST = HS - 2 * P
ROUTE = HS + NE + 1
LN_EPS = 1e-5
DEN_EPS = 1e-8
BIG = float(np.finfo(np.float32).max)


def wait(eng, sem, count):
    if isinstance(count, int) and count <= 0:
        return
    eng.wait_ge(sem, count)


def spread(ap, axis, n):
    shape = list(ap.shape)
    shape[axis] = n
    return ap.broadcast_to(shape)


def build(nc, a, out):
    with ExitStack() as ctx:
        def sb(name, shape, dt=F32):
            return ctx.enter_context(nc.sbuf_tensor(name, shape, dt))

        def sem(name):
            return ctx.enter_context(nc.semaphore(name))

        ident = sb("ident", [P, P])
        wq = sb("wq", [P, KC, D])
        wkv = sb("wkv", [P, KC, 2 * D])
        wo = sb("wo", [P, KC, D])
        bq1 = sb("bq1", [P, KC])
        bkv = sb("bkv", [P, 2 * D])
        bo = sb("bo", [P, D])
        xwq = sb("xwq", [P, KC, D])
        xwk = sb("xwk", [P, KC, GROUPS * DH])
        xwk_rep = sb("xwk_rep", [P, KC, GROUPS, HEADS // GROUPS, DH])
        xwv = sb("xwv", [P, KC, GROUPS * DH])
        xwo = sb("xwo", [P, KC, D])
        block_mask = sb("block_mask", [P, 32])
        row_head = sb("row_head", [P, 2])
        row_half = sb("row_half", [P, 2])
        alibi = sb("alibi", [P, HEADS * S])
        mask_u8 = sb("mask_u8", [P, TILES, S], U8)
        key_off = sb("key_off", [P, TILES, S])
        neg_half = sb("neg_half", [P, 1])
        eps = sb("eps", [P, 1])
        minus_one = sb("minus_one", [P, 1])
        iota8 = sb("iota8", [P, NE])
        w_route = sb("w_route", [P, KC, ROUTE])
        w_sh_up = sb("w_sh_up", [P, KC, HS])
        w_sh_down = sb("w_sh_down", [P, 3, D])
        w_gu = sb("w_gu", [P, NE, KC, 2 * H])
        w_down = sb("w_down", [HC, NE, 2, D])

        x_all = sb("x_all", [P, TILES, D])
        st1 = sb("st1", [P, 6])
        mv1 = sb("mv1", [P, 2])
        rs1 = sb("rs1", [P, 1])
        xn1 = sb("xn1", [P, D])
        xn1T = sb("xn1T", [P, KC, P])
        k1 = sb("k1", [P, D])
        ke = sb("ke", [P, D])
        kf = sb("kf", [P, D])
        vo = sb("vo", [P, HALF, 33])
        q1 = sb("q1", [P, KC, P])
        qe = sb("qe", [P, KC, P])
        qf = sb("qf", [P, KC, P])
        kv_bd = sb("kv_bd", [P, SEQS, 2, 32])
        ks_bd = sb("ks_bd", [P, SEQS, 2, 32])
        den = sb("den", [P, KC, P])
        rden = sb("rden", [P, KC, P])
        oT = sb("oT", [P, KC, P])
        ctx_sb = sb("ctx_sb", [P, D])
        st2 = sb("st2", [P, 6])
        mv2 = sb("mv2", [P, 2])
        rs2 = sb("rs2", [P, 1])
        xn2 = sb("xn2", [P, D])
        xcT = sb("xcT", [P, 2 * KC, P])
        q2T = sb("q2T", [P, KC, P])
        k_bd = sb("k_bd", [P, 2, 2, P])
        v_bd = sb("v_bd", [P, SEQS * GROUPS, 2, DH])
        bias_t = sb("bias_t", [P, HEADS * S])
        sc = sb("sc", [P, HEADS * S])
        smax = sb("smax", [P, HEADS])
        pr = sb("pr", [P, HEADS * S])
        ssum = sb("ssum", [P, HEADS])
        rsum = sb("rsum", [P, HEADS])
        prT = sb("prT", [P, 8, P])
        o2T = sb("o2T", [P, KC, P])
        st3 = sb("st3", [P, 2, 6])
        mv3 = sb("mv3", [P, 2, 2])
        rs3 = sb("rs3", [P, 2])
        xn3 = sb("xn3", [P, 2, D])
        xn3T = sb("xn3T", [P, 2, KC, P])
        lg = sb("lg", [P, 2, NE + 1])
        nmx = sb("nmx", [P, 2])
        pe8 = sb("pe8", [P, 2, NE])
        ps8 = sb("ps8", [P, 2, 2])
        pb8 = sb("pb8", [P, 2, NE])
        top = sb("top", [P, 2, 8])
        topi = sb("topi", [P, 2, 8], U32)
        topf = sb("topf", [P, 2, 2])
        tsum = sb("tsum", [P, 2, 2])
        tw = sb("tw", [P, 2, 2])
        hot = sb("hot", [P, 2, 2, NE])
        half_c = sb("half_c", [P, 2, NE])
        sgt = sb("sgt", [P, 2])
        sg4 = sb("sg4", [P, 2])
        s_th = sb("s_th", [P, HS])
        s_gg = sb("s_gg", [P, HS])
        s_h = sb("s_h", [P, HS])
        s_hT = sb("s_hT", [P, 3, P])
        e_th = sb("e_th", [P, 2, H])
        e_gg = sb("e_gg", [P, 2, H])
        e_h = sb("e_h", [P, 2, H])
        e_hT = sb("e_hT", [HC, 2, 2, P])

        ps = ctx.enter_context(nc.psum_tensor("ps", [P, 8, 512], F32))
        A0, A1, A2, A3, B0, B1, B2, B3 = range(8)
        F0, G0, G1, G2, H0, H1, D0, D1 = range(8)

        names = """x_first x_rest w_self w_cross const_in ctx_in w_ffn consts_v consts_p
            ln1_st ln1_mv ln1_ve ln1_rs ln1_done xn1T_mm xn1T_ready kv_mm q_mm k1_ready ke_ready kf_ready
            v_ready q1_ready qe_ready qf_ready kvs_mm kvs_ready numden_mm den_ready rden_ready oT_ready
            attn_mm xbo_ready x1_ready
            ln2_st ln2_mv ln2_ve ln2_rs ln2_done xcT_mm xcT_ready ckv_mm q2_mm kbd_ready vbd_ready q2T_ready
            scores_mm bias_ready sc_ready smax_ready sub_ready exp_ready ssum_ready rsum_ready pn_ready
            prT_mm prT_ready pv_mm o2T_ready xo_mm x2_ready
            ln3_st ln3_mv ln3_ve ln3_rs ln3_done xn3T_mm xn3T_ready route_mm lg_ready nmx_ready pe8_ready
            psum_ready prec_ready pb8_ready top_ready topi_ready topf_ready tsum_ready trec_ready tw_ready
            hot0_ready hot1_ready half_c_ready sgt_ready sg4_ready s_th_ready s_gg_ready s_h_ready
            s_hT_mm s_hT_ready s_up_mm
            gu_mm e_th_ready e_gg_ready e_h_ready e_hT_mm e_hT_ready down_mm y_ready stored dve_passed pe_passed"""
        sm = {n: sem(n) for n in names.split()}

        x_d = a["x"].rearrange("b s d -> (b s) d").rearrange("(t p) d -> p t d", p=P)
        ctx_d = a["ctx"].rearrange("b s d -> (b s) d")
        out_d = out.rearrange("b s d -> (b s) d")

        def bcast(vec, n):
            return bass.AP(vec.tensor, vec.offset, [[0, P], [1, n]])

        W_SELF, W_CROSS, W_CONST, W_FFN = 6, 4, 6 + SEQS, 6

        def alone(eng, passed):
            eng.sem_inc(passed, 1)

        block = ctx.enter_context(nc.Block())

        @block.sync
        def _(sp):
            sp.dma_start(x_all[:, 0:2, :], x_d[:, 0:2, :]).then_inc(sm["x_first"], 16)
            sp.dma_start(ident[:, :], a["ident"]).then_inc(sm["const_in"], 16)
            sp.dma_start(wkv[:, :, :], a["wkv"]).then_inc(sm["w_self"], 16)
            sp.dma_start(bkv[:, :], bcast(a["bkv"], 2 * D)).then_inc(sm["w_self"], 16)
            sp.dma_start(wq[:, :, :], a["wq"]).then_inc(sm["w_self"], 16)
            sp.dma_start(bq1[:, :], a["bq"]).then_inc(sm["w_self"], 16)
            sp.dma_start(block_mask[:, :], a["block_mask"]).then_inc(sm["const_in"], 16)
            sp.dma_start(row_head[:, :], a["row_head"]).then_inc(sm["const_in"], 16)
            sp.dma_start(row_half[:, :], a["row_half"]).then_inc(sm["const_in"], 16)
            sp.dma_start(iota8[:, :], a["iota8"]).then_inc(sm["const_in"], 16)
            sp.dma_start(wo[:, :, :], a["wo"]).then_inc(sm["w_self"], 16)
            sp.dma_start(bo[:, :], bcast(a["bo"], D)).then_inc(sm["w_self"], 16)
            sp.dma_start(ctx_sb[:, :], ctx_d[0:P, :]).then_inc(sm["ctx_in"], 16)
            sp.dma_start(xwk[:, :, :], a["xwk"]).then_inc(sm["w_cross"], 16)
            sp.dma_start(xwv[:, :, :], a["xwv"]).then_inc(sm["w_cross"], 16)
            sp.dma_start(xwq[:, :, :], a["xwq"]).then_inc(sm["w_cross"], 16)
            sp.dma_start(xwo[:, :, :], a["xwo"]).then_inc(sm["w_cross"], 16)
            sp.dma_start(alibi[:, :], a["alibi"]).then_inc(sm["const_in"], 16)
            for s in range(SEQS):
                src = bass.AP(a["mask"].tensor, a["mask"].offset + s * S, [[0, S], [SEQS * S, TILES], [1, S]])
                sp.dma_start(mask_u8[s * S:(s + 1) * S, :, :], src).then_inc(sm["const_in"], 16)
            sp.dma_start(x_all[:, 2:TILES, :], x_d[:, 2:TILES, :]).then_inc(sm["x_rest"], 16)
            with sp.Fori(1, TILES) as t:
                sp.wait_ge(sm["xcT_mm"], t)
                sp.dma_start(ctx_sb[:, :], ctx_d[bass.ds(t * P, P), :]).then_inc(sm["ctx_in"], 16)
            with sp.Fori(0, TILES) as t:
                sp.wait_ge(sm["y_ready"], t + 1)
                sp.dma_start(out_d[bass.ds(t * P, P), :], x_all[:, bass.ds(t, 1), :].rearrange("p t d -> p (t d)")).then_inc(sm["stored"], 16)
            sp.wait_ge(sm["stored"], 16 * TILES)

        @block.gpsimd
        def _(pool):
            nc.gpsimd.memset(neg_half[:, :], -0.5).then_inc(sm["consts_p"], 1)
            nc.gpsimd.memset(eps[:, :], LN_EPS).then_inc(sm["consts_p"], 1)
            pool.wait_ge(sm["consts_p"], 2)

            def rstd(mv, ve, rs, mv_sem, ve_sem, rs_sem, n):
                pool.wait_ge(mv_sem, n)
                nc.gpsimd.tensor_tensor(ve, mv, eps[:, :], ALU.add).then_inc(ve_sem, 1)
                pool.wait_ge(ve_sem, n)
                nc.gpsimd.tensor_tensor(rs, ve, neg_half[:, :], ALU.pow).then_inc(rs_sem, 1)

            def rstd1(t):
                wait(pool, sm["ln1_done"], t)
                rstd(mv1[:, 1:2], st1[:, 0:1], rs1[:, :], sm["ln1_mv"], sm["ln1_ve"], sm["ln1_rs"], t + 1)

            def rstd2(t):
                wait(pool, sm["ln2_done"], t)
                rstd(mv2[:, 1:2], st2[:, 0:1], rs2[:, :], sm["ln2_mv"], sm["ln2_ve"], sm["ln2_rs"], t + 1)

            def add_bo(t):
                pool.wait_ge(sm["ln1_done"], t + 1)
                xt = x_all[:, bass.ds(t, 1), :].rearrange("p t d -> p (t d)")
                nc.gpsimd.tensor_tensor(xt, xt, bo[:, :], ALU.add).then_inc(sm["xbo_ready"], 1)

            def score_bias(t):
                wait(pool, sm["sc_ready"], t)
                ko = spread(key_off[:, bass.ds(t, 1), :], 1, HEADS)
                nc.gpsimd.tensor_tensor(bias_t[:, :].rearrange("p (h k) -> p h k", h=HEADS),
                                        alibi[:, :].rearrange("p (h k) -> p h k", h=HEADS), ko,
                                        ALU.add).then_inc(sm["bias_ready"], 1)

            def subtract_max(t):
                pool.wait_ge(sm["smax_ready"], t + 1)
                v = sc[:, :].rearrange("p (h k) -> p h k", h=HEADS)
                nc.gpsimd.tensor_tensor(v, v, spread(smax[:, :].rearrange("p (h o) -> p h o", o=1), 2, S),
                                        ALU.subtract).then_inc(sm["sub_ready"], 1)

            def divide_sum(t):
                pool.wait_ge(sm["rsum_ready"], t + 1)
                v = pr[:, :].rearrange("p (h k) -> p h k", h=HEADS)
                nc.gpsimd.tensor_tensor(v, v, spread(rsum[:, :].rearrange("p (h o) -> p h o", o=1), 2, S),
                                        ALU.mult).then_inc(sm["pn_ready"], 1)

            def body(t, self_attn, front, nxt):
                if nxt:
                    rstd1(t + 1)
                if self_attn:
                    add_bo(t)
                if front:
                    score_bias(t - 1)
                    subtract_max(t - 1)
                if self_attn:
                    rstd2(t)
                if front:
                    divide_sum(t - 1)

            rstd1(0)
            pool.wait_ge(sm["w_self"], 16 * W_SELF)
            pool.wait_ge(sm["consts_v"], 3)
            body(0, True, False, True)
            body(1, True, True, True)
            body(2, True, True, True)
            with pool.Fori(3, TILES - 1) as t:
                body(t, True, True, True)
            body(TILES - 1, True, True, False)
            body(TILES, False, True, False)

            def rstd3(t, p):
                wait(pool, sm["ln3_done"], t - 1)
                rstd(mv3[:, p, 1:2], st3[:, p, 0:1], rs3[:, p:p + 1], sm["ln3_mv"], sm["ln3_ve"], sm["ln3_rs"], t + 1)
            rstd3(0, 0)
            rstd3(1, 1)
            with pool.Fori(2, TILES, 2) as t:
                rstd3(t, 0)
                rstd3(t + 1, 1)

        @block.tensor
        def _(pe):
            T = nc.tensor

            def transpose_x(t):
                pe.wait_ge(sm["ln1_done"], t + 1)
                wait(pe, sm["xn1T_ready"], t)
                wait(pe, sm["kvs_ready"], t)
                for k in range(KC):
                    mm = T.transpose(ps[:, A0, k * P:(k + 1) * P], xn1[:, k * P:(k + 1) * P], ident[:, :])
                mm.then_inc(sm["xn1T_mm"], 1)

            def project_qkv(t):
                pe.wait_ge(sm["xn1T_ready"], t + 1)
                wait(pe, sm["x1_ready"], t)
                for k in range(KC):
                    mm = T.matmul(ps[:, A2, :], xn1T[:, k, :], wkv[:, k, :], start=(k == 0), stop=(k == KC - 1))
                mm.then_inc(sm["kv_mm"], 1)
                wait(pe, sm["oT_ready"], t)
                for c in range(KC):
                    for k in range(KC):
                        mm = T.matmul(ps[:, A1, c * P:(c + 1) * P], wq[:, k, c * P:(c + 1) * P], xn1T[:, k, :],
                                      start=(k == 0), stop=(k == KC - 1))
                mm.then_inc(sm["q_mm"], 1)

            def key_value(t):
                pe.wait_ge(sm["kf_ready"], t + 1)
                pe.wait_ge(sm["v_ready"], t + 1)
                wait(pe, sm["x2_ready"], t - 2)
                alone(pe, sm["pe_passed"])
                for s in range(SEQS):
                    rows = slice(s * S, (s + 1) * S)
                    for c in range(2):
                        for j in range(4):
                            g = c * 4 + j
                            mm = T.matmul(ps[32 * j:32 * j + 32, (A3, A0)[s], c * 33:c * 33 + 33],
                                          kf[rows, g * 32:g * 32 + 32], vo[rows, g, :], start=True, stop=True)
                mm.then_inc(sm["kvs_mm"], 1)

            def query_kv(t):
                pe.wait_ge(sm["kvs_ready"], t + 1)
                pe.wait_ge(sm["qf_ready"], t + 1)
                alone(pe, sm["pe_passed"])
                for s in range(SEQS):
                    for c in range(2):
                        for which, w in enumerate((kv_bd, ks_bd)):
                            for j in range(4):
                                q = slice(32 * j, 32 * j + 32)
                                col = c * 256 + which * 128 + s * S
                                mm = T.matmul(ps[q, A1, col:col + S], w[q, s, c, :], qf[q, c, s * S:(s + 1) * S],
                                              start=True, stop=True)
                mm.then_inc(sm["numden_mm"], 1)

            def project_attn(t):
                pe.wait_ge(sm["oT_ready"], t + 1)
                for k in range(KC):
                    mm = T.matmul(ps[:, A2, 0:D], oT[:, k, :], wo[:, k, :], start=(k == 0), stop=(k == KC - 1))
                mm.then_inc(sm["attn_mm"], 1)

            def transpose_xc(t):
                pe.wait_ge(sm["ctx_in"], 16 * (t + 1))
                wait(pe, sm["sc_ready"], t)
                for k in range(KC):
                    T.transpose(ps[:, B3, (KC + k) * P:(KC + k + 1) * P], ctx_sb[:, k * P:(k + 1) * P], ident[:, :])
                pe.wait_ge(sm["ln2_done"], t + 1)
                for k in range(KC):
                    mm = T.transpose(ps[:, B3, k * P:(k + 1) * P], xn2[:, k * P:(k + 1) * P], ident[:, :])
                mm.then_inc(sm["xcT_mm"], 1)

            def project_ctx(t):
                pe.wait_ge(sm["xcT_ready"], t + 1)
                for c in range(2):
                    for k in range(KC):
                        T.matmul(ps[:, B2, c * P:(c + 1) * P],
                                 xwk_rep[:, k, 2 * c:2 * c + 2, :, :].rearrange("p g h d -> p (g h d)"),
                                 xcT[:, KC + k, :], start=(k == 0), stop=(k == KC - 1))
                for s in range(SEQS):
                    for r in range(2):
                        for k in range(KC):
                            mm = T.matmul(ps[r * S:(r + 1) * S, B2, 256 + s * S:256 + (s + 1) * S],
                                          xcT[:, KC + k, s * S:(s + 1) * S], xwv[:, k, :],
                                          start=(k == 0), stop=(k == KC - 1))
                mm.then_inc(sm["ckv_mm"], 1)

            def project_q2(t):
                for c in range(KC):
                    for k in range(KC):
                        mm = T.matmul(ps[:, B3, c * P:(c + 1) * P], xwq[:, k, c * P:(c + 1) * P], xcT[:, k, :],
                                      start=(k == 0), stop=(k == KC - 1))
                mm.then_inc(sm["q2_mm"], 1)

            def scores(t):
                pe.wait_ge(sm["q2T_ready"], t + 1)
                pe.wait_ge(sm["kbd_ready"], t + 1)
                pe.wait_ge(sm["vbd_ready"], t + 1)
                wait(pe, sm["prT_ready"], 2 * t)
                wait(pe, sm["o2T_ready"], t)
                alone(pe, sm["pe_passed"])
                for c in range(2):
                    for j in range(4):
                        q = slice(32 * j, 32 * j + 32)
                        for s in range(SEQS):
                            mm = T.matmul(ps[s * S:(s + 1) * S, B0 + j, c * P:(c + 1) * P],
                                          q2T[q, c, s * S:(s + 1) * S], k_bd[q, c, :, s * S:(s + 1) * S],
                                          start=True, stop=True)
                mm.then_inc(sm["scores_mm"], 1)

            def transpose_probs(t):
                pe.wait_ge(sm["pn_ready"], t + 1)
                for b in range(8):
                    mm = T.transpose(ps[:, B0 + b // 4, (b % 4) * P:(b % 4 + 1) * P], pr[:, b * P:(b + 1) * P],
                                     ident[:, :])
                mm.then_inc(sm["prT_mm"], 1)

            def probs_values(t):
                pe.wait_ge(sm["prT_ready"], 2 * (t + 1))
                alone(pe, sm["pe_passed"])
                for c in range(2):
                    for s in range(SEQS):
                        for j in range(4):
                            mm = T.matmul(ps[32 * j:32 * j + 32, B1, c * P + s * S:c * P + (s + 1) * S],
                                          v_bd[:, s * GROUPS + 2 * c + j // 2, :, :].rearrange("p h e -> p (h e)"),
                                          prT[:, 2 * j + c, s * S:(s + 1) * S], start=True, stop=True)
                mm.then_inc(sm["pv_mm"], 1)

            def project_cross(t):
                pe.wait_ge(sm["o2T_ready"], t + 1)
                for k in range(KC):
                    mm = T.matmul(ps[:, A3, 0:D], o2T[:, k, :], xwo[:, k, :], start=(k == 0), stop=(k == KC - 1))
                mm.then_inc(sm["xo_mm"], 1)

            def body(t, self_attn, front, back, nxt):
                if self_attn:
                    project_qkv(t)
                if front:
                    transpose_xc(t - 1)
                if self_attn:
                    key_value(t)
                if back:
                    transpose_probs(t - 2)
                if front:
                    project_ctx(t - 1)
                    project_q2(t - 1)
                if back:
                    probs_values(t - 2)
                if self_attn:
                    query_kv(t)
                if front:
                    scores(t - 1)
                if back:
                    project_cross(t - 2)
                if self_attn:
                    project_attn(t)
                if nxt:
                    transpose_x(t + 1)

            pe.wait_ge(sm["const_in"], 16 * W_CONST)
            transpose_x(0)
            pe.wait_ge(sm["w_self"], 16 * W_SELF)
            body(0, True, False, False, True)
            pe.wait_ge(sm["w_cross"], 16 * W_CROSS)
            pe.wait_ge(sm["consts_v"], 6)
            body(1, True, True, False, True)
            body(2, True, True, True, True)
            with pe.Fori(3, TILES - 1) as t:
                body(t, True, True, True, True)
            body(TILES - 1, True, True, True, False)
            body(TILES, False, True, True, False)
            body(TILES + 1, False, False, True, False)

            def transpose_n3(t, p):
                pe.wait_ge(sm["ln3_done"], t + 1)
                wait(pe, sm["xn3T_ready"], t)
                for k in range(KC):
                    mm = T.transpose(ps[:, F0, k * P:(k + 1) * P], xn3[:, p, k * P:(k + 1) * P], ident[:, :])
                mm.then_inc(sm["xn3T_mm"], 1)

            def shared_gate_up(t, p):
                pe.wait_ge(sm["xn3T_ready"], t + 1)
                wait(pe, sm["e_h_ready"], NE * t)
                for k in range(KC):
                    mm = T.matmul(ps[:, G0, 0:ROUTE], xn3T[:, p, k, :], w_route[:, k, :], start=(k == 0), stop=(k == KC - 1))
                mm.then_inc(sm["route_mm"], 1)
                for k in range(KC):
                    mm = T.matmul(ps[:, G1, 0:HS], xn3T[:, p, k, :], w_sh_up[:, k, :], start=(k == 0), stop=(k == KC - 1))
                mm.then_inc(sm["s_up_mm"], 1)

            def gate_up(t, p, e):
                bank = (G2, G0, G1)[e % 3]
                if e in (1, 2):
                    pe.wait_ge(sm["s_h_ready"], t + 1)
                if e >= 3:
                    pe.wait_ge(sm["e_h_ready"], NE * t + e - 2)
                for k in range(KC):
                    mm = T.matmul(ps[:, bank, 0:2 * H], xn3T[:, p, k, :], w_gu[:, e, k, :], start=(k == 0), stop=(k == KC - 1))
                mm.then_inc(sm["gu_mm"], 1)

            def shared_transpose(t):
                pe.wait_ge(sm["s_h_ready"], t + 1)
                wait(pe, sm["e_hT_ready"], NE * t)
                T.transpose(ps[:, H1, 0:P], s_h[:, 0:P], ident[:, :])
                T.transpose(ps[:, H1, P:2 * P], s_h[:, P:2 * P], ident[:, :])
                T.transpose(ps[0:HS_LAST, H1, 2 * P:3 * P], s_h[:, 2 * P:HS], ident[:, :]).then_inc(sm["s_hT_mm"], 1)

            def shared_down(t, p):
                pe.wait_ge(sm["s_hT_ready"], 2 * (t + 1))
                wait(pe, sm["y_ready"], t - 1)
                for c in range(3):
                    rows = P if c < 2 else HS_LAST
                    T.matmul(ps[:, D0 + p, 0:D], s_hT[0:rows, c, :], w_sh_down[0:rows, c, :], start=(c == 0), stop=False)

            def expert_transpose(t, e):
                pe.wait_ge(sm["e_h_ready"], NE * t + e + 1)
                if e == 1:
                    pe.wait_ge(sm["s_hT_ready"], 2 * (t + 1))
                elif e >= 2:
                    pe.wait_ge(sm["e_hT_ready"], NE * t + e - 1)
                for c in range(2):
                    mm = T.transpose(ps[0:HC, H0 + e % 2, c * P:(c + 1) * P], e_h[:, e % 2, c * HC:(c + 1) * HC], ident[:, :])
                mm.then_inc(sm["e_hT_mm"], 1)

            def expert_down(t, p, e):
                pe.wait_ge(sm["e_hT_ready"], NE * t + e + 1)
                for c in range(2):
                    mm = T.matmul(ps[:, D0 + p, 0:D], e_hT[:, e % 2, c, :], w_down[:, e, c, :],
                                  start=False, stop=(e == NE - 1 and c == 1))
                if e == NE - 1:
                    mm.then_inc(sm["down_mm"], 1)

            def ffn(t, p, nxt):
                shared_gate_up(t, p)
                gate_up(t, p, 0)
                shared_transpose(t)
                expert_transpose(t, 0)
                gate_up(t, p, 1)
                shared_down(t, p)
                gate_up(t, p, 2)
                for e in range(1, NE):
                    expert_transpose(t, e)
                    expert_down(t, p, e - 1)
                    if e + 2 < NE:
                        gate_up(t, p, e + 2)
                    if e == 4 and nxt:
                        transpose_n3(t + 1, 1 - p)
                expert_down(t, p, NE - 1)

            pe.wait_ge(sm["w_ffn"], 16 * W_FFN)
            pe.wait_ge(sm["x2_ready"], TILES)
            transpose_n3(0, 0)
            ffn(0, 0, True)
            ffn(1, 1, True)
            with pe.Fori(2, TILES - 2, 2) as t:
                ffn(t, 0, True)
                ffn(t + 1, 1, True)
            ffn(TILES - 2, 0, True)
            ffn(TILES - 1, 1, False)

        @block.scalar
        def _(act):
            A = nc.scalar
            act.dma_start(w_route[:, :, :], a["w_route"]).then_inc(sm["w_ffn"], 16)
            act.dma_start(w_sh_up[:, :, :], a["w_sh_up"]).then_inc(sm["w_ffn"], 16)
            act.dma_start(w_sh_down[:, 0:2, :], bass.AP(a["w_sh_down"].tensor, a["w_sh_down"].offset, [[D, P], [P * D, 2], [1, D]])).then_inc(sm["w_ffn"], 16)
            act.dma_start(w_sh_down[0:HS_LAST, 2, :], a["w_sh_down"][2 * P:HS, :]).then_inc(sm["w_ffn"], 16)
            act.dma_start(w_gu[:, :, :, :], a["w_gu"]).then_inc(sm["w_ffn"], 16)
            act.dma_start(w_down[:, :, :, :], a["w_down"]).then_inc(sm["w_ffn"], 16)

            def k_exp(t):
                act.wait_ge(sm["k1_ready"], t + 1)
                wait(act, sm["kf_ready"], t)
                A.activation(ke[:, :], k1[:, :], ACT.Exp, bias=minus_one[:, :]).then_inc(sm["ke_ready"], 1)

            def q_exp(t):
                act.wait_ge(sm["q_mm"], t + 1)
                wait(act, sm["qf_ready"], t)
                for c in range(KC):
                    A.activation(q1[:, c, :], ps[:, A1, c * P:(c + 1) * P], ACT.Identity,
                                 bias=bq1[:, c:c + 1]).then_inc(sm["q1_ready"], 1)
                act.wait_ge(sm["q1_ready"], 2 * (t + 1))
                A.activation(qe[:, :, :], q1[:, :, :], ACT.Exp, bias=minus_one[:, :]).then_inc(sm["qe_ready"], 1)

            def copy_xcT(t):
                act.wait_ge(sm["xcT_mm"], t + 1)
                wait(act, sm["q2_mm"], t)
                A.activation(xcT[:, :, :].rearrange("p c t -> p (c t)"), ps[:, B3, :], ACT.Copy).then_inc(sm["xcT_ready"], 1)

            def copy_prT(t):
                act.wait_ge(sm["prT_mm"], t + 1)
                wait(act, sm["pv_mm"], t)
                for b in range(2):
                    A.activation(prT[:, 4 * b:4 * b + 4, :].rearrange("p c t -> p (c t)"), ps[:, B0 + b, :],
                                 ACT.Copy).then_inc(sm["prT_ready"], 1)

            def scale_q2(t):
                act.wait_ge(sm["q2_mm"], t + 1)
                wait(act, sm["scores_mm"], t)
                A.activation(q2T[:, :, :].rearrange("p c t -> p (c t)"), ps[:, B3, 0:D], ACT.Copy,
                             scale=DH ** -0.5).then_inc(sm["q2T_ready"], 1)

            def copy_o2T(t):
                act.wait_ge(sm["pv_mm"], t + 1)
                wait(act, sm["xo_mm"], t)
                A.activation(o2T[:, :, :].rearrange("p c t -> p (c t)"), ps[:, B1, 0:D], ACT.Copy).then_inc(sm["o2T_ready"], 1)

            def copy_xn1T(t):
                act.wait_ge(sm["xn1T_mm"], t + 1)
                wait(act, sm["q_mm"], t)
                A.activation(xn1T[:, :, :].rearrange("p c t -> p (c t)"), ps[:, A0, 0:D], ACT.Copy).then_inc(sm["xn1T_ready"], 1)

            def score_exp(t):
                act.wait_ge(sm["sub_ready"], t + 1)
                wait(act, sm["prT_mm"], t)
                A.activation(pr[:, :], sc[:, :], ACT.Exp).then_inc(sm["exp_ready"], 1)

            def body(t, self_attn, front, back, nxt):
                if self_attn:
                    k_exp(t)
                    q_exp(t)
                if front:
                    copy_xcT(t - 1)
                if back:
                    copy_prT(t - 2)
                if front:
                    scale_q2(t - 1)
                if back:
                    copy_o2T(t - 2)
                if nxt:
                    copy_xn1T(t + 1)
                if front:
                    score_exp(t - 1)

            act.wait_ge(sm["consts_v"], 3)
            copy_xn1T(0)
            body(0, True, False, False, True)
            body(1, True, True, False, True)
            body(2, True, True, True, True)
            with act.Fori(3, TILES - 1) as t:
                body(t, True, True, True, True)
            body(TILES - 1, True, True, True, False)
            body(TILES, False, True, True, False)
            body(TILES + 1, False, False, True, False)

            def copy_xn3T(t, p):
                act.wait_ge(sm["xn3T_mm"], t + 1)
                wait(act, sm["gu_mm"], NE * (t - 1))
                A.activation(xn3T[:, p, :, :].rearrange("p c t -> p (c t)"), ps[:, F0, 0:D], ACT.Copy).then_inc(sm["xn3T_ready"], 1)

            def shared_tanh(t):
                act.wait_ge(sm["route_mm"], t + 1)
                act.wait_ge(sm["lg_ready"], t + 1)
                wait(act, sm["s_gg_ready"], t)
                A.activation(s_th[:, :], ps[:, G0, 0:HS], ACT.Tanh, scale=0.5).then_inc(sm["s_th_ready"], 1)

            def route_exp(t, p):
                act.wait_ge(sm["nmx_ready"], t + 1)
                wait(act, sm["pb8_ready"], t - 1)
                A.activation(pe8[:, p, :], lg[:, p, 0:NE], ACT.Exp, bias=nmx[:, p:p + 1]).then_inc(sm["pe8_ready"], 1)
                A.activation(sgt[:, p:p + 1], lg[:, p, NE:NE + 1], ACT.Tanh, scale=0.5).then_inc(sm["sgt_ready"], 1)

            def copy_s_hT(t):
                act.wait_ge(sm["s_hT_mm"], t + 1)
                wait(act, sm["down_mm"], t)
                A.activation(s_hT[:, 0:2, :].rearrange("p c t -> p (c t)"), ps[:, H1, 0:2 * P], ACT.Copy).then_inc(sm["s_hT_ready"], 1)
                A.activation(s_hT[0:HS_LAST, 2, :], ps[0:HS_LAST, H1, 2 * P:3 * P], ACT.Copy).then_inc(sm["s_hT_ready"], 1)

            def expert_tanh(t, e):
                act.wait_ge(sm["gu_mm"], NE * t + e + 1)
                wait(act, sm["e_gg_ready"], NE * t + e - 1)
                A.activation(e_th[:, e % 2, :], ps[:, (G2, G0, G1)[e % 3], 0:H], ACT.Tanh, scale=0.5).then_inc(sm["e_th_ready"], 1)

            def copy_e_hT(t, e):
                act.wait_ge(sm["e_hT_mm"], NE * t + e + 1)
                A.activation(e_hT[:, e % 2, :, :].rearrange("p c t -> p (c t)"), ps[0:HC, H0 + e % 2, 0:2 * P],
                             ACT.Copy).then_inc(sm["e_hT_ready"], 1)

            def ffn(t, p, nxt):
                shared_tanh(t)
                route_exp(t, p)
                expert_tanh(t, 0)
                copy_s_hT(t)
                copy_e_hT(t, 0)
                expert_tanh(t, 1)
                expert_tanh(t, 2)
                for e in range(1, NE):
                    copy_e_hT(t, e)
                    if e + 2 < NE:
                        expert_tanh(t, e + 2)
                    if e == 4 and nxt:
                        copy_xn3T(t + 1, 1 - p)

            copy_xn3T(0, 0)
            ffn(0, 0, True)
            ffn(1, 1, True)
            with act.Fori(2, TILES - 2, 2) as t:
                ffn(t, 0, True)
                ffn(t + 1, 1, True)
            ffn(TILES - 2, 0, True)
            ffn(TILES - 1, 1, False)

        @block.vector
        def _(v):
            V = nc.vector

            def xt(t):
                return x_all[:, bass.ds(t, 1), :].rearrange("p t d -> p (t d)")

            V.memset(minus_one[:, :], -1.0).then_inc(sm["consts_v"], 1)
            V.memset(vo[:, :, 32:33], 1.0).then_inc(sm["consts_v"], 1)

            def ln1_stats(t):
                wait(v, sm["ln1_rs"], t)
                wait(v, sm["ln1_done"], t)
                alone(v, sm["dve_passed"])
                V.bn_stats(st1[:, :], xt(t)).then_inc(sm["ln1_st"], 1)
                v.wait_ge(sm["ln1_st"], t + 1)
                alone(v, sm["dve_passed"])
                V.bn_aggr(mv1[:, :], st1[:, :]).then_inc(sm["ln1_mv"], 1)

            def ln1_norm(t):
                v.wait_ge(sm["ln1_rs"], t + 1)
                wait(v, sm["xn1T_mm"], t)
                V.tensor_scalar(xn1[:, :], xt(t), mv1[:, 0:1], rs1[:, :], ALU.subtract, ALU.mult).then_inc(sm["ln1_done"], 1)

            def k_v_bias(t):
                v.wait_ge(sm["kv_mm"], t + 1)
                wait(v, sm["kf_ready"], t)
                V.tensor_tensor(k1[:, :], ps[:, A2, 0:D], bkv[:, 0:D], ALU.add).then_inc(sm["k1_ready"], 1)
                wait(v, sm["kvs_mm"], t)
                V.tensor_tensor(vo[:, :, 0:32], ps[:, A2, D:2 * D].rearrange("p (g e) -> p g e", e=32),
                                bkv[:, D:2 * D].rearrange("p (g e) -> p g e", e=32), ALU.add).then_inc(sm["v_ready"], 1)

            def k_feature(t):
                v.wait_ge(sm["ke_ready"], t + 1)
                V.scalar_tensor_tensor(out=kf[:, :], in0=k1[:, :], scalar=1.0, in1=ke[:, :], op0=ALU.max,
                                       op1=ALU.min).then_inc(sm["kf_ready"], 1)

            def q_feature(t):
                v.wait_ge(sm["qe_ready"], t + 1)
                wait(v, sm["numden_mm"], t)
                V.scalar_tensor_tensor(out=qf[:, :, :].rearrange("p c t -> p (c t)"),
                                       in0=q1[:, :, :].rearrange("p c t -> p (c t)"), scalar=1.0,
                                       in1=qe[:, :, :].rearrange("p c t -> p (c t)"), op0=ALU.max,
                                       op1=ALU.min).then_inc(sm["qf_ready"], 1)

            def block_diagonal(t):
                v.wait_ge(sm["kvs_mm"], t + 1)
                wait(v, sm["numden_mm"], t)
                for s in range(SEQS):
                    g = ps[:, (A3, A0)[s], 0:66].rearrange("p (c e) -> p c e", e=33)
                    bm = spread(block_mask[:, :].rearrange("p (o e) -> p o e", o=1), 1, 2)
                    V.tensor_tensor(kv_bd[:, s, :, :], g[:, :, 0:32], bm, ALU.mult)
                    last = V.tensor_tensor(ks_bd[:, s, :, :], spread(g[:, :, 32:33], 2, 32), bm, ALU.mult)
                last.then_inc(sm["kvs_ready"], 1)

            def divide(t):
                nd = ps[:, A1, :].rearrange("p (c w t) -> p c w t", c=2, w=2)
                v.wait_ge(sm["numden_mm"], t + 1)
                V.tensor_scalar(den[:, :, :], nd[:, :, 1, :], DEN_EPS, None, ALU.add).then_inc(sm["den_ready"], 1)
                v.wait_ge(sm["den_ready"], t + 1)
                V.reciprocal(rden[:, :, :], den[:, :, :]).then_inc(sm["rden_ready"], 1)
                v.wait_ge(sm["rden_ready"], t + 1)
                wait(v, sm["attn_mm"], t)
                V.tensor_tensor(oT[:, :, :], nd[:, :, 0, :], rden[:, :, :], ALU.mult).then_inc(sm["oT_ready"], 1)

            def residual1(t):
                v.wait_ge(sm["attn_mm"], t + 1)
                v.wait_ge(sm["xbo_ready"], t + 1)
                V.tensor_tensor(xt(t), ps[:, A2, 0:D], xt(t), ALU.add).then_inc(sm["x1_ready"], 1)

            def ln2_stats(t):
                v.wait_ge(sm["x1_ready"], t + 1)
                wait(v, sm["ln2_rs"], t)
                wait(v, sm["ln2_done"], t)
                alone(v, sm["dve_passed"])
                V.bn_stats(st2[:, :], xt(t)).then_inc(sm["ln2_st"], 1)
                v.wait_ge(sm["ln2_st"], t + 1)
                alone(v, sm["dve_passed"])
                V.bn_aggr(mv2[:, :], st2[:, :]).then_inc(sm["ln2_mv"], 1)

            def ln2_norm(t):
                v.wait_ge(sm["ln2_rs"], t + 1)
                wait(v, sm["xcT_mm"], t)
                V.tensor_scalar(xn2[:, :], xt(t), mv2[:, 0:1], rs2[:, :], ALU.subtract, ALU.mult).then_inc(sm["ln2_done"], 1)

            def k_block(t):
                v.wait_ge(sm["ckv_mm"], t + 1)
                wait(v, sm["scores_mm"], t)
                for c in range(2):
                    kk = spread(ps[:, B2, c * P:(c + 1) * P].rearrange("p (o t) -> p o t", o=1), 1, 2)
                    last = V.tensor_tensor(k_bd[:, c, :, :], kk,
                                           spread(row_head[:, :].rearrange("p (h o) -> p h o", o=1), 2, P), ALU.mult)
                last.then_inc(sm["kbd_ready"], 1)

            def v_block(t):
                wait(v, sm["pv_mm"], t)
                vv = ps[:, B2, 256:384].rearrange("p (g e) -> p g e", e=DH)
                for h in range(2):
                    last = V.tensor_scalar(v_bd[:, :, h, :], vv, row_half[:, h:h + 1], None, ALU.mult)
                last.then_inc(sm["vbd_ready"], 1)

            def score_max(t):
                v.wait_ge(sm["scores_mm"], t + 1)
                v.wait_ge(sm["bias_ready"], t + 1)
                wait(v, sm["exp_ready"], t)
                V.tensor_tensor(sc[:, :].rearrange("p (j c) -> p j c", j=4), ps[:, B0:B3 + 1, 0:256],
                                bias_t[:, :].rearrange("p (j c) -> p j c", j=4), ALU.add).then_inc(sm["sc_ready"], 1)
                v.wait_ge(sm["sc_ready"], t + 1)
                wait(v, sm["sub_ready"], t)
                V.tensor_reduce(smax[:, :], sc[:, :].rearrange("p (h k) -> p h k", h=HEADS), AX.X,
                                ALU.max).then_inc(sm["smax_ready"], 1)

            def score_sum(t):
                v.wait_ge(sm["exp_ready"], t + 1)
                wait(v, sm["rsum_ready"], t)
                V.tensor_reduce(ssum[:, :], pr[:, :].rearrange("p (h k) -> p h k", h=HEADS), AX.X,
                                ALU.add).then_inc(sm["ssum_ready"], 1)
                v.wait_ge(sm["ssum_ready"], t + 1)
                wait(v, sm["pn_ready"], t)
                V.reciprocal(rsum[:, :], ssum[:, :]).then_inc(sm["rsum_ready"], 1)

            def residual2(t):
                v.wait_ge(sm["xo_mm"], t + 1)
                V.tensor_tensor(xt(t), ps[:, A3, 0:D], xt(t), ALU.add).then_inc(sm["x2_ready"], 1)

            def body(t, self_attn, front, back, nxt):
                if nxt:
                    ln1_stats(t + 1)
                if self_attn:
                    k_v_bias(t)
                if nxt:
                    ln1_norm(t + 1)
                if self_attn:
                    k_feature(t)
                    q_feature(t)
                if front:
                    k_block(t - 1)
                if self_attn:
                    block_diagonal(t)
                if front:
                    v_block(t - 1)
                if self_attn:
                    divide(t)
                if front:
                    score_max(t - 1)
                if back:
                    residual2(t - 2)
                if self_attn:
                    residual1(t)
                    ln2_stats(t)
                    ln2_norm(t)
                if front:
                    score_sum(t - 1)

            v.wait_ge(sm["x_first"], 16)
            ln1_stats(0)
            ln1_norm(0)
            v.wait_ge(sm["w_self"], 16 * W_SELF)
            V.tensor_scalar(bkv[:, 0:D], bkv[:, 0:D], 1.0, None, ALU.add).then_inc(sm["consts_v"], 1)
            V.tensor_scalar(bq1[:, :], bq1[:, :], 1.0, None, ALU.add).then_inc(sm["consts_v"], 1)
            v.wait_ge(sm["const_in"], 16 * W_CONST)
            v.wait_ge(sm["consts_v"], 4)
            body(0, True, False, False, True)
            v.wait_ge(sm["w_cross"], 16 * W_CROSS)
            V.tensor_copy(xwk_rep[:, :, :, :, :].rearrange("p k g h d -> p (k g) h d"),
                          spread(xwk[:, :, :].rearrange("p k (g o d) -> p (k g) o d", g=GROUPS, o=1), 2, HEADS // GROUPS)
                          ).then_inc(sm["consts_v"], 1)
            V.tensor_scalar(key_off[:, :, :], mask_u8[:, :, :], -1.0, BIG, ALU.add, ALU.mult).then_inc(sm["consts_v"], 1)
            v.wait_ge(sm["x_rest"], 16)
            body(1, True, True, False, True)
            body(2, True, True, True, True)
            with v.Fori(3, TILES - 1) as t:
                body(t, True, True, True, True)
            body(TILES - 1, True, True, True, False)
            body(TILES, False, True, True, False)
            body(TILES + 1, False, False, True, False)

            v.wait_ge(sm["x2_ready"], TILES)

            def ln3(t, p):
                wait(v, sm["ln3_rs"], t - 1)
                wait(v, sm["ln3_done"], t - 1)
                alone(v, sm["dve_passed"])
                V.bn_stats(st3[:, p, :], xt(t)).then_inc(sm["ln3_st"], 1)
                v.wait_ge(sm["ln3_st"], t + 1)
                alone(v, sm["dve_passed"])
                V.bn_aggr(mv3[:, p, :], st3[:, p, :]).then_inc(sm["ln3_mv"], 1)
                v.wait_ge(sm["ln3_rs"], t + 1)
                wait(v, sm["xn3T_mm"], t - 1)
                V.tensor_scalar(xn3[:, p, :], xt(t), mv3[:, p, 0:1], rs3[:, p:p + 1], ALU.subtract,
                                ALU.mult).then_inc(sm["ln3_done"], 1)

            def logits(t, p):
                v.wait_ge(sm["route_mm"], t + 1)
                V.tensor_copy(lg[:, p, :], ps[:, G0, HS:ROUTE]).then_inc(sm["lg_ready"], 1)
                v.wait_ge(sm["lg_ready"], t + 1)
                V.tensor_reduce(nmx[:, p:p + 1], lg[:, p, 0:NE], AX.X, ALU.max, negate=True).then_inc(sm["nmx_ready"], 1)

            def route(t, p):
                v.wait_ge(sm["sgt_ready"], t + 1)
                V.tensor_scalar(sg4[:, p:p + 1], sgt[:, p:p + 1], 1.0, 0.25, ALU.add, ALU.mult).then_inc(sm["sg4_ready"], 1)
                v.wait_ge(sm["pe8_ready"], t + 1)
                V.tensor_reduce(ps8[:, p, 0:1], pe8[:, p, :], AX.X, ALU.add).then_inc(sm["psum_ready"], 1)
                v.wait_ge(sm["psum_ready"], t + 1)
                V.reciprocal(ps8[:, p, 1:2], ps8[:, p, 0:1]).then_inc(sm["prec_ready"], 1)
                v.wait_ge(sm["prec_ready"], t + 1)
                V.tensor_scalar(pb8[:, p, :], pe8[:, p, :], ps8[:, p, 1:2], None, ALU.mult).then_inc(sm["pb8_ready"], 1)
                v.wait_ge(sm["pb8_ready"], t + 1)
                alone(v, sm["dve_passed"])
                V.max(top[:, p, :], pb8[:, p, :]).then_inc(sm["top_ready"], 1)
                v.wait_ge(sm["top_ready"], t + 1)
                alone(v, sm["dve_passed"])
                V.max_index(topi[:, p, :], top[:, p, :], pb8[:, p, :]).then_inc(sm["topi_ready"], 1)
                V.tensor_reduce(tsum[:, p, 0:1], top[:, p, 0:2], AX.X, ALU.add).then_inc(sm["tsum_ready"], 1)
                v.wait_ge(sm["topi_ready"], t + 1)
                V.tensor_copy(topf[:, p, :], topi[:, p, 0:2]).then_inc(sm["topf_ready"], 1)
                v.wait_ge(sm["tsum_ready"], t + 1)
                V.reciprocal(tsum[:, p, 1:2], tsum[:, p, 0:1]).then_inc(sm["trec_ready"], 1)
                v.wait_ge(sm["trec_ready"], t + 1)
                V.tensor_scalar(tw[:, p, :], top[:, p, 0:2], tsum[:, p, 1:2], 0.5, ALU.mult, ALU.mult).then_inc(sm["tw_ready"], 1)
                v.wait_ge(sm["tw_ready"], t + 1)
                v.wait_ge(sm["topf_ready"], t + 1)
                for r, ready in ((0, sm["hot0_ready"]), (1, sm["hot1_ready"])):
                    V.tensor_scalar(hot[:, p, r, :], iota8[:, :], topf[:, p, r:r + 1], tw[:, p, r:r + 1],
                                    ALU.is_equal, ALU.mult).then_inc(ready, 1)
                v.wait_ge(sm["hot0_ready"], t + 1)
                v.wait_ge(sm["hot1_ready"], t + 1)
                V.tensor_tensor(half_c[:, p, :], hot[:, p, 0, :], hot[:, p, 1, :], ALU.add).then_inc(sm["half_c_ready"], 1)

            def shared_h(t, p):
                v.wait_ge(sm["s_th_ready"], t + 1)
                V.scalar_tensor_tensor(out=s_gg[:, :], in0=s_th[:, :], scalar=1.0, in1=ps[:, G0, 0:HS],
                                       op0=ALU.add, op1=ALU.mult).then_inc(sm["s_gg_ready"], 1)
                v.wait_ge(sm["s_gg_ready"], t + 1)
                v.wait_ge(sm["s_up_mm"], t + 1)
                v.wait_ge(sm["sg4_ready"], t + 1)
                wait(v, sm["s_hT_mm"], t)
                V.scalar_tensor_tensor(out=s_h[:, :], in0=s_gg[:, :], scalar=sg4[:, p:p + 1], in1=ps[:, G1, 0:HS],
                                       op0=ALU.mult, op1=ALU.mult).then_inc(sm["s_h_ready"], 1)

            def expert_h(t, p, e):
                bank = (G2, G0, G1)[e % 3]
                n = NE * t + e + 1
                v.wait_ge(sm["e_th_ready"], n)
                V.scalar_tensor_tensor(out=e_gg[:, e % 2, :], in0=e_th[:, e % 2, :], scalar=1.0,
                                       in1=ps[:, bank, 0:H], op0=ALU.add, op1=ALU.mult).then_inc(sm["e_gg_ready"], 1)
                v.wait_ge(sm["e_gg_ready"], n)
                if e == 0:
                    v.wait_ge(sm["half_c_ready"], t + 1)
                wait(v, sm["e_hT_mm"], n - 2)
                V.scalar_tensor_tensor(out=e_h[:, e % 2, :], in0=e_gg[:, e % 2, :], scalar=half_c[:, p, e:e + 1],
                                       in1=ps[:, bank, H:2 * H], op0=ALU.mult, op1=ALU.mult).then_inc(sm["e_h_ready"], 1)

            def residual3(t, p):
                v.wait_ge(sm["down_mm"], t + 1)
                V.tensor_tensor(xt(t), ps[:, D0 + p, 0:D], xt(t), ALU.add).then_inc(sm["y_ready"], 1)

            def ffn(t, p, prev, nxt):
                logits(t, p)
                if prev:
                    residual3(t - 1, 1 - p)
                route(t, p)
                shared_h(t, p)
                for e in range(NE):
                    expert_h(t, p, e)
                    if e == 1 and nxt:
                        ln3(t + 1, 1 - p)

            ln3(0, 0)
            ffn(0, 0, False, True)
            ffn(1, 1, True, True)
            with v.Fori(2, TILES - 2, 2) as t:
                ffn(t, 0, True, True)
                ffn(t + 1, 1, True, True)
            ffn(TILES - 2, 0, True, True)
            ffn(TILES - 1, 1, True, False)
            residual3(TILES - 1, 1)


def kernel(**inputs):
    import concourse.bacc as _bacc
    from concourse import mybir as _mybir
    from concourse.bass_utils import run_bass_kernel_spmd as _run

    i = {k: np.asarray(v) for k, v in inputs.items()}

    def chunks(w, c=KC):
        return np.ascontiguousarray(w.reshape(c, w.shape[0] // c, w.shape[1]).transpose(1, 0, 2))

    def experts(w, c):
        return np.ascontiguousarray(w.reshape(NE, c, w.shape[1] // c, w.shape[2]).transpose(2, 0, 1, 3))

    pos = np.arange(P)
    slopes = (2.0 ** (-8.0 / HEADS * np.arange(1, HEADS + 1))).astype(np.float32)
    order = [c * 8 + j * 2 + h for j in range(4) for c in range(2) for h in range(2)]
    rel = (np.arange(S)[None, :] - (pos % S)[:, None]).astype(np.float32)
    alibi = slopes[order][None, :, None] * rel[:, None, :]
    arrays = {
        "x": i["x"], "ctx": i["ctx_2048"], "mask": i["mask_BxS2_bf1"].view(np.uint8),
        "ident": np.eye(P, dtype=np.float32),
        "block_mask": ((pos[:, None] % 32) // DH == np.arange(32)[None, :] // DH).astype(np.float32),
        "row_head": ((pos[:, None] % 32) // DH == np.arange(2)[None, :]).astype(np.float32),
        "row_half": (pos[:, None] // S == np.arange(2)[None, :]).astype(np.float32),
        "alibi": np.ascontiguousarray(alibi.reshape(P, HEADS * S)),
        "iota8": np.tile(np.arange(NE, dtype=np.float32), (P, 1)),
        "wq": chunks(i["L0_attn_wq"].T), "wkv": chunks(np.concatenate([i["L0_attn_wk"].T, i["L0_attn_wv"].T], 1)),
        "wo": chunks(i["L0_attn_wo"].T),
        "bq": np.ascontiguousarray(i["L0_attn_bq"].reshape(KC, P).T),
        "bkv": np.concatenate([i["L0_attn_bk"], i["L0_attn_bv"]]), "bo": i["L0_attn_bo"],
        "xwq": chunks(i["L0_xattn_Wq"]), "xwk": chunks(i["L0_xattn_Wk"]), "xwv": chunks(i["L0_xattn_Wv"]),
        "xwo": chunks(i["L0_xattn_Wo"]),
        "w_route": chunks(np.concatenate([i["L0_ffn_shw_gate"], i["L0_ffn_gate_w"].T, i["L0_ffn_shgate_w"][:, None]], 1)),
        "w_sh_up": chunks(i["L0_ffn_shw_up"]), "w_sh_down": np.ascontiguousarray(i["L0_ffn_shw_down"]),
        "w_gu": experts(np.concatenate([i["L0_ffn_w_gate"], i["L0_ffn_w_up"]], 2), KC),
        "w_down": experts(i["L0_ffn_w_down"], 2),
    }
    nc = _bacc.Bacc("TRN2", target_bir_lowering=False, num_devices=1)
    args, feeds = {}, {}
    for name, arr in arrays.items():
        feeds[f"in_{name}_dram"] = arr
        args[name] = nc.dram_tensor(f"in_{name}_dram", arr.shape, _mybir.dt.from_np(arr.dtype), kind="ExternalInput").ap()
    out = nc.dram_tensor("out_0_dram", (B, S, D), F32, kind="ExternalOutput").ap()
    build(nc, args, out)
    r = _run(nc, [feeds], core_ids=[0])
    return r.results[0]["out_0_dram"]
```

```python
from contextlib import ExitStack

import numpy as np

import concourse.bass as bass
from concourse import mybir

F32 = mybir.dt.float32
U32 = mybir.dt.uint32
I32 = mybir.dt.int32
U8 = mybir.dt.uint8
BF16 = mybir.dt.bfloat16
F32R = mybir.dt.float32r
ALU = mybir.AluOpType
ACT = mybir.ActivationFunctionType
AX = mybir.AxisListType

P = 128
B, S, D = 32, 64, 256
TILES = B * S // P
KC = D // P
HEADS, DH = 16, 16
GROUPS = 4
SEQS = P // S
HALF = HEADS // 2
NE, H = 8, 176
HC = H // 2
HS = 352
HS_LAST = HS - 2 * P
ROUTE = NE + 2

SLOT_TILES = 2 * TILES + NE

W_GU = 0
W_DOWN = W_GU + NE * KC * 2 * H
W_ROUTE = W_DOWN + NE * 2 * D
W_SHGATE = W_ROUTE + KC * ROUTE
W_SHUP = W_SHGATE + KC * HS
W_SHDOWN = W_SHUP + KC * HS
W_END = W_SHDOWN + 3 * D
FIRST_SPLIT = 2
W_PARTS = 12
W_PART = -(-W_END // (2 * W_PARTS)) * 2
W_ALL = W_PART * W_PARTS
STEADY = range(4, TILES - 2)
LN_EPS = 1e-5
DEN_EPS = 1e-8
BIG = float(np.finfo(np.float32).max)


def wait(eng, sem, count):
    if isinstance(count, int) and count <= 0:
        return
    eng.wait_ge(sem, count)


def has(t, ahead):
    return not isinstance(t, int) or 0 <= t + ahead < TILES


def splits(t):
    return not isinstance(t, int) or 0 <= t - FIRST_SPLIT < W_PARTS


def attention_iterations(eng, body, last):
    for t in range(-1, STEADY.start):
        body(t, t % 2)
    with eng.Fori(0, len(STEADY) // 2) as pair:
        t = STEADY.start + 2 * pair
        body(t, 0)
        body(t + 1, 1)
    for t in range(STEADY.stop, last):
        body(t, t % 2)


def spread(ap, axis, n):
    shape = list(ap.shape)
    shape[axis] = n
    return ap.broadcast_to(shape)


def build(nc, a, out):
    with ExitStack() as ctx:
        def sb(name, shape, dt=F32):
            return ctx.enter_context(nc.sbuf_tensor(name, shape, dt))

        def sem(name):
            return ctx.enter_context(nc.semaphore(name))

        ident = sb("ident", [P, P])
        neg_half = sb("neg_half", [P, 1])
        eps = sb("eps", [P, 1])
        minus_one = sb("minus_one", [P, 1])
        rev8 = sb("rev8", [P, NE])
        not_first = sb("not_first", [P, NE, TILES])
        iota_slot = sb("iota_slot", [1, SLOT_TILES])
        ones8 = sb("ones8", [P, NE])
        before = sb("before", [P, P])
        before_b = sb("before_b", [P, P], BF16)
        ones_b = sb("ones_b", [P, P], BF16)
        zeros = sb("zeros", [P, D])
        w_hi = sb("w_hi", [P, W_ALL], F32R)
        w_lo = sb("w_lo", [P, W_ALL], F32R)

        x_all = sb("x_all", [P, TILES, D])
        st3 = sb("st3", [P, 6])
        mv3 = sb("mv3", [P, 2])
        ve3 = sb("ve3", [P, 1])
        mean3 = sb("mean3", [P, TILES])
        rs3 = sb("rs3", [P, TILES])
        xn3 = sb("xn3", [P, 2, D])
        xh = sb("xh", [P, 2, KC, P], F32R)
        xl = sb("xl", [P, 2, KC, P], F32R)
        lg = sb("lg", [P, TILES, NE + 1])
        nmx = sb("nmx", [P, TILES])
        lgs = sb("lgs", [P, TILES, NE])
        pe8 = sb("pe8", [P, TILES, NE])
        psum8 = sb("psum8", [P, TILES])
        prec8 = sb("prec8", [P, TILES])
        prob = sb("prob", [P, TILES, NE])
        prob2 = sb("prob2", [P, TILES, NE])
        is_top = sb("is_top", [P, TILES, NE])
        top = sb("top", [P, 2, TILES])
        top_e = sb("top_e", [P, TILES])
        tsum = sb("tsum", [P, TILES])
        trec = sb("trec", [P, TILES])
        w_choice = sb("w_choice", [P, 2, TILES])
        hot = sb("hot", [P, 2, TILES, NE])
        hot_b = sb("hot_b", [P, 2, TILES * NE], BF16)
        in_tile = sb("in_tile", [P, NE, TILES])
        upto = sb("upto", [P, NE, TILES])
        rowf = sb("rowf", [P, TILES, NE])
        row_x = sb("row_x", [P, 2, TILES, NE])
        posf = sb("posf", [P, 2, TILES])
        pos = sb("pos", [P, 2, TILES], U32)
        pos_now = sb("pos_now", [P, 2, 2], U32)
        cnt_i = sb("cnt_i", [P, NE], I32)
        til_i = sb("til_i", [P, NE], I32)
        til = sb("til", [P, NE])
        cum = sb("cum", [P, NE])
        first = sb("first", [P, NE])
        ge = sb("ge", [1, SLOT_TILES, NE])
        slot_e = sb("slot_e", [1, SLOT_TILES])
        slot_ei = sb("slot_ei", [1, SLOT_TILES], I32)
        sgt = sb("sgt", [P, TILES])
        sg4 = sb("sg4", [P, TILES])
        with ExitStack() as attention:
            def sb_attn(name, shape, dt=F32):
                return attention.enter_context(nc.sbuf_tensor(name, shape, dt))
            wq = sb_attn("wq", [P, KC, D])
            wkv = sb_attn("wkv", [P, KC, 2 * D])
            wo = sb_attn("wo", [P, KC, D])
            bq1 = sb_attn("bq1", [P, KC])
            bkv = sb_attn("bkv", [P, 2 * D])
            bo = sb_attn("bo", [P, D])
            xwq = sb_attn("xwq", [P, KC, D])
            xwk = sb_attn("xwk", [P, KC, GROUPS * DH])
            xwk_rep = sb_attn("xwk_rep", [P, KC, GROUPS, HEADS // GROUPS, DH])
            xwv = sb_attn("xwv", [P, KC, GROUPS * DH])
            xwo = sb_attn("xwo", [P, KC, D])
            own_head = sb_attn("own_head", [P, HALF])
            block_mask = sb_attn("block_mask", [P, P])
            row_head = sb_attn("row_head", [P, 2])
            row_half = sb_attn("row_half", [P, 2])
            mask_u8 = sb_attn("mask_u8", [P, TILES, S], U8)
            st1 = sb_attn("st1", [P, 6])
            mv1 = sb_attn("mv1", [P, 2])
            rs1 = sb_attn("rs1", [P, 1])
            xn1 = sb_attn("xn1", [P, D])
            xn1T = sb_attn("xn1T", [P, KC, P])
            k1 = sb_attn("k1", [P, D])
            ke = sb_attn("ke", [P, D])
            kf = sb_attn("kf", [P, D])
            vo = sb_attn("vo", [P, HALF, 33])
            q1 = sb_attn("q1", [P, KC, P])
            qe = sb_attn("qe", [P, KC, P])
            qf = sb_attn("qf", [P, KC, P])
            kv_bd = sb_attn("kv_bd", [P, SEQS, 2, P + HALF])
            den = sb_attn("den", [P, 2, HALF])
            rden = sb_attn("rden", [P, 2, HALF])
            o = sb_attn("o", [P, D])
            oT = sb_attn("oT", [P, KC, P])
            ctx_sb = sb_attn("ctx_sb", [P, D])
            st2 = sb_attn("st2", [P, 6])
            mv2 = sb_attn("mv2", [P, 2])
            rs2 = sb_attn("rs2", [P, 1])
            xn2 = sb_attn("xn2", [P, D])
            xcT = sb_attn("xcT", [P, 2 * KC, P])
            q2T = sb_attn("q2T", [P, KC, P])
            k_bd = sb_attn("k_bd", [P, 2, 2, P])
            v_bd = sb_attn("v_bd", [P, 2, SEQS * GROUPS, 2, DH + 1])
            smax = sb_attn("smax", [P, HEADS])
            rsum = sb_attn("rsum", [P, HEADS])
            o2 = sb_attn("o2", [P, D])
            o2T = sb_attn("o2T", [P, KC, P])
            alibi = sb_attn("alibi", [P, HEADS * S])
            key_off = sb_attn("key_off", [P, TILES, S])
            bias_t = sb_attn("bias_t", [P, HEADS * S])
            sc = sb_attn("sc", [P, HEADS * S])
            pr = sb_attn("pr", [P, HEADS * S])
            prT = sb_attn("prT", [P, 8, P])
            w_stage = sb_attn("w_stage", [P, 2, W_PART])
        xn3_all = sb("xn3_all", [P, TILES, D])
        s_th = sb("s_th", [P, HS])
        s_gg = sb("s_gg", [P, HS])
        s_h = sb("s_h", [P, 2, HS])
        s_hh = sb("s_hh", [P, 2, 3, P], F32R)
        s_hl = sb("s_hl", [P, 2, 3, P], F32R)
        xs = sb("xs", [P, 4, D])
        e_th = sb("e_th", [P, 2, H])
        e_gg = sb("e_gg", [P, 2, H])
        e_h = sb("e_h", [P, 2, H])
        e_hh = sb("e_hh", [HC, 2, 2, P], F32R)
        e_hl = sb("e_hl", [HC, 2, 2, P], F32R)
        e_y = sb("e_y", [P, 4, D])
        yg = sb("yg", [P, 2, 2, D])
        y1 = sb("y1", [P, 2, D])
        y2 = sb("y2", [P, 2, D])

        xs_d = nc.dram_tensor("xs_rows", (SLOT_TILES * P, D), F32).ap()
        ys_d = nc.dram_tensor("ys_rows", (SLOT_TILES * P, D), F32).ap()

        ps = ctx.enter_context(nc.psum_tensor("ps", [P, 8, 512], F32))
        A0, A1, A2, A3, B0, B1, B2, B3 = range(8)
        TX, GT, UP, HT, DN, LG = 0, 1, 3, 5, 6, 7
        EX, EG, EH, ED = 0, 2, 4, 6

        names = """x_first x_rest w_self w_cross const_in ctx_in w_ffn consts_v consts_p
            ln1_st ln1_mv ln1_ve ln1_rs ln1_done xn1T_mm xn1T_ready kv_mm q_mm k1_ready ke_ready kf_ready
            v_ready q1_ready qe_ready qf_ready kvs_mm kvs_ready numden_mm den_ready rden_ready o_ready oT_mm oT_ready
            attn_mm xbo_ready x1_ready
            ln2_st ln2_mv ln2_ve ln2_rs ln2_done xcT_mm xcT_ready ckv_mm q2_mm kbd_ready vbd_ready q2T_ready
            scores_mm bias_ready sc_ready smax_ready sub_ready exp_ready rsum_ready o2_ready o2T_mm
            prT_mm prT_ready pv_mm o2T_ready xo_mm x2_ready
            w_part0 w_part1 w_hi_ready w_lo_ready zeros_ready zeroed
            ln3_st ln3_mv mean_kept ln3_ve ln3_rs ln3_done xT_mm xh_ready xl_ready route_mm kept
            routing lgs_ready pe8_ready lg_ready sgt_ready sg4_ready hotb_ready rank_mm pos_ready pos_now_ready slots_ready sent0 sent1
            s_x_ready s_xT_mm s_xh_ready s_xl_ready s_gate_mm s_up_mm
            s_th_ready s_gg_ready s_h_ready hT_mm s_hh_ready s_hl_ready s_down_mm x3_ready
            xs_in0 xs_in1 xs_in2 xs_in3
            e_xT_mm e_xh_ready e_xl_ready gu_mm e_th_ready e_gg_ready e_h_ready e_hT_mm e_hh_ready e_hl_ready
            e_down_mm e_y_ready ys_out0 ys_out1 ys_out2 ys_out3 gathered0 gathered1 y1_ready y_ready stored0 stored1
            dve_passed pe_passed pool_passed"""
        sm = {n: sem(n) for n in names.split()}

        x_d = a["x"].rearrange("b s d -> (b s) d").rearrange("(t p) d -> p t d", p=P)
        ctx_d = a["ctx"].rearrange("b s d -> (b s) d")
        out_d = out.rearrange("b s d -> (b s) d")

        def bcast(vec, n):
            return bass.AP(vec.tensor, vec.offset, [[0, P], [1, n]])

        W_SELF, W_CROSS, W_CONST = 6, 4, 10 + SEQS


        def alone(eng, passed):
            eng.sem_inc(passed, 1)

        block = ctx.enter_context(nc.Block())

        @block.sync
        def _(sp):
            sp.dma_start(x_all[:, 0:2, :], x_d[:, 0:2, :]).then_inc(sm["x_first"], 16)
            sp.dma_start(ident[:, :], a["ident"]).then_inc(sm["const_in"], 16)
            sp.dma_start(wkv[:, :, :], a["wkv"]).then_inc(sm["w_self"], 16)
            sp.dma_start(bkv[:, :], bcast(a["bkv"], 2 * D)).then_inc(sm["w_self"], 16)
            sp.dma_start(wq[:, :, :], a["wq"]).then_inc(sm["w_self"], 16)
            sp.dma_start(bq1[:, :], a["bq"]).then_inc(sm["w_self"], 16)
            sp.dma_start(block_mask[:, :], a["block_mask"]).then_inc(sm["const_in"], 16)
            sp.dma_start(own_head[:, :], a["own_head"]).then_inc(sm["const_in"], 16)
            sp.dma_start(row_head[:, :], a["row_head"]).then_inc(sm["const_in"], 16)
            sp.dma_start(row_half[:, :], a["row_half"]).then_inc(sm["const_in"], 16)
            sp.dma_start(rev8[:, :], a["rev8"]).then_inc(sm["const_in"], 16)
            sp.dma_start(not_first[:, :, :].rearrange("p e t -> p (e t)"), a["not_first"]).then_inc(sm["const_in"], 16)
            sp.dma_start(iota_slot[:, :], a["iota_slot"]).then_inc(sm["const_in"], 16)
            sp.dma_start(before[:, :], a["before"]).then_inc(sm["const_in"], 16)
            sp.dma_start(wo[:, :, :], a["wo"]).then_inc(sm["w_self"], 16)
            sp.dma_start(bo[:, :], bcast(a["bo"], D)).then_inc(sm["w_self"], 16)
            sp.dma_start(ctx_sb[:, :], ctx_d[0:P, :]).then_inc(sm["ctx_in"], 16)
            sp.dma_start(xwk[:, :, :], a["xwk"]).then_inc(sm["w_cross"], 16)
            sp.dma_start(xwv[:, :, :], a["xwv"]).then_inc(sm["w_cross"], 16)
            sp.dma_start(xwq[:, :, :], a["xwq"]).then_inc(sm["w_cross"], 16)
            sp.dma_start(xwo[:, :, :], a["xwo"]).then_inc(sm["w_cross"], 16)
            sp.dma_start(alibi[:, :], a["alibi"]).then_inc(sm["const_in"], 16)
            for s in range(SEQS):
                src = bass.AP(a["mask"].tensor, a["mask"].offset + s * S, [[0, S], [SEQS * S, TILES], [1, S]])
                sp.dma_start(mask_u8[s * S:(s + 1) * S, :, :], src).then_inc(sm["const_in"], 16)
            sp.dma_start(x_all[:, 2:TILES, :], x_d[:, 2:TILES, :]).then_inc(sm["x_rest"], 16)
            sp.wait_ge(sm["zeros_ready"], 1)
            sp.dma_start(xs_d.rearrange("(n p) d -> p n d", p=P),
                         spread(zeros[:, :].rearrange("p (o d) -> p o d", o=1), 1, SLOT_TILES)).then_inc(sm["zeroed"], 16)

            def next_ctx(t):
                sp.wait_ge(sm["xcT_mm"], t)
                sp.dma_start(ctx_sb[:, :], ctx_d[bass.ds(t * P, P), :]).then_inc(sm["ctx_in"], 16)

            def next_weights(c, half):
                wait(sp, sm["w_lo_ready"], c - 1)
                sp.dma_start(w_stage[:, half, :], a["w_ffn"][:, bass.ds(c * W_PART, W_PART)]).then_inc(sm[f"w_part{half}"], 16)

            next_ctx(1)
            next_weights(0, 0)
            next_weights(1, 1)
            next_ctx(2)
            with sp.Fori(0, W_PARTS // 2 - 1) as pair:
                c = 2 + 2 * pair
                next_ctx(c + 1)
                next_weights(c, 0)
                next_ctx(c + 2)
                next_weights(c + 1, 1)
            for t in range(W_PARTS + 1, TILES):
                next_ctx(t)

            def load_slots(i, q):
                wait(sp, sm["e_xT_mm"], i - 3)
                sp.dma_start(xs[:, q, :], xs_d[bass.ds(i * P, P), :]).then_inc(sm[f"xs_in{q}"], 16)

            def store_slots(i, q):
                sp.wait_ge(sm["e_y_ready"], i + 1)
                sp.dma_start(ys_d[bass.ds(i * P, P), :], e_y[:, q, :]).then_inc(sm[f"ys_out{q}"], 16)

            for p in range(2):
                sp.wait_ge(sm[f"sent{p}"], 16 * TILES)
            for i in range(6):
                load_slots(i, i % 4)
            load_slots(6, 2)
            store_slots(0, 0)
            load_slots(7, 3)
            store_slots(1, 1)
            with sp.Fori(2, SLOT_TILES // 4) as quad:
                i = 4 * quad
                for q in range(4):
                    load_slots(i + q, q)
                    store_slots(i + q - 6, (q + 2) % 4)
            for i in range(SLOT_TILES - 6, SLOT_TILES):
                store_slots(i, i % 4)

            def store_out(t, p):
                sp.wait_ge(sm["y_ready"], t + 1)
                sp.dma_start(out_d[bass.ds(t * P, P), :], y2[:, p, :]).then_inc(sm[f"stored{p}"], 16)
            with sp.Fori(0, TILES // 2) as pair:
                t = 2 * pair
                store_out(t, 0)
                store_out(t + 1, 1)
            for p in range(2):
                sp.wait_ge(sm[f"stored{p}"], 8 * TILES)

        @block.gpsimd
        def _(pool):
            nc.gpsimd.memset(neg_half[:, :], -0.5).then_inc(sm["consts_p"], 1)
            nc.gpsimd.memset(eps[:, :], LN_EPS).then_inc(sm["consts_p"], 1)
            pool.wait_ge(sm["consts_p"], 2)

            def rstd(mv, ve, rs, mv_sem, ve_sem, rs_sem, n):
                pool.wait_ge(mv_sem, n)
                nc.gpsimd.tensor_tensor(ve, mv, eps[:, :], ALU.add).then_inc(ve_sem, 1)
                pool.wait_ge(ve_sem, n)
                nc.gpsimd.tensor_tensor(rs, ve, neg_half[:, :], ALU.pow).then_inc(rs_sem, 1)

            def rstd1(t):
                wait(pool, sm["ln1_done"], t)
                rstd(mv1[:, 1:2], st1[:, 0:1], rs1[:, :], sm["ln1_mv"], sm["ln1_ve"], sm["ln1_rs"], t + 1)

            def rstd2(t):
                wait(pool, sm["ln2_done"], t)
                rstd(mv2[:, 1:2], st2[:, 0:1], rs2[:, :], sm["ln2_mv"], sm["ln2_ve"], sm["ln2_rs"], t + 1)

            def rstd3(t):
                wait(pool, sm["ln3_rs"], t)
                rstd(mv3[:, 1:2], ve3[:, :], rs3[:, bass.ds(t, 1)], sm["ln3_mv"], sm["ln3_ve"], sm["ln3_rs"], t + 1)

            def add_bo(t):
                pool.wait_ge(sm["ln1_done"], t + 1)
                xt = x_all[:, bass.ds(t, 1), :].rearrange("p t d -> p (t d)")
                nc.gpsimd.tensor_tensor(xt, xt, bo[:, :], ALU.add).then_inc(sm["xbo_ready"], 1)

            def score_bias(t):
                wait(pool, sm["sc_ready"], t)
                ko = spread(key_off[:, bass.ds(t, 1), :], 1, HEADS)
                nc.gpsimd.tensor_tensor(bias_t[:, :].rearrange("p (h k) -> p h k", h=HEADS),
                                        alibi[:, :].rearrange("p (h k) -> p h k", h=HEADS), ko,
                                        ALU.add).then_inc(sm["bias_ready"], 1)

            def subtract_max(t):
                pool.wait_ge(sm["smax_ready"], t + 1)
                v = sc[:, :].rearrange("p (h k) -> p h k", h=HEADS)
                nc.gpsimd.tensor_tensor(v, v, spread(smax[:, :].rearrange("p (h o) -> p h o", o=1), 2, S),
                                        ALU.subtract).then_inc(sm["sub_ready"], 1)

            def split_low(c, half):
                pool.wait_ge(sm["w_hi_ready"], c + 1)
                cols = bass.ds(c * W_PART, W_PART)
                nc.gpsimd.tensor_tensor(w_lo[:, cols], w_stage[:, half, :], w_hi[:, cols].bitcast(F32),
                                        ALU.subtract).then_inc(sm["w_lo_ready"], 1)

            def body(t, q):
                if has(t, -2):
                    subtract_max(t - 2)
                if has(t, 0):
                    add_bo(t)
                if has(t, -1):
                    score_bias(t - 1)
                if has(t, -3):
                    rstd3(t - 3)
                if has(t, 0):
                    rstd2(t)
                if splits(t):
                    split_low(t - FIRST_SPLIT, q)
                if has(t, 2):
                    rstd1(t + 2)

            nc.gpsimd.memset(zeros[:, :], 0.0).then_inc(sm["zeros_ready"], 1)
            rstd1(0)
            pool.wait_ge(sm["w_self"], 16 * W_SELF)
            pool.wait_ge(sm["consts_v"], 8)
            attention_iterations(pool, body, TILES + 3)

            pool.wait_ge(sm["zeroed"], 16)
            pool.wait_ge(sm["pos_ready"], 1)
            def rows_of(t, p, n, moved):
                wait(pool, sm[f"{moved}{p}"], 16 * (t - p))
                nc.gpsimd.tensor_copy(pos_now[:, p, :], pos[:, :, bass.ds(t, 1)].rearrange("p r t -> p (r t)")
                                      ).then_inc(sm["pos_now_ready"], 1)
                pool.wait_ge(sm["pos_now_ready"], n + t + 1)

            def send(t, p):
                rows_of(t, p, 0, "sent")
                pool.wait_ge(sm["s_x_ready"], t + 1)
                alone(pool, sm["pool_passed"])
                for r in range(2):
                    nc.gpsimd.indirect_dma_start(
                        out=xs_d[:, :], out_offset=bass.IndirectOffsetOnAxis(ap=pos_now[:, p, r:r + 1], axis=0),
                        in_=xn3[:, p, :], in_offset=None).then_inc(sm[f"sent{p}"], 16)

            send(0, 0)
            send(1, 1)
            with pool.Fori(1, TILES // 2) as pair:
                t = 2 * pair
                send(t, 0)
                send(t + 1, 1)

            def gather(t, p):
                rows_of(t, p, TILES, "gathered")
                wait(pool, sm["y_ready"], t - 1)
                alone(pool, sm["pool_passed"])
                for r in range(2):
                    nc.gpsimd.indirect_dma_start(
                        out=yg[:, p, r, :], out_offset=None, in_=ys_d[:, :],
                        in_offset=bass.IndirectOffsetOnAxis(ap=pos_now[:, p, r:r + 1], axis=0)).then_inc(sm[f"gathered{p}"], 16)

            for p in range(2):
                pool.wait_ge(sm[f"sent{p}"], 16 * TILES)
            for q in range(4):
                pool.wait_ge(sm[f"ys_out{q}"], 4 * SLOT_TILES)
            gather(0, 0)
            gather(1, 1)
            with pool.Fori(1, TILES // 2) as pair:
                t = 2 * pair
                gather(t, 0)
                gather(t + 1, 1)

        @block.tensor
        def _(pe):
            T = nc.tensor

            def transpose_x(t):
                pe.wait_ge(sm["ln1_done"], t + 1)
                for k in range(KC):
                    mm = T.transpose(ps[:, A0, k * P:(k + 1) * P], xn1[:, k * P:(k + 1) * P], ident[:, :])
                mm.then_inc(sm["xn1T_mm"], 1)

            def project_qkv(t):
                pe.wait_ge(sm["xn1T_ready"], t + 1)
                for k in range(KC):
                    mm = T.matmul(ps[:, A2, :], xn1T[:, k, :], wkv[:, k, :], start=(k == 0), stop=(k == KC - 1))
                mm.then_inc(sm["kv_mm"], 1)
                for c in range(KC):
                    for k in range(KC):
                        mm = T.matmul(ps[:, A0, (KC + c) * P:(KC + c + 1) * P], wq[:, k, c * P:(c + 1) * P], xn1T[:, k, :],
                                      start=(k == 0), stop=(k == KC - 1))
                mm.then_inc(sm["q_mm"], 1)

            def key_value(t):
                pe.wait_ge(sm["kf_ready"], t + 1)
                pe.wait_ge(sm["v_ready"], t + 1)
                wait(pe, sm["x1_ready"], t)
                alone(pe, sm["pe_passed"])
                for s in range(SEQS):
                    rows = slice(s * S, (s + 1) * S)
                    for c in range(2):
                        for j in range(4):
                            g = c * 4 + j
                            mm = T.matmul(ps[32 * j:32 * j + 32, (A2, A1)[s], c * 33:c * 33 + 33],
                                          kf[rows, g * 32:g * 32 + 32], vo[rows, g, :], start=True, stop=True)
                mm.then_inc(sm["kvs_mm"], 1)

            def query_kv(t):
                pe.wait_ge(sm["kvs_ready"], t + 1)
                pe.wait_ge(sm["qf_ready"], t + 1)
                for c in range(2):
                    for s in range(SEQS):
                        mm = T.matmul(ps[s * S:(s + 1) * S, A1, c * (P + HALF):(c + 1) * (P + HALF)],
                                      qf[:, c, s * S:(s + 1) * S], kv_bd[:, s, c, :], start=True, stop=True)
                mm.then_inc(sm["numden_mm"], 1)

            def transpose_o(t):
                pe.wait_ge(sm["o_ready"], t + 1)
                for k in range(KC):
                    mm = T.transpose(ps[:, A1, k * P:(k + 1) * P], o[:, k * P:(k + 1) * P], ident[:, :])
                mm.then_inc(sm["oT_mm"], 1)

            def project_attn(t):
                pe.wait_ge(sm["oT_ready"], t + 1)
                for k in range(KC):
                    mm = T.matmul(ps[:, A1, 0:D], oT[:, k, :], wo[:, k, :], start=(k == 0), stop=(k == KC - 1))
                mm.then_inc(sm["attn_mm"], 1)

            def transpose_xc(t):
                pe.wait_ge(sm["ctx_in"], 16 * (t + 1))
                pe.wait_ge(sm["q1_ready"], 2 * (t + 2 if has(t, 1) else t + 1))
                for k in range(KC):
                    T.transpose(ps[:, A0, (KC + k) * P:(KC + k + 1) * P], ctx_sb[:, k * P:(k + 1) * P], ident[:, :])
                pe.wait_ge(sm["ln2_done"], t + 1)
                for k in range(KC):
                    mm = T.transpose(ps[:, A0, k * P:(k + 1) * P], xn2[:, k * P:(k + 1) * P], ident[:, :])
                mm.then_inc(sm["xcT_mm"], 1)

            def project_ctx(t):
                pe.wait_ge(sm["xcT_ready"], t + 1)
                wait(pe, sm["sc_ready"], t)
                for c in range(2):
                    for k in range(KC):
                        T.matmul(ps[:, B2, c * P:(c + 1) * P],
                                 xwk_rep[:, k, 2 * c:2 * c + 2, :, :].rearrange("p g h d -> p (g h d)"),
                                 xcT[:, KC + k, :], start=(k == 0), stop=(k == KC - 1))
                for s in range(SEQS):
                    for r in range(2):
                        for k in range(KC):
                            mm = T.matmul(ps[r * S:(r + 1) * S, B2, 256 + s * S:256 + (s + 1) * S],
                                          xcT[:, KC + k, s * S:(s + 1) * S], xwv[:, k, :],
                                          start=(k == 0), stop=(k == KC - 1))
                mm.then_inc(sm["ckv_mm"], 1)

            def project_q2(t):
                for c in range(KC):
                    for k in range(KC):
                        mm = T.matmul(ps[:, B3, c * P:(c + 1) * P], xwq[:, k, c * P:(c + 1) * P], xcT[:, k, :],
                                      start=(k == 0), stop=(k == KC - 1))
                mm.then_inc(sm["q2_mm"], 1)

            def scores(t, c):
                if c == 0:
                    pe.wait_ge(sm["q2T_ready"], t + 1)
                    pe.wait_ge(sm["kbd_ready"], t + 1)
                    pe.wait_ge(sm["vbd_ready"], t + 1)
                    wait(pe, sm["prT_ready"], 2 * t)
                    alone(pe, sm["pe_passed"])
                for j in range(4):
                    q = slice(32 * j, 32 * j + 32)
                    for s in range(SEQS):
                        mm = T.matmul(ps[s * S:(s + 1) * S, B0 + j, c * P:(c + 1) * P],
                                      q2T[q, c, s * S:(s + 1) * S], k_bd[q, c, :, s * S:(s + 1) * S],
                                      start=True, stop=True)
                if c == 1:
                    mm.then_inc(sm["scores_mm"], 1)

            def transpose_probs(t):
                pe.wait_ge(sm["exp_ready"], t + 1)
                for b in range(8):
                    mm = T.transpose(ps[:, B0 + b // 4, (b % 4) * P:(b % 4 + 1) * P], pr[:, b * P:(b + 1) * P],
                                     ident[:, :])
                mm.then_inc(sm["prT_mm"], 1)

            def probs_values(t, q):
                pe.wait_ge(sm["prT_ready"], 2 * (t + 1))
                wait(pe, sm["x2_ready"], t)
                alone(pe, sm["pe_passed"])
                for c in range(2):
                    for j in range(4):
                        for s in range(SEQS):
                            col = (c * 4 + j) * 2 * (DH + 1)
                            mm = T.matmul(ps[s * S:(s + 1) * S, A3, col:col + 2 * (DH + 1)],
                                          prT[:, 2 * j + c, s * S:(s + 1) * S],
                                          v_bd[:, q, s * GROUPS + 2 * c + j // 2, :, :].rearrange("p h e -> p (h e)"),
                                          start=True, stop=True)
                mm.then_inc(sm["pv_mm"], 1)

            def transpose_o2(t):
                pe.wait_ge(sm["o2_ready"], t + 1)
                for k in range(KC):
                    mm = T.transpose(ps[:, A3, k * P:(k + 1) * P], o2[:, k * P:(k + 1) * P], ident[:, :])
                mm.then_inc(sm["o2T_mm"], 1)

            def project_cross(t):
                pe.wait_ge(sm["o2T_ready"], t + 1)
                for k in range(KC):
                    mm = T.matmul(ps[:, A3, 0:D], o2T[:, k, :], xwo[:, k, :], start=(k == 0), stop=(k == KC - 1))
                mm.then_inc(sm["xo_mm"], 1)

            def body(t, q):
                if has(t, 0):
                    key_value(t)
                if has(t, -1):
                    if not has(t, -2):
                        pe.wait_ge(sm["consts_v"], 8)
                    project_ctx(t - 1)
                if has(t, 0):
                    query_kv(t)
                if has(t, -1):
                    project_q2(t - 1)
                if has(t, 1):
                    transpose_x(t + 1)
                if has(t, 0):
                    transpose_o(t)
                if has(t, -2):
                    transpose_probs(t - 2)
                if has(t, 0):
                    project_attn(t)
                if has(t, 1):
                    project_qkv(t + 1)
                if has(t, -2):
                    probs_values(t - 2, q)
                if has(t, -1):
                    scores(t - 1, 0)
                if has(t, -2):
                    transpose_o2(t - 2)
                if has(t, -1):
                    scores(t - 1, 1)
                if has(t, 0):
                    transpose_xc(t)
                if has(t, -2):
                    project_cross(t - 2)

            pe.wait_ge(sm["const_in"], 16 * W_CONST)
            pe.wait_ge(sm["w_self"], 16 * W_SELF)
            pe.wait_ge(sm["w_cross"], 16 * W_CROSS)
            attention_iterations(pe, body, TILES + 2)

            def product(out_ap, hi, lo, rows, cols, first, last):
                for lhs, rhs, st, en in ((hi, w_hi, first, False), (hi, w_lo, False, False), (lo, w_hi, False, last)):
                    mm = T.matmul(out_ap, lhs, rhs[rows, cols], start=st, stop=en)
                return mm

            def transpose_x3(t, p):
                pe.wait_ge(sm["ln3_done"], t + 1)
                wait(pe, sm["xl_ready"], t - 1)
                for k in range(KC):
                    mm = T.transpose(ps[:, (TX, HT)[p], k * P:(k + 1) * P], xn3[:, p, k * P:(k + 1) * P], ident[:, :])
                mm.then_inc(sm["xT_mm"], 1)

            def router(t, p):
                pe.wait_ge(sm["xl_ready"], t + 1)
                for k in range(KC):
                    mm = product(ps[:, LG, bass.ds(t * ROUTE, ROUTE)], xh[:, p, k, :], xl[:, p, k, :], slice(0, P),
                                 slice(W_ROUTE + k * ROUTE, W_ROUTE + (k + 1) * ROUTE), k == 0, k == KC - 1)
                mm.then_inc(sm["route_mm"], 1)

            pe.wait_ge(sm["w_lo_ready"], W_PARTS)
            pe.wait_ge(sm["x2_ready"], TILES)
            transpose_x3(0, 0)
            transpose_x3(1, 1)
            router(0, 0)
            with pe.Fori(1, TILES // 2) as pair:
                t = 2 * pair
                transpose_x3(t, 0)
                router(t - 1, 1)
                transpose_x3(t + 1, 1)
                router(t, 0)
            router(TILES - 1, 1)

            def ranks():
                pe.wait_ge(sm["hotb_ready"], 1)
                for r in range(2):
                    T.matmul(ps[:, LG, 0:NE * TILES], before_b[:, :], hot_b[:, r, :], start=(r == 0), stop=(r == 1))
                for r in range(2):
                    mm = T.matmul(ps[:, LG, NE * TILES:2 * NE * TILES], ones_b[:, :], hot_b[:, r, :], start=(r == 0), stop=(r == 1))
                mm.then_inc(sm["rank_mm"], 1)

            def transpose_sx(t, p):
                pe.wait_ge(sm["s_x_ready"], t + 1)
                wait(pe, sm["s_xl_ready"], t)
                for k in range(KC):
                    mm = T.transpose(ps[:, TX, k * P:(k + 1) * P], xn3[:, p, k * P:(k + 1) * P], ident[:, :])
                mm.then_inc(sm["s_xT_mm"], 1)

            def shared_gate_up(t, p):
                pe.wait_ge(sm["s_xl_ready"], t + 1)
                wait(pe, sm["s_h_ready"], t - 1)
                for bank, base, done in ((GT, W_SHGATE, "s_gate_mm"), (UP, W_SHUP, "s_up_mm")):
                    for k in range(KC):
                        mm = product(ps[:, bank + p, 0:HS], xh[:, p, k, :], xl[:, p, k, :], slice(0, P),
                                     slice(base + k * HS, base + (k + 1) * HS), k == 0, k == KC - 1)
                    mm.then_inc(sm[done], 1)

            def transpose_sh(t, p):
                pe.wait_ge(sm["s_h_ready"], t + 1)
                wait(pe, sm["s_hl_ready"], t)
                T.transpose(ps[:, HT, 0:P], s_h[:, p, 0:P], ident[:, :])
                T.transpose(ps[:, HT, P:2 * P], s_h[:, p, P:2 * P], ident[:, :])
                T.transpose(ps[0:HS_LAST, HT, 2 * P:3 * P], s_h[:, p, 2 * P:HS], ident[:, :]).then_inc(sm["hT_mm"], 1)

            def shared_down(t, p):
                pe.wait_ge(sm["s_hl_ready"], t + 1)
                wait(pe, sm["x3_ready"], t)
                for c in range(3):
                    rows = slice(0, P if c < 2 else HS_LAST)
                    mm = product(ps[:, DN, 0:D], s_hh[rows, p, c, :], s_hl[rows, p, c, :], rows,
                                 slice(W_SHDOWN + c * D, W_SHDOWN + (c + 1) * D), c == 0, c == 2)
                mm.then_inc(sm["s_down_mm"], 1)

            def shared(t, p, prev, prev2, nxt):
                shared_gate_up(t, p)
                if nxt:
                    transpose_sx(t + 1, 1 - p)
                if prev:
                    transpose_sh(t - 1, 1 - p)
                if prev2:
                    shared_down(t - 2, p)

            pe.wait_ge(sm["xl_ready"], TILES)
            transpose_sx(0, 0)
            shared(0, 0, False, False, True)
            ranks()
            shared(1, 1, True, False, True)
            with pe.Fori(1, TILES // 2 - 1) as pair:
                t = 2 * pair
                shared(t, 0, True, True, True)
                shared(t + 1, 1, True, True, True)
            shared(TILES - 2, 0, True, True, True)
            shared(TILES - 1, 1, True, True, False)
            shared_down(TILES - 2, 0)
            transpose_sh(TILES - 1, 1)
            shared_down(TILES - 1, 1)

            def expert_of(i):
                return pe.value_load(slot_ei[0:1, i:i + 1], min_val=0, max_val=NE - 1)

            def transpose_slots(i, q):
                p = q % 2
                pe.wait_ge(sm[f"xs_in{q}"], 4 * (i - q) + 16)
                wait(pe, sm["e_xl_ready"], i - 1)
                for k in range(KC):
                    mm = T.transpose(ps[:, EX + p, k * P:(k + 1) * P], xs[:, q, k * P:(k + 1) * P], ident[:, :])
                mm.then_inc(sm["e_xT_mm"], 1)

            def gate_up(i, p, e):
                pe.wait_ge(sm["e_xl_ready"], i + 1)
                wait(pe, sm["e_h_ready"], i - 1)
                for k in range(KC):
                    mm = product(ps[:, EG + p, 0:2 * H], xh[:, p, k, :], xl[:, p, k, :], slice(0, P),
                                 bass.ds(e * (KC * 2 * H) + (W_GU + k * 2 * H), 2 * H), k == 0, k == KC - 1)
                mm.then_inc(sm["gu_mm"], 1)

            def transpose_h(i, p):
                pe.wait_ge(sm["e_h_ready"], i + 1)
                wait(pe, sm["e_hl_ready"], i - 1)
                for c in range(2):
                    mm = T.transpose(ps[0:HC, EH + p, c * P:(c + 1) * P], e_h[:, p, c * HC:(c + 1) * HC], ident[:, :])
                mm.then_inc(sm["e_hT_mm"], 1)

            def expert_down(i, p, e):
                pe.wait_ge(sm["e_hl_ready"], i + 1)
                wait(pe, sm["e_y_ready"], i - 1)
                for c in range(2):
                    mm = product(ps[:, ED + p, 0:D], e_hh[:, p, c, :], e_hl[:, p, c, :], slice(0, HC),
                                 bass.ds(e * (2 * D) + (W_DOWN + c * D), D), c == 0, c == 1)
                mm.then_inc(sm["e_down_mm"], 1)

            pe.wait_ge(sm["slots_ready"], 1)
            pe.wait_ge(sm["x3_ready"], TILES)
            transpose_slots(0, 0)
            transpose_slots(1, 1)
            expert = {}
            for i in range(SLOT_TILES + 2):
                p = i % 2
                if i < SLOT_TILES:
                    expert[i] = expert_of(i)
                    gate_up(i, p, expert[i])
                if 1 <= i <= SLOT_TILES:
                    transpose_h(i - 1, 1 - p)
                if i + 2 < SLOT_TILES:
                    transpose_slots(i + 2, (i + 2) % 4)
                if i >= 2:
                    expert_down(i - 2, p, expert[i - 2])

        @block.scalar
        def _(act):
            A = nc.scalar
            def k_exp(t):
                act.wait_ge(sm["k1_ready"], t + 1)
                wait(act, sm["kf_ready"], t)
                A.activation(ke[:, :], k1[:, :], ACT.Exp, bias=minus_one[:, :]).then_inc(sm["ke_ready"], 1)

            def q_exp(t):
                act.wait_ge(sm["q_mm"], t + 1)
                wait(act, sm["qf_ready"], t)
                for c in range(KC):
                    A.activation(q1[:, c, :], ps[:, A0, (KC + c) * P:(KC + c + 1) * P], ACT.Identity,
                                 bias=bq1[:, c:c + 1]).then_inc(sm["q1_ready"], 1)
                act.wait_ge(sm["q1_ready"], 2 * (t + 1))
                A.activation(qe[:, :, :], q1[:, :, :], ACT.Exp, bias=minus_one[:, :]).then_inc(sm["qe_ready"], 1)

            def copy_xcT(t):
                act.wait_ge(sm["xcT_mm"], t + 1)
                wait(act, sm["q2_mm"], t)
                A.activation(xcT[:, :, :].rearrange("p c t -> p (c t)"), ps[:, A0, :], ACT.Copy).then_inc(sm["xcT_ready"], 1)

            def copy_prT(t):
                act.wait_ge(sm["prT_mm"], t + 1)
                wait(act, sm["pv_mm"], t)
                for b in range(2):
                    A.activation(prT[:, 4 * b:4 * b + 4, :].rearrange("p c t -> p (c t)"), ps[:, B0 + b, :],
                                 ACT.Copy).then_inc(sm["prT_ready"], 1)

            def scale_q2(t):
                act.wait_ge(sm["q2_mm"], t + 1)
                wait(act, sm["scores_mm"], t)
                A.activation(q2T[:, :, :].rearrange("p c t -> p (c t)"), ps[:, B3, 0:D], ACT.Copy,
                             scale=DH ** -0.5).then_inc(sm["q2T_ready"], 1)

            def copy_oT(t):
                act.wait_ge(sm["oT_mm"], t + 1)
                wait(act, sm["attn_mm"], t)
                A.activation(oT[:, :, :].rearrange("p c t -> p (c t)"), ps[:, A1, 0:D], ACT.Copy).then_inc(sm["oT_ready"], 1)

            def copy_o2T(t):
                act.wait_ge(sm["o2T_mm"], t + 1)
                wait(act, sm["xo_mm"], t)
                A.activation(o2T[:, :, :].rearrange("p c t -> p (c t)"), ps[:, A3, 0:D], ACT.Copy).then_inc(sm["o2T_ready"], 1)

            def copy_xn1T(t):
                act.wait_ge(sm["xn1T_mm"], t + 1)
                wait(act, sm["q_mm"], t)
                A.activation(xn1T[:, :, :].rearrange("p c t -> p (c t)"), ps[:, A0, 0:D], ACT.Copy).then_inc(sm["xn1T_ready"], 1)

            def score_exp(t):
                act.wait_ge(sm["sub_ready"], t + 1)
                wait(act, sm["prT_mm"], t)
                A.activation(pr[:, :], sc[:, :], ACT.Exp).then_inc(sm["exp_ready"], 1)

            def split_high(c, half):
                act.wait_ge(sm[f"w_part{half}"], 8 * (c - half) + 16)
                A.activation(w_hi[:, bass.ds(c * W_PART, W_PART)], w_stage[:, half, :], ACT.Copy).then_inc(sm["w_hi_ready"], 1)

            def body(t, q):
                if has(t, -2):
                    score_exp(t - 2)
                if has(t, -1):
                    scale_q2(t - 1)
                if has(t, 1):
                    copy_xn1T(t + 1)
                if has(t, 0):
                    copy_oT(t)
                if has(t, -2):
                    copy_prT(t - 2)
                if splits(t):
                    split_high(t - FIRST_SPLIT, q)
                if has(t, 1):
                    k_exp(t + 1)
                    q_exp(t + 1)
                if has(t, -2):
                    copy_o2T(t - 2)
                if has(t, 0):
                    copy_xcT(t)

            act.wait_ge(sm["consts_v"], 4)
            attention_iterations(act, body, TILES + 2)

            def x_high(t, p):
                act.wait_ge(sm["xT_mm"], t + 1)
                wait(act, sm["route_mm"], t - 1)
                A.activation(xh[:, p, :, :].rearrange("p c t -> p (c t)"), ps[:, (TX, HT)[p], 0:D], ACT.Copy).then_inc(sm["xh_ready"], 1)

            def keep(t, p):
                act.wait_ge(sm["ln3_done"], t + 1)
                A.activation(xn3_all[:, bass.ds(t, 1), :].rearrange("p t d -> p (t d)"), xn3[:, p, :], ACT.Copy).then_inc(sm["kept"], 1)

            x_high(0, 0)
            keep(0, 0)
            x_high(1, 1)
            keep(1, 1)
            with act.Fori(1, TILES // 2) as pair:
                t = 2 * pair
                for p in range(2):
                    x_high(t + p, p)
                    keep(t + p, p)

            def shared_x(t, p):
                wait(act, sm["s_xT_mm"], t - 1)
                wait(act, sm[f"sent{p}"], 16 * (t - p))
                A.activation(xn3[:, p, :], xn3_all[:, bass.ds(t, 1), :].rearrange("p t d -> p (t d)"), ACT.Copy).then_inc(sm["s_x_ready"], 1)

            def shared_x_high(t, p):
                act.wait_ge(sm["s_xT_mm"], t + 1)
                wait(act, sm["s_up_mm"], t - 1)
                A.activation(xh[:, p, :, :].rearrange("p c t -> p (c t)"), ps[:, TX, 0:D], ACT.Copy).then_inc(sm["s_xh_ready"], 1)

            def shared_tanh(t, p):
                act.wait_ge(sm["s_gate_mm"], t + 1)
                wait(act, sm["s_gg_ready"], t)
                A.activation(s_th[:, :], ps[:, GT + p, 0:HS], ACT.Tanh, scale=0.5).then_inc(sm["s_th_ready"], 1)

            def sh_high(t, p):
                act.wait_ge(sm["hT_mm"], t + 1)
                wait(act, sm["s_down_mm"], t - 1)
                A.activation(s_hh[:, p, 0:2, :].rearrange("p c t -> p (c t)"), ps[:, HT, 0:2 * P], ACT.Copy)
                A.activation(s_hh[0:HS_LAST, p, 2, :], ps[0:HS_LAST, HT, 2 * P:3 * P], ACT.Copy).then_inc(sm["s_hh_ready"], 1)

            def shared(t, p, prev, nxt, nxt2):
                shared_tanh(t, p)
                if nxt:
                    shared_x_high(t + 1, 1 - p)
                if prev:
                    sh_high(t - 1, 1 - p)
                if nxt2:
                    shared_x(t + 2, p)

            act.wait_ge(sm["xT_mm"], TILES)
            act.wait_ge(sm["kept"], TILES)
            shared_x(0, 0)
            shared_x(1, 1)
            act.wait_ge(sm["route_mm"], TILES)
            shared_x_high(0, 0)
            act.wait_ge(sm["lg_ready"], 1)
            A.activation(sgt[:, :], lg[:, :, NE:NE + 1].rearrange("p t o -> p (t o)"), ACT.Tanh, scale=0.5).then_inc(sm["sgt_ready"], 1)
            act.wait_ge(sm["lgs_ready"], 1)
            A.activation(pe8[:, :, :], lgs[:, :, :], ACT.Exp).then_inc(sm["pe8_ready"], 1)
            shared(0, 0, False, True, True)
            shared(1, 1, True, True, True)
            with act.Fori(1, TILES // 2 - 1) as pair:
                t = 2 * pair
                shared(t, 0, True, True, True)
                shared(t + 1, 1, True, True, True)
            shared(TILES - 2, 0, True, True, False)
            shared(TILES - 1, 1, True, False, False)
            sh_high(TILES - 1, 1)

            def slots_high(i, p):
                act.wait_ge(sm["e_xT_mm"], i + 1)
                A.activation(xh[:, p, :, :].rearrange("p c t -> p (c t)"), ps[:, EX + p, 0:D], ACT.Copy).then_inc(sm["e_xh_ready"], 1)

            def expert_tanh(i, p):
                act.wait_ge(sm["gu_mm"], i + 1)
                wait(act, sm["e_gg_ready"], i - 1)
                A.activation(e_th[:, p, :], ps[:, EG + p, 0:H], ACT.Tanh, scale=0.5).then_inc(sm["e_th_ready"], 1)

            def h_high(i, p):
                act.wait_ge(sm["e_hT_mm"], i + 1)
                wait(act, sm["e_down_mm"], i - 1)
                A.activation(e_hh[:, p, :, :].rearrange("p c t -> p (c t)"), ps[0:HC, EH + p, 0:2 * P], ACT.Copy).then_inc(sm["e_hh_ready"], 1)

            def copy_y(i, q):
                act.wait_ge(sm["e_down_mm"], i + 1)
                wait(act, sm[f"ys_out{q}"], 4 * (i - q))
                A.activation(e_y[:, q, :], ps[:, ED + q % 2, 0:D], ACT.Copy).then_inc(sm["e_y_ready"], 1)

            def experts(i, q, prev, prev2, nxt2):
                p = q % 2
                expert_tanh(i, p)
                if prev:
                    h_high(i - 1, 1 - p)
                if nxt2:
                    slots_high(i + 2, p)
                if prev2:
                    copy_y(i - 2, (q + 2) % 4)

            slots_high(0, 0)
            slots_high(1, 1)
            for i in range(8):
                experts(i, i % 4, i >= 1, i >= 2, True)
            with act.Fori(2, SLOT_TILES // 4 - 1) as quad:
                i = 4 * quad
                for q in range(4):
                    experts(i + q, q, True, True, True)
            for q in range(4):
                experts(SLOT_TILES - 4 + q, q, True, True, q < 2)
            h_high(SLOT_TILES - 1, 1)
            copy_y(SLOT_TILES - 2, 2)
            copy_y(SLOT_TILES - 1, 3)

        @block.vector
        def _(v):
            V = nc.vector

            def xt(t):
                return x_all[:, bass.ds(t, 1), :].rearrange("p t d -> p (t d)")

            V.memset(minus_one[:, :], -1.0).then_inc(sm["consts_v"], 1)
            V.memset(vo[:, :, 32:33], 1.0).then_inc(sm["consts_v"], 1)

            def ln1_stats(t):
                wait(v, sm["ln1_rs"], t)
                wait(v, sm["ln1_done"], t)
                alone(v, sm["dve_passed"])
                V.bn_stats(st1[:, :], xt(t)).then_inc(sm["ln1_st"], 1)
                v.wait_ge(sm["ln1_st"], t + 1)
                alone(v, sm["dve_passed"])
                V.bn_aggr(mv1[:, :], st1[:, :]).then_inc(sm["ln1_mv"], 1)

            def ln1_norm(t):
                v.wait_ge(sm["ln1_rs"], t + 1)
                wait(v, sm["xn1T_mm"], t)
                V.tensor_scalar(xn1[:, :], xt(t), mv1[:, 0:1], rs1[:, :], ALU.subtract, ALU.mult).then_inc(sm["ln1_done"], 1)

            def k_v_bias(t):
                v.wait_ge(sm["kv_mm"], t + 1)
                wait(v, sm["kf_ready"], t)
                V.tensor_tensor(k1[:, :], ps[:, A2, 0:D], bkv[:, 0:D], ALU.add).then_inc(sm["k1_ready"], 1)
                wait(v, sm["kvs_mm"], t)
                V.tensor_tensor(vo[:, :, 0:32], ps[:, A2, D:2 * D].rearrange("p (g e) -> p g e", e=32),
                                bkv[:, D:2 * D].rearrange("p (g e) -> p g e", e=32), ALU.add).then_inc(sm["v_ready"], 1)

            def k_feature(t):
                v.wait_ge(sm["ke_ready"], t + 1)
                V.scalar_tensor_tensor(out=kf[:, :], in0=k1[:, :], scalar=1.0, in1=ke[:, :], op0=ALU.max,
                                       op1=ALU.min).then_inc(sm["kf_ready"], 1)

            def q_feature(t):
                v.wait_ge(sm["qe_ready"], t + 1)
                wait(v, sm["numden_mm"], t)
                V.scalar_tensor_tensor(out=qf[:, :, :].rearrange("p c t -> p (c t)"),
                                       in0=q1[:, :, :].rearrange("p c t -> p (c t)"), scalar=1.0,
                                       in1=qe[:, :, :].rearrange("p c t -> p (c t)"), op0=ALU.max,
                                       op1=ALU.min).then_inc(sm["qf_ready"], 1)

            def block_diagonal(t):
                v.wait_ge(sm["kvs_mm"], t + 1)
                wait(v, sm["numden_mm"], t)
                for s in range(SEQS):
                    g = ps[:, (A2, A1)[s], 0:66].rearrange("p (c o e) -> p c o e", o=1, e=33)
                    bm = spread(block_mask[:, :].rearrange("p (o j e) -> p o j e", o=1, e=32), 1, 2)
                    oh = spread(own_head[:, :].rearrange("p (o j) -> p o j", o=1), 1, 2)
                    V.tensor_tensor(kv_bd[:, s, :, 0:P].rearrange("p c (j e) -> p c j e", e=32),
                                    spread(g[:, :, :, 0:32], 2, 4), bm, ALU.mult)
                    last = V.tensor_tensor(kv_bd[:, s, :, P:P + HALF],
                                           spread(g[:, :, :, 32:33].rearrange("p c o e -> p c (o e)"), 2, HALF), oh, ALU.mult)
                last.then_inc(sm["kvs_ready"], 1)

            def divide(t):
                nd = ps[:, A1, 0:2 * (P + HALF)].rearrange("p (c n) -> p c n", c=2)
                v.wait_ge(sm["numden_mm"], t + 1)
                V.tensor_scalar(den[:, :, :], nd[:, :, P:P + HALF], DEN_EPS, None, ALU.add).then_inc(sm["den_ready"], 1)
                v.wait_ge(sm["den_ready"], t + 1)
                V.reciprocal(rden[:, :, :], den[:, :, :]).then_inc(sm["rden_ready"], 1)
                v.wait_ge(sm["rden_ready"], t + 1)
                wait(v, sm["oT_mm"], t)
                V.tensor_tensor(o[:, :].rearrange("p (c h e) -> p c h e", c=2, e=DH),
                                nd[:, :, 0:P].rearrange("p c (h e) -> p c h e", e=DH),
                                spread(rden[:, :, :].rearrange("p c (h o) -> p c h o", o=1), 3, DH),
                                ALU.mult).then_inc(sm["o_ready"], 1)

            def residual1(t):
                v.wait_ge(sm["attn_mm"], t + 1)
                v.wait_ge(sm["xbo_ready"], t + 1)
                V.tensor_tensor(xt(t), ps[:, A1, 0:D], xt(t), ALU.add).then_inc(sm["x1_ready"], 1)

            def ln2_stats(t):
                v.wait_ge(sm["x1_ready"], t + 1)
                wait(v, sm["ln2_rs"], t)
                wait(v, sm["ln2_done"], t)
                alone(v, sm["dve_passed"])
                V.bn_stats(st2[:, :], xt(t)).then_inc(sm["ln2_st"], 1)
                v.wait_ge(sm["ln2_st"], t + 1)
                alone(v, sm["dve_passed"])
                V.bn_aggr(mv2[:, :], st2[:, :]).then_inc(sm["ln2_mv"], 1)

            def ln2_norm(t):
                v.wait_ge(sm["ln2_rs"], t + 1)
                wait(v, sm["xcT_mm"], t)
                V.tensor_scalar(xn2[:, :], xt(t), mv2[:, 0:1], rs2[:, :], ALU.subtract, ALU.mult).then_inc(sm["ln2_done"], 1)

            def k_block(t):
                v.wait_ge(sm["ckv_mm"], t + 1)
                wait(v, sm["scores_mm"], t)
                for c in range(2):
                    kk = spread(ps[:, B2, c * P:(c + 1) * P].rearrange("p (o t) -> p o t", o=1), 1, 2)
                    last = V.tensor_tensor(k_bd[:, c, :, :], kk,
                                           spread(row_head[:, :].rearrange("p (h o) -> p h o", o=1), 2, P), ALU.mult)
                last.then_inc(sm["kbd_ready"], 1)

            def v_block(t, q):
                wait(v, sm["pv_mm"], t - 1)
                vv = ps[:, B2, 256:384].rearrange("p (g e) -> p g e", e=DH)
                for h in range(2):
                    last = V.tensor_scalar(v_bd[:, q, :, h, 0:DH], vv, row_half[:, h:h + 1], None, ALU.mult)
                last.then_inc(sm["vbd_ready"], 1)

            def score_max(t):
                v.wait_ge(sm["scores_mm"], t + 1)
                v.wait_ge(sm["bias_ready"], t + 1)
                wait(v, sm["exp_ready"], t)
                V.tensor_tensor(sc[:, :].rearrange("p (j c) -> p j c", j=4), ps[:, B0:B3 + 1, 0:256],
                                bias_t[:, :].rearrange("p (j c) -> p j c", j=4), ALU.add).then_inc(sm["sc_ready"], 1)
                v.wait_ge(sm["sc_ready"], t + 1)
                wait(v, sm["sub_ready"], t)
                V.tensor_reduce(smax[:, :], sc[:, :].rearrange("p (h k) -> p h k", h=HEADS), AX.X,
                                ALU.max).then_inc(sm["smax_ready"], 1)

            def scale_values(t):
                nd = ps[:, A3, 0:HEADS * (DH + 1)].rearrange("p (h e) -> p h e", e=DH + 1)
                v.wait_ge(sm["pv_mm"], t + 1)
                V.reciprocal(rsum[:, :], nd[:, :, DH:DH + 1].rearrange("p h o -> p (h o)")).then_inc(sm["rsum_ready"], 1)
                v.wait_ge(sm["rsum_ready"], t + 1)
                wait(v, sm["o2T_mm"], t)
                V.tensor_tensor(o2[:, :].rearrange("p (h e) -> p h e", e=DH), nd[:, :, 0:DH],
                                spread(rsum[:, :].rearrange("p (h o) -> p h o", o=1), 2, DH), ALU.mult).then_inc(sm["o2_ready"], 1)

            def residual2(t):
                v.wait_ge(sm["xo_mm"], t + 1)
                V.tensor_tensor(xt(t), ps[:, A3, 0:D], xt(t), ALU.add).then_inc(sm["x2_ready"], 1)

            def ln3_stats(t):
                v.wait_ge(sm["x2_ready"], t + 1)
                alone(v, sm["dve_passed"])
                V.bn_stats(st3[:, :], xt(t)).then_inc(sm["ln3_st"], 1)
                v.wait_ge(sm["ln3_st"], t + 1)
                wait(v, sm["ln3_ve"], t)
                wait(v, sm["mean_kept"], t)
                alone(v, sm["dve_passed"])
                V.bn_aggr(mv3[:, :], st3[:, :]).then_inc(sm["ln3_mv"], 1)

            def keep_mean3(t):
                v.wait_ge(sm["ln3_mv"], t + 1)
                V.tensor_copy(mean3[:, bass.ds(t, 1)], mv3[:, 0:1]).then_inc(sm["mean_kept"], 1)

            def body(t, q):
                if has(t, 0):
                    block_diagonal(t)
                if has(t, -1):
                    k_block(t - 1)
                if has(t, 0):
                    divide(t)
                if has(t, -1):
                    v_block(t - 1, 1 - q)
                if has(t, -3):
                    residual2(t - 3)
                    ln3_stats(t - 3)
                if has(t, 0):
                    residual1(t)
                    ln2_stats(t)
                if has(t, -3):
                    keep_mean3(t - 3)
                if has(t, 1):
                    k_v_bias(t + 1)
                if has(t, 0):
                    ln2_norm(t)
                if has(t, 1):
                    k_feature(t + 1)
                    q_feature(t + 1)
                if has(t, -2):
                    scale_values(t - 2)
                if has(t, 2):
                    ln1_stats(t + 2)
                if has(t, -1):
                    score_max(t - 1)
                if has(t, 2):
                    ln1_norm(t + 2)

            v.wait_ge(sm["x_first"], 16)
            ln1_stats(0)
            ln1_norm(0)
            v.wait_ge(sm["w_self"], 16 * W_SELF)
            V.tensor_scalar(bkv[:, 0:D], bkv[:, 0:D], 1.0, None, ALU.add).then_inc(sm["consts_v"], 1)
            V.tensor_scalar(bq1[:, :], bq1[:, :], 1.0, None, ALU.add).then_inc(sm["consts_v"], 1)
            v.wait_ge(sm["const_in"], 16 * W_CONST)
            v.wait_ge(sm["w_cross"], 16 * W_CROSS)
            V.tensor_copy(xwk_rep[:, :, :, :, :].rearrange("p k g h d -> p (k g) h d"),
                          spread(xwk[:, :, :].rearrange("p k (g o d) -> p (k g) o d", g=GROUPS, o=1), 2, HEADS // GROUPS)
                          ).then_inc(sm["consts_v"], 1)
            for h in range(2):
                V.tensor_copy(v_bd[:, :, :, h, DH:DH + 1].rearrange("p q g o -> p (q g) o"),
                              spread(row_half[:, h:h + 1].rearrange("p (g o) -> p g o", o=1), 1, 2 * SEQS * GROUPS)
                              ).then_inc(sm["consts_v"], 1)
            V.tensor_scalar(key_off[:, :, :], mask_u8[:, :, :], -1.0, BIG, ALU.add, ALU.mult).then_inc(sm["consts_v"], 1)
            v.wait_ge(sm["consts_v"], 8)
            v.wait_ge(sm["x_rest"], 16)
            attention_iterations(v, body, TILES + 3)

            V.tensor_copy(before_b[:, :], before[:, :]).then_inc(sm["consts_v"], 1)
            V.memset(ones_b[:, :], 1.0).then_inc(sm["consts_v"], 1)
            V.memset(ones8[:, :], 1.0).then_inc(sm["consts_v"], 1)
            v.wait_ge(sm["consts_v"], 11)
            v.wait_ge(sm["x2_ready"], TILES)

            def ln3_norm(t, p):
                wait(v, sm["xT_mm"], t - 1)
                wait(v, sm["kept"], t - 1)
                V.tensor_scalar(xn3[:, p, :], xt(t), mean3[:, bass.ds(t, 1)],
                                rs3[:, bass.ds(t, 1)], ALU.subtract, ALU.mult).then_inc(sm["ln3_done"], 1)

            def x_low(t, p):
                v.wait_ge(sm["xh_ready"], t + 1)
                V.tensor_tensor(xl[:, p, :, :].rearrange("p c t -> p (c t)"), ps[:, (TX, HT)[p], 0:D],
                                xh[:, p, :, :].rearrange("p c t -> p (c t)").bitcast(F32), ALU.subtract).then_inc(sm["xl_ready"], 1)

            v.wait_ge(sm["ln3_rs"], TILES)
            ln3_norm(0, 0)
            ln3_norm(1, 1)
            x_low(0, 0)
            with v.Fori(1, TILES // 2) as pair:
                t = 2 * pair
                ln3_norm(t, 0)
                x_low(t - 1, 1)
                ln3_norm(t + 1, 1)
                x_low(t, 0)
            x_low(TILES - 1, 1)

            def shared_x_low(t, p):
                v.wait_ge(sm["s_xh_ready"], t + 1)
                V.tensor_tensor(xl[:, p, :, :].rearrange("p c t -> p (c t)"), ps[:, TX, 0:D],
                                xh[:, p, :, :].rearrange("p c t -> p (c t)").bitcast(F32), ALU.subtract).then_inc(sm["s_xl_ready"], 1)

            step = [0]

            def chained(ins):
                step[0] += 1
                ins.then_inc(sm["routing"], 1)
                v.wait_ge(sm["routing"], step[0])

            def by_expert(ap):
                return spread(ap.rearrange("p (t o) -> p t o", o=1), 2, NE)

            def by_tile(ap):
                return spread(ap.rearrange("p (o e) -> p o e", o=1), 1, TILES)

            v.wait_ge(sm["route_mm"], TILES)
            shared_x_low(0, 0)
            V.tensor_copy(lg[:, :, :], ps[:, LG, 0:TILES * ROUTE].rearrange("p (t e) -> p t e", e=ROUTE)[:, :, 0:NE + 1]
                          ).then_inc(sm["lg_ready"], 1)
            v.wait_ge(sm["lg_ready"], 1)
            chained(V.tensor_reduce(nmx[:, :], lg[:, :, 0:NE], AX.X, ALU.max))
            V.tensor_tensor(lgs[:, :, :], lg[:, :, 0:NE], by_expert(nmx[:, :]), ALU.subtract).then_inc(sm["lgs_ready"], 1)
            v.wait_ge(sm["sgt_ready"], 1)
            V.tensor_scalar(sg4[:, :], sgt[:, :], 1.0, 0.25, ALU.add, ALU.mult).then_inc(sm["sg4_ready"], 1)
            v.wait_ge(sm["pe8_ready"], 1)
            chained(V.tensor_reduce(psum8[:, :], pe8[:, :, :], AX.X, ALU.add))
            chained(V.reciprocal(prec8[:, :], psum8[:, :]))
            chained(V.tensor_tensor(prob[:, :, :], pe8[:, :, :], by_expert(prec8[:, :]), ALU.mult))
            for r, pr_r in enumerate((prob, prob2)):
                chained(V.tensor_reduce(top[:, r, :], pr_r[:, :, :], AX.X, ALU.max))
                chained(V.tensor_tensor(is_top[:, :, :], pr_r[:, :, :], by_expert(top[:, r, :]), ALU.is_equal))
                chained(V.tensor_tensor(is_top[:, :, :], is_top[:, :, :], by_tile(rev8[:, :]), ALU.mult))
                chained(V.tensor_reduce(top_e[:, :], is_top[:, :, :], AX.X, ALU.max))
                chained(V.tensor_tensor(hot[:, r, :, :], by_expert(top_e[:, :]), by_tile(rev8[:, :]), ALU.is_equal))
                if r == 0:
                    chained(V.scalar_tensor_tensor(out=prob2[:, :, :], in0=hot[:, 0, :, :], scalar=-2.0, in1=prob[:, :, :],
                                                   op0=ALU.mult, op1=ALU.add))
            V.tensor_copy(hot_b[:, :, :], hot[:, :, :, :].rearrange("p r t e -> p r (t e)")).then_inc(sm["hotb_ready"], 1)
            chained(V.tensor_tensor(tsum[:, :], top[:, 0, :], top[:, 1, :], ALU.add))
            chained(V.reciprocal(trec[:, :], tsum[:, :]))
            chained(V.tensor_tensor(w_choice[:, :, :], top[:, :, :], spread(trec[:, :].rearrange("p (o t) -> p o t", o=1), 1, 2),
                                    ALU.mult))
            v.wait_ge(sm["rank_mm"], 1)
            chained(V.tensor_copy(in_tile[:, :, :], ps[:, LG, NE * TILES:2 * NE * TILES].rearrange("p (t e) -> p e t", e=NE)))
            chained(V.tensor_tensor_scan(upto[:, :, :].rearrange("p e t -> p (e t)"), not_first[:, :, :].rearrange("p e t -> p (e t)"),
                                         in_tile[:, :, :].rearrange("p e t -> p (e t)"), 0.0, ALU.mult, ALU.add))
            chained(V.tensor_scalar(cnt_i[:, :], upto[:, :, TILES - 1:TILES].rearrange("p e o -> p (e o)"), float(P - 1), None, ALU.add))
            chained(V.tensor_scalar(til_i[:, :], cnt_i[:, :], 7, None, ALU.logical_shift_right))
            chained(V.tensor_copy(til[:, :], til_i[:, :]))
            chained(V.tensor_tensor_scan(cum[:, :], ones8[:, :], til[:, :], 0.0, ALU.mult, ALU.add))
            chained(V.tensor_tensor(first[:, :], cum[:, :], til[:, :], ALU.subtract))
            chained(V.tensor_tensor(upto[:, :, :], upto[:, :, :], in_tile[:, :, :], ALU.subtract))
            chained(V.scalar_tensor_tensor(out=rowf[:, :, :], in0=by_tile(first[:, :]), scalar=float(P),
                                           in1=upto[:, :, :].rearrange("p e t -> p t e"), op0=ALU.mult, op1=ALU.add))
            chained(V.tensor_tensor(rowf[:, :, :], rowf[:, :, :], ps[:, LG, 0:NE * TILES].rearrange("p (t e) -> p t e", e=NE), ALU.add))
            for r in range(2):
                chained(V.tensor_tensor(row_x[:, r, :, :], hot[:, r, :, :], rowf[:, :, :], ALU.mult))
            chained(V.tensor_reduce(posf[:, :, :], row_x[:, :, :, :], AX.X, ALU.add))
            V.tensor_copy(pos[:, :, :], posf[:, :, :]).then_inc(sm["pos_ready"], 1)

            def slot_table():
                slots_x = spread(iota_slot[:, :].rearrange("p (i o) -> p i o", o=1), 2, NE)
                chained(V.tensor_tensor(ge[:, :, :], slots_x, spread(cum[0:1, :].rearrange("p (o e) -> p o e", o=1), 1, SLOT_TILES),
                                        ALU.is_ge))
                chained(V.tensor_reduce(slot_e[:, :], ge[:, :, :], AX.X, ALU.add))
                V.tensor_scalar(slot_ei[:, :], slot_e[:, :], float(NE - 1), None, ALU.min).then_inc(sm["slots_ready"], 1)

            def shared_h(t, p):
                v.wait_ge(sm["s_th_ready"], t + 1)
                V.scalar_tensor_tensor(out=s_gg[:, :], in0=s_th[:, :], scalar=1.0, in1=ps[:, GT + p, 0:HS],
                                       op0=ALU.add, op1=ALU.mult).then_inc(sm["s_gg_ready"], 1)
                v.wait_ge(sm["s_gg_ready"], t + 1)
                v.wait_ge(sm["s_up_mm"], t + 1)
                wait(v, sm["hT_mm"], t - 1)
                V.scalar_tensor_tensor(out=s_h[:, p, :], in0=s_gg[:, :], scalar=sg4[:, bass.ds(t, 1)], in1=ps[:, UP + p, 0:HS],
                                       op0=ALU.mult, op1=ALU.mult).then_inc(sm["s_h_ready"], 1)

            def sh_low(t, p):
                v.wait_ge(sm["s_hh_ready"], t + 1)
                V.tensor_tensor(s_hl[:, p, 0:2, :].rearrange("p c t -> p (c t)"), ps[:, HT, 0:2 * P],
                                s_hh[:, p, 0:2, :].rearrange("p c t -> p (c t)").bitcast(F32), ALU.subtract)
                V.tensor_tensor(s_hl[0:HS_LAST, p, 2, :], ps[0:HS_LAST, HT, 2 * P:3 * P],
                                s_hh[0:HS_LAST, p, 2, :].bitcast(F32), ALU.subtract).then_inc(sm["s_hl_ready"], 1)

            def residual3(t):
                v.wait_ge(sm["s_down_mm"], t + 1)
                V.tensor_tensor(xt(t), ps[:, DN, 0:D], xt(t), ALU.add).then_inc(sm["x3_ready"], 1)

            def shared(t, p, prev, prev2, nxt):
                shared_h(t, p)
                if nxt:
                    shared_x_low(t + 1, 1 - p)
                if prev:
                    sh_low(t - 1, 1 - p)
                if prev2:
                    residual3(t - 2)

            v.wait_ge(sm["sg4_ready"], 1)
            shared(0, 0, False, False, True)
            slot_table()
            shared(1, 1, True, False, True)
            with v.Fori(1, TILES // 2 - 1) as pair:
                t = 2 * pair
                shared(t, 0, True, True, True)
                shared(t + 1, 1, True, True, True)
            shared(TILES - 2, 0, True, True, True)
            shared(TILES - 1, 1, True, True, False)
            residual3(TILES - 2)
            sh_low(TILES - 1, 1)
            residual3(TILES - 1)

            def slots_low(i, p):
                v.wait_ge(sm["e_xh_ready"], i + 1)
                V.tensor_tensor(xl[:, p, :, :].rearrange("p c t -> p (c t)"), ps[:, EX + p, 0:D],
                                xh[:, p, :, :].rearrange("p c t -> p (c t)").bitcast(F32), ALU.subtract).then_inc(sm["e_xl_ready"], 1)

            def expert_h(i, p):
                v.wait_ge(sm["e_th_ready"], i + 1)
                V.scalar_tensor_tensor(out=e_gg[:, p, :], in0=e_th[:, p, :], scalar=1.0, in1=ps[:, EG + p, 0:H],
                                       op0=ALU.add, op1=ALU.mult).then_inc(sm["e_gg_ready"], 1)
                v.wait_ge(sm["e_gg_ready"], i + 1)
                wait(v, sm["e_hT_mm"], i - 1)
                V.scalar_tensor_tensor(out=e_h[:, p, :], in0=e_gg[:, p, :], scalar=0.5, in1=ps[:, EG + p, H:2 * H],
                                       op0=ALU.mult, op1=ALU.mult).then_inc(sm["e_h_ready"], 1)

            def h_low(i, p):
                v.wait_ge(sm["e_hh_ready"], i + 1)
                V.tensor_tensor(e_hl[:, p, :, :].rearrange("p c t -> p (c t)"), ps[0:HC, EH + p, 0:2 * P],
                                e_hh[:, p, :, :].rearrange("p c t -> p (c t)").bitcast(F32), ALU.subtract).then_inc(sm["e_hl_ready"], 1)

            def experts(i, p, prev, nxt2):
                expert_h(i, p)
                if prev:
                    h_low(i - 1, 1 - p)
                if nxt2:
                    slots_low(i + 2, p)

            slots_low(0, 0)
            slots_low(1, 1)
            experts(0, 0, False, True)
            experts(1, 1, True, True)
            with v.Fori(1, SLOT_TILES // 2 - 1) as pair:
                i = 2 * pair
                experts(i, 0, True, True)
                experts(i + 1, 1, True, True)
            experts(SLOT_TILES - 2, 0, True, False)
            experts(SLOT_TILES - 1, 1, True, False)
            h_low(SLOT_TILES - 1, 1)

            def combine(t, p):
                v.wait_ge(sm[f"gathered{p}"], 16 * (t - p) + 32)
                V.scalar_tensor_tensor(out=y1[:, p, :], in0=yg[:, p, 0, :], scalar=w_choice[:, 0, bass.ds(t, 1)], in1=xt(t),
                                       op0=ALU.mult, op1=ALU.add).then_inc(sm["y1_ready"], 1)
                v.wait_ge(sm["y1_ready"], t + 1)
                wait(v, sm[f"stored{p}"], 8 * (t - p))
                V.scalar_tensor_tensor(out=y2[:, p, :], in0=yg[:, p, 1, :], scalar=w_choice[:, 1, bass.ds(t, 1)], in1=y1[:, p, :],
                                       op0=ALU.mult, op1=ALU.add).then_inc(sm["y_ready"], 1)

            combine(0, 0)
            combine(1, 1)
            with v.Fori(1, TILES // 2) as pair:
                t = 2 * pair
                combine(t, 0)
                combine(t + 1, 1)


def kernel(**inputs):
    import concourse.bacc as _bacc
    from concourse import mybir as _mybir
    from concourse.bass_utils import run_bass_kernel_spmd as _run

    i = {k: np.asarray(v) for k, v in inputs.items()}

    def chunks(w, c=KC):
        return np.ascontiguousarray(w.reshape(c, w.shape[0] // c, w.shape[1]).transpose(1, 0, 2))

    def experts(w, c):
        return np.ascontiguousarray(w.reshape(NE, c, w.shape[1] // c, w.shape[2]).transpose(2, 0, 1, 3))

    pos = np.arange(P)
    slopes = (2.0 ** (-8.0 / HEADS * np.arange(1, HEADS + 1))).astype(np.float32)
    order = [c * 8 + j * 2 + h for j in range(4) for c in range(2) for h in range(2)]
    rel = (np.arange(S)[None, :] - (pos % S)[:, None]).astype(np.float32)
    alibi = slopes[order][None, :, None] * rel[:, None, :]
    w_ffn = np.zeros((P, W_ALL), np.float32)
    w_ffn[:, W_GU:W_DOWN] = experts(np.concatenate([i["L0_ffn_w_gate"], i["L0_ffn_w_up"]], 2), KC).reshape(P, -1)
    w_ffn[:HC, W_DOWN:W_ROUTE] = experts(i["L0_ffn_w_down"], 2).reshape(HC, -1)
    pad = np.zeros((D, 1), np.float32)
    w_ffn[:, W_ROUTE:W_SHGATE] = chunks(np.concatenate(
        [i["L0_ffn_gate_w"].T, i["L0_ffn_shgate_w"][:, None], pad], 1)).reshape(P, -1)
    w_ffn[:, W_SHGATE:W_SHUP] = chunks(i["L0_ffn_shw_gate"]).reshape(P, -1)
    w_ffn[:, W_SHUP:W_SHDOWN] = chunks(i["L0_ffn_shw_up"]).reshape(P, -1)
    w_ffn[:, W_SHDOWN:W_SHDOWN + 2 * D] = chunks(i["L0_ffn_shw_down"][:2 * P]).reshape(P, -1)
    w_ffn[:HS_LAST, W_SHDOWN + 2 * D:W_END] = i["L0_ffn_shw_down"][2 * P:]
    arrays = {
        "x": i["x"], "ctx": i["ctx_2048"], "mask": i["mask_BxS2_bf1"].view(np.uint8),
        "ident": np.eye(P, dtype=np.float32),
        "own_head": (pos[:, None] // DH == np.arange(HALF)[None, :]).astype(np.float32),
        "block_mask": (pos[:, None] // DH == pos[None, :] // DH).astype(np.float32),
        "row_head": ((pos[:, None] % 32) // DH == np.arange(2)[None, :]).astype(np.float32),
        "row_half": (pos[:, None] // S == np.arange(2)[None, :]).astype(np.float32),
        "alibi": np.ascontiguousarray(alibi.reshape(P, HEADS * S)),
        "rev8": np.tile(NE - np.arange(NE, dtype=np.float32), (P, 1)),
        "not_first": np.tile((np.arange(NE * TILES) % TILES > 0).astype(np.float32), (P, 1)),
        "iota_slot": np.arange(SLOT_TILES, dtype=np.float32)[None],
        "before": (pos[:, None] < pos[None, :]).astype(np.float32),
        "wq": chunks(i["L0_attn_wq"].T), "wkv": chunks(np.concatenate([i["L0_attn_wk"].T, i["L0_attn_wv"].T], 1)),
        "wo": chunks(i["L0_attn_wo"].T),
        "bq": np.ascontiguousarray(i["L0_attn_bq"].reshape(KC, P).T),
        "bkv": np.concatenate([i["L0_attn_bk"], i["L0_attn_bv"]]), "bo": i["L0_attn_bo"],
        "xwq": chunks(i["L0_xattn_Wq"]), "xwk": chunks(i["L0_xattn_Wk"]), "xwv": chunks(i["L0_xattn_Wv"]),
        "xwo": chunks(i["L0_xattn_Wo"]),
        "w_ffn": w_ffn,
    }
    nc = _bacc.Bacc("TRN2", target_bir_lowering=False, num_devices=1)
    args, feeds = {}, {}
    for name, arr in arrays.items():
        feeds[f"in_{name}_dram"] = arr
        args[name] = nc.dram_tensor(f"in_{name}_dram", arr.shape, _mybir.dt.from_np(arr.dtype), kind="ExternalInput").ap()
    out = nc.dram_tensor("out_0_dram", (B, S, D), F32, kind="ExternalOutput").ap()
    build(nc, args, out)
    r = _run(nc, [feeds], core_ids=[0])
    return r.results[0]["out_0_dram"]
```

```python
from contextlib import ExitStack

import numpy as np

import concourse.bass as bass
from concourse import mybir

F32 = mybir.dt.float32
U32 = mybir.dt.uint32
I32 = mybir.dt.int32
U8 = mybir.dt.uint8
BF16 = mybir.dt.bfloat16
F32R = mybir.dt.float32r
ALU = mybir.AluOpType
ACT = mybir.ActivationFunctionType
AX = mybir.AxisListType

P = 128
B, S, D = 32, 64, 256
TILES = B * S // P
KC = D // P
HEADS, DH = 16, 16
GROUPS = 4
SEQS = P // S
HALF = HEADS // 2
NE, H = 8, 176
HC = H // 2
HS = 352
HS_LAST = HS - 2 * P
ROUTE = NE + 1

SLOT_TILES = 2 * TILES + NE
SPARE = SLOT_TILES * P

W_GU = 0
W_DOWN = W_GU + NE * KC * 2 * H
W_SHGATE = W_DOWN + NE * 2 * D
W_SHUP = W_SHGATE + KC * HS
W_SHDOWN = W_SHUP + KC * HS
W_END = W_SHDOWN + 3 * D
FIRST_SPLIT = 2
W_PARTS = 12
WARM_UP = 10
ZERO_TILES = SLOT_TILES // (W_PARTS // 2 - 1)
W_PART = -(-W_END // (2 * W_PARTS)) * 2
W_ALL = W_PART * W_PARTS
STEADY = range(6, TILES - 2)
LN_EPS = 1e-5
DEN_EPS = 1e-8
BIG = float(np.finfo(np.float32).max)


def wait(eng, sem, count):
    if isinstance(count, int) and count <= 0:
        return
    eng.wait_ge(sem, count)


def has(t, ahead):
    return not isinstance(t, int) or 0 <= t + ahead < TILES


def splits(t):
    return not isinstance(t, int) or 0 <= t - FIRST_SPLIT < W_PARTS


def attention_iterations(eng, body, last, before_0, before_1):
    for t in range(-1, STEADY.start):
        if t == 0:
            before_0()
        if t == 1:
            before_1()
        body(t, t % 2)
    with eng.Fori(0, len(STEADY) // 2) as pair:
        t = STEADY.start + 2 * pair
        body(t, 0)
        body(t + 1, 1)
    for t in range(STEADY.stop, last):
        body(t, t % 2)


def spread(ap, axis, n):
    shape = list(ap.shape)
    shape[axis] = n
    return ap.broadcast_to(shape)


def build(nc, a, out):
    with ExitStack() as ctx:
        def sb(name, shape, dt=F32):
            return ctx.enter_context(nc.sbuf_tensor(name, shape, dt))

        def sem(name):
            return ctx.enter_context(nc.semaphore(name))

        ident = sb("ident", [P, P])
        neg_half = sb("neg_half", [P, 1])
        eps = sb("eps", [P, 1])
        early = sb("early", [P, 1])
        minus_one = sb("minus_one", [P, 1])
        out_rows = sb("out_rows", [P, TILES, 2])
        spare_rows = sb("spare_rows", [P, SLOT_TILES])
        rev8 = sb("rev8", [P, NE])
        not_first = sb("not_first", [P, NE, TILES])
        iota_slot = sb("iota_slot", [1, SLOT_TILES])
        ones8 = sb("ones8", [P, NE])
        before = sb("before", [P, P])
        before_b = sb("before_b", [P, P], BF16)
        ones_b = sb("ones_b", [P, P], BF16)
        zeros = sb("zeros", [P, D + 1])
        w_hi = sb("w_hi", [P, W_ALL], F32R)
        w_lo = sb("w_lo", [P, W_ALL], F32R)

        x_all = sb("x_all", [P, TILES, D])
        st3 = sb("st3", [P, 6])
        mv3 = sb("mv3", [P, 2])
        neg_mean3 = sb("neg_mean3", [P, 1])
        ve3 = sb("ve3", [P, 1])
        rs3 = sb("rs3", [P, TILES])
        nb3 = sb("nb3", [P, TILES])
        xn3 = sb("xn3", [P, 2, D])
        lg = sb("lg", [P, TILES, NE + 1])
        nmx = sb("nmx", [P, TILES])
        lgs = sb("lgs", [P, TILES, NE])
        pe8 = sb("pe8", [P, TILES, NE])
        psum8 = sb("psum8", [P, TILES])
        prec8 = sb("prec8", [P, TILES])
        prob = sb("prob", [P, TILES, NE])
        prob2 = sb("prob2", [P, TILES, NE])
        is_top = sb("is_top", [P, TILES, NE])
        top = sb("top", [P, 2, TILES])
        top_e = sb("top_e", [P, TILES])
        tsum = sb("tsum", [P, TILES])
        trec = sb("trec", [P, TILES])
        w_choice = sb("w_choice", [P, 2, TILES])
        hot = sb("hot", [P, 2, TILES, NE])
        hot_b = sb("hot_b", [P, 2, TILES * NE], BF16)
        in_tile = sb("in_tile", [P, NE, TILES])
        upto = sb("upto", [P, NE, TILES])
        rowf = sb("rowf", [P, TILES, NE])
        row_x = sb("row_x", [P, 2, TILES, NE])
        posf = sb("posf", [P, 2, TILES])
        pos = sb("pos", [P, TILES, 2], U32)
        cnt_i = sb("cnt_i", [P, NE], I32)
        til_i = sb("til_i", [P, NE], I32)
        til = sb("til", [P, NE])
        cum = sb("cum", [P, NE])
        first = sb("first", [P, NE])
        ge = sb("ge", [1, SLOT_TILES, NE])
        slot_e = sb("slot_e", [1, SLOT_TILES])
        slot_ei = sb("slot_ei", [1, SLOT_TILES], I32)
        sgt = sb("sgt", [P, TILES])
        sg4 = sb("sg4", [P, TILES])
        with ExitStack() as attention:
            def sb_attn(name, shape, dt=F32):
                return attention.enter_context(nc.sbuf_tensor(name, shape, dt))
            wq = sb_attn("wq", [P, KC, D])
            wkv = sb_attn("wkv", [P, KC, 2 * D])
            wo = sb_attn("wo", [P, KC, D])
            bq1 = sb_attn("bq1", [P, KC])
            bkv = sb_attn("bkv", [P, 2 * D])
            bo = sb_attn("bo", [P, D])
            xwq = sb_attn("xwq", [P, KC, D])
            xwk = sb_attn("xwk", [P, KC, GROUPS * DH])
            xwk_rep = sb_attn("xwk_rep", [P, KC, GROUPS, HEADS // GROUPS, DH])
            xwv = sb_attn("xwv", [P, KC, GROUPS * DH])
            xwo = sb_attn("xwo", [P, KC, D])
            own_head = sb_attn("own_head", [P, HALF])
            block_mask = sb_attn("block_mask", [P, P])
            row_head = sb_attn("row_head", [P, 2])
            row_half = sb_attn("row_half", [P, 2])
            mask_u8 = sb_attn("mask_u8", [P, TILES, S], U8)
            st1 = sb_attn("st1", [P, 6])
            mv1 = sb_attn("mv1", [P, 2])
            rs1 = sb_attn("rs1", [P, 1])
            xn1 = sb_attn("xn1", [P, D])
            xn1T = sb_attn("xn1T", [P, KC, P])
            k1 = sb_attn("k1", [P, D])
            ke = sb_attn("ke", [P, D])
            kf = sb_attn("kf", [P, D])
            vo = sb_attn("vo", [P, HALF, 33])
            q1 = sb_attn("q1", [P, KC, P])
            qe = sb_attn("qe", [P, KC, P])
            qf = sb_attn("qf", [P, KC, P])
            kv_bd = sb_attn("kv_bd", [P, SEQS, 2, P + HALF])
            den = sb_attn("den", [P, 2, HALF])
            rden = sb_attn("rden", [P, 2, HALF])
            o = sb_attn("o", [P, D])
            oT = sb_attn("oT", [P, KC, P])
            ctx_sb = sb_attn("ctx_sb", [P, D])
            st2 = sb_attn("st2", [P, 6])
            mv2 = sb_attn("mv2", [P, 2])
            rs2 = sb_attn("rs2", [P, 1])
            xn2 = sb_attn("xn2", [P, D])
            xcT = sb_attn("xcT", [P, 2 * KC, P])
            q2T = sb_attn("q2T", [P, KC, P])
            k_bd = sb_attn("k_bd", [P, 2, 2, P])
            v_bd = sb_attn("v_bd", [P, 2, SEQS * GROUPS, 2, DH + 1])
            smax = sb_attn("smax", [P, HEADS])
            rsum = sb_attn("rsum", [P, HEADS])
            o2 = sb_attn("o2", [P, D])
            o2T = sb_attn("o2T", [P, KC, P])
            w_route = sb_attn("w_route", [P, KC, ROUTE])
            xn3T = sb_attn("xn3T", [P, KC, P])
            alibi = sb_attn("alibi", [P, HEADS * S])
            key_off = sb_attn("key_off", [P, TILES, S])
            bias_t = sb_attn("bias_t", [P, HEADS * S])
            sc = sb_attn("sc", [P, HEADS * S])
            pr = sb_attn("pr", [P, HEADS * S])
            prT = sb_attn("prT", [P, 8, P])
            w_stage = sb_attn("w_stage", [P, 2, W_PART])
        x_send = sb("x_send", [P, TILES, 2, D + 1])
        xh = sb("xh", [P, 2, KC, P], F32R)
        xl = sb("xl", [P, 2, KC, P], F32R)
        s_th = sb("s_th", [P, HS])
        s_gg = sb("s_gg", [P, HS])
        s_h = sb("s_h", [P, 2, HS])
        s_hh = sb("s_hh", [P, 2, 3, P], F32R)
        s_hl = sb("s_hl", [P, 2, 3, P], F32R)
        xs = sb("xs", [P, 4, D + 1])
        out_row = sb("out_row", [P, 4], U32)
        e_th = sb("e_th", [P, 2, H])
        e_gg = sb("e_gg", [P, 2, H])
        e_h = sb("e_h", [P, 2, H])
        e_hh = sb("e_hh", [HC, 2, 2, P], F32R)
        e_hl = sb("e_hl", [HC, 2, 2, P], F32R)
        e_y = sb("e_y", [P, 4, D])
        yg = sb("yg", [P, 4, 2, D])
        y1 = sb("y1", [P, 2, D])
        y2 = sb("y2", [P, 4, D])

        xs_d = nc.dram_tensor("xs_rows", (SLOT_TILES * P, D + 1), F32).ap()
        y_d = nc.dram_tensor("y_rows", (SPARE + 2 * B * S, D), F32).ap()

        ps = ctx.enter_context(nc.psum_tensor("ps", [P, 8, 512], F32))
        A0, A1, A2, A3, B0, B1, B2, B3 = range(8)
        TX, GT, UP, HT, DN, LG = 0, 1, 3, 5, 6, 7
        EX, EG, EH, ED = 0, 2, 4, 6

        names = """x_first x_rest w_self w_cross const_in ident_in heads_in mask_in ctx_in w_out consts_v consts_p early_exp
            ln1_st ln1_mv ln1_ve ln1_rs ln1_done xn1T_mm xn1T_ready kv_mm q_mm k1_ready ke_ready kf_ready
            v_ready q1_ready qe_ready qf_ready kvs_mm kvs_ready numden_mm den_ready rden_ready o_ready oT_mm oT_ready
            attn_mm xbo_ready x1_ready
            ln2_st ln2_mv ln2_ve ln2_rs ln2_done xcT_mm xcT_ready ckv_mm q2_mm kbd_ready vbd_ready q2T_ready
            scores_mm bias_ready sc_ready smax_ready sub_ready exp_ready rsum_ready o2_ready o2T_mm
            prT_mm prT_ready pv_mm o2T_ready xo_mm x2_ready
            w_part0 w_part1 w_hi_ready w_lo_ready zeros_ready zeroed
            ln3_st ln3_mv neg_mean_ready ln3_ve ln3_rs ln3_nb ln3_done xT_mm xn3T_ready route_mm logits_ready
            routing lgs_ready pe8_ready sgt_ready sg4_ready hotb_ready rank_mm pos_ready slots_ready sent
            s_x_ready rows_ready s_xT_mm s_xh_ready s_xl_ready s_gate_mm s_up_mm
            s_th_ready s_gg_ready s_h_ready hT_mm s_hh_ready s_hl_ready s_down_mm x3_ready
            xs_in0 xs_in1 xs_in2 xs_in3
            e_xT_mm e_xh_ready e_xl_ready gu_mm e_th_ready e_gg_ready e_h_ready e_hT_mm e_hh_ready e_hl_ready
            e_down_mm e_y_ready ys_out0 ys_out1 ys_out2 ys_out3 out_rows_ready out_row_ready y_in0 y_in1 y_in2 y_in3 y1_ready y_ready
            stored0 stored1 stored2 stored3
            dve_passed act_passed pe_passed pool_passed"""
        sm = {n: sem(n) for n in names.split()}

        x_d = a["x"].rearrange("b s d -> (b s) d").rearrange("(t p) d -> p t d", p=P)
        ctx_d = a["ctx"].rearrange("b s d -> (b s) d")
        out_d = out.rearrange("b s d -> (b s) d")

        def bcast(vec, n):
            return bass.AP(vec.tensor, vec.offset, [[0, P], [1, n]])

        W_SELF, W_OUT, W_CROSS, W_MASK, W_CONST = 4, 2, 4, 3 + SEQS, 7


        def alone(eng, passed):
            eng.sem_inc(passed, 1)

        block = ctx.enter_context(nc.Block())

        @block.sync
        def _(sp):
            sp.dma_start(x_all[:, 0:2, :], x_d[:, 0:2, :]).then_inc(sm["x_first"], 16)
            sp.dma_start(ident[:, :], a["ident"]).then_inc(sm["ident_in"], 16)
            sp.dma_start(wkv[:, :, :], a["wkv"]).then_inc(sm["w_self"], 16)
            sp.dma_start(bkv[:, :], bcast(a["bkv"], 2 * D)).then_inc(sm["w_self"], 16)
            sp.dma_start(wq[:, :, :], a["wq"]).then_inc(sm["w_self"], 16)
            sp.dma_start(bq1[:, :], a["bq"]).then_inc(sm["w_self"], 16)
            sp.dma_start(own_head[:, :], a["own_head"]).then_inc(sm["heads_in"], 16)
            sp.dma_start(block_mask[:, :], a["block_mask"]).then_inc(sm["heads_in"], 16)
            sp.dma_start(x_all[:, 2:TILES, :], x_d[:, 2:TILES, :]).then_inc(sm["x_rest"], 16)
            sp.dma_start(wo[:, :, :], a["wo"]).then_inc(sm["w_out"], 16)
            sp.dma_start(bo[:, :], bcast(a["bo"], D)).then_inc(sm["w_out"], 16)
            sp.dma_start(ctx_sb[:, :], ctx_d[0:P, :]).then_inc(sm["ctx_in"], 16)
            sp.dma_start(xwk[:, :, :], a["xwk"]).then_inc(sm["w_cross"], 16)
            sp.dma_start(xwv[:, :, :], a["xwv"]).then_inc(sm["w_cross"], 16)
            sp.dma_start(xwq[:, :, :], a["xwq"]).then_inc(sm["w_cross"], 16)
            sp.dma_start(xwo[:, :, :], a["xwo"]).then_inc(sm["w_cross"], 16)
            sp.dma_start(row_head[:, :], a["row_head"]).then_inc(sm["mask_in"], 16)
            sp.dma_start(row_half[:, :], a["row_half"]).then_inc(sm["mask_in"], 16)
            sp.dma_start(alibi[:, :], a["alibi"]).then_inc(sm["mask_in"], 16)
            for s in range(SEQS):
                src = bass.AP(a["mask"].tensor, a["mask"].offset + s * S, [[0, S], [SEQS * S, TILES], [1, S]])
                sp.dma_start(mask_u8[s * S:(s + 1) * S, :, :], src).then_inc(sm["mask_in"], 16)
            sp.dma_start(w_route[:, :, :], a["w_route"]).then_inc(sm["const_in"], 16)
            sp.dma_start(out_rows[:, :, :], a["out_rows"]).then_inc(sm["const_in"], 16)
            sp.dma_start(spare_rows[:, :], a["spare_rows"]).then_inc(sm["const_in"], 16)
            sp.dma_start(rev8[:, :], a["rev8"]).then_inc(sm["const_in"], 16)
            sp.dma_start(not_first[:, :, :].rearrange("p e t -> p (e t)"), a["not_first"]).then_inc(sm["const_in"], 16)
            sp.dma_start(iota_slot[:, :], a["iota_slot"]).then_inc(sm["const_in"], 16)
            sp.dma_start(before[:, :], a["before"]).then_inc(sm["const_in"], 16)
            sp.wait_ge(sm["zeros_ready"], 1)

            def next_ctx(t):
                sp.wait_ge(sm["xcT_mm"], t)
                sp.dma_start(ctx_sb[:, :], ctx_d[bass.ds(t * P, P), :]).then_inc(sm["ctx_in"], 16)

            def next_weights(c, half):
                wait(sp, sm["w_lo_ready"], c - 1)
                sp.dma_start(w_stage[:, half, :], a["w_ffn"][:, bass.ds(c * W_PART, W_PART)]).then_inc(sm[f"w_part{half}"], 16)

            def zero_rows(part):
                sp.dma_start(xs_d[bass.ds(part * (ZERO_TILES * P), ZERO_TILES * P), :].rearrange("(n p) d -> p n d", p=P),
                             spread(zeros[:, :].rearrange("p (o d) -> p o d", o=1), 1, ZERO_TILES)).then_inc(sm["zeroed"], 16)

            next_ctx(1)
            next_weights(0, 0)
            next_weights(1, 1)
            next_ctx(2)
            with sp.Fori(0, W_PARTS // 2 - 1) as pair:
                c = 2 + 2 * pair
                next_ctx(c + 1)
                next_weights(c, 0)
                next_ctx(c + 2)
                next_weights(c + 1, 1)
                zero_rows(pair)
            for t in range(W_PARTS + 1, TILES):
                next_ctx(t)

            def load_slots(i, q):
                wait(sp, sm["e_xT_mm"], i - 3)
                wait(sp, sm["out_row_ready"], i - 3)
                sp.dma_start(xs[:, q, :], xs_d[bass.ds(i * P, P), :]).then_inc(sm[f"xs_in{q}"], 16)

            sp.wait_ge(sm["sent"], 2 * 16 * TILES)
            for i in range(4):
                load_slots(i, i)
            with sp.Fori(1, SLOT_TILES // 4) as quad:
                i = 4 * quad
                for q in range(4):
                    load_slots(i + q, q)

            def load_y(t, q):
                wait(sp, sm["y_ready"], t - 3)
                sp.dma_start(yg[:, q, :, :], y_d[bass.ds(t * 2 * P + SPARE, 2 * P), :].rearrange("(p r) d -> p r d", r=2)
                             ).then_inc(sm[f"y_in{q}"], 16)

            for q in range(4):
                sp.wait_ge(sm[f"ys_out{q}"], 4 * SLOT_TILES)
            for t in range(4):
                load_y(t, t)
            with sp.Fori(1, TILES // 4) as quad:
                t = 4 * quad
                for q in range(4):
                    load_y(t + q, q)
            for q in range(4):
                sp.wait_ge(sm[f"stored{q}"], 4 * TILES)

        @block.gpsimd
        def _(pool):
            nc.gpsimd.memset(neg_half[:, :], -0.5).then_inc(sm["consts_p"], 1)
            nc.gpsimd.memset(eps[:, :], LN_EPS).then_inc(sm["consts_p"], 1)
            pool.wait_ge(sm["consts_p"], 2)

            def rstd(mv, ve, rs, mv_sem, ve_sem, rs_sem, n):
                pool.wait_ge(mv_sem, n)
                nc.gpsimd.tensor_tensor(ve, mv, eps[:, :], ALU.add).then_inc(ve_sem, 1)
                pool.wait_ge(ve_sem, n)
                nc.gpsimd.tensor_tensor(rs, ve, neg_half[:, :], ALU.pow).then_inc(rs_sem, 1)

            def rstd1(t):
                wait(pool, sm["ln1_done"], t)
                rstd(mv1[:, 1:2], st1[:, 0:1], rs1[:, :], sm["ln1_mv"], sm["ln1_ve"], sm["ln1_rs"], t + 1)

            def rstd2(t):
                wait(pool, sm["ln2_done"], t)
                rstd(mv2[:, 1:2], st2[:, 0:1], rs2[:, :], sm["ln2_mv"], sm["ln2_ve"], sm["ln2_rs"], t + 1)

            def rstd3(t):
                wait(pool, sm["ln3_rs"], t)
                rstd(mv3[:, 1:2], ve3[:, :], rs3[:, bass.ds(t, 1)], sm["ln3_mv"], sm["ln3_ve"], sm["ln3_rs"], t + 1)
                pool.wait_ge(sm["neg_mean_ready"], t + 1)
                pool.wait_ge(sm["ln3_rs"], t + 1)
                nc.gpsimd.tensor_tensor(nb3[:, bass.ds(t, 1)], neg_mean3[:, :], rs3[:, bass.ds(t, 1)], ALU.mult).then_inc(sm["ln3_nb"], 1)

            def add_bo(t):
                pool.wait_ge(sm["ln1_done"], t + 1)
                xt = x_all[:, bass.ds(t, 1), :].rearrange("p t d -> p (t d)")
                nc.gpsimd.tensor_tensor(xt, xt, bo[:, :], ALU.add).then_inc(sm["xbo_ready"], 1)

            def score_bias(t):
                wait(pool, sm["sc_ready"], t)
                ko = spread(key_off[:, bass.ds(t, 1), :], 1, HEADS)
                nc.gpsimd.tensor_tensor(bias_t[:, :].rearrange("p (h k) -> p h k", h=HEADS),
                                        alibi[:, :].rearrange("p (h k) -> p h k", h=HEADS), ko,
                                        ALU.add).then_inc(sm["bias_ready"], 1)

            def subtract_max(t):
                pool.wait_ge(sm["smax_ready"], t + 1)
                v = sc[:, :].rearrange("p (h k) -> p h k", h=HEADS)
                nc.gpsimd.tensor_tensor(v, v, spread(smax[:, :].rearrange("p (h o) -> p h o", o=1), 2, S),
                                        ALU.subtract).then_inc(sm["sub_ready"], 1)

            def split_low(c, half):
                pool.wait_ge(sm["w_hi_ready"], c + 1)
                cols = bass.ds(c * W_PART, W_PART)
                nc.gpsimd.tensor_tensor(w_lo[:, cols], w_stage[:, half, :], w_hi[:, cols].bitcast(F32),
                                        ALU.subtract).then_inc(sm["w_lo_ready"], 1)

            def body(t, q):
                if has(t, -2):
                    subtract_max(t - 2)
                if has(t, 0):
                    add_bo(t)
                if has(t, -1):
                    score_bias(t - 1)
                if has(t, -3):
                    rstd3(t - 3)
                if has(t, 0):
                    rstd2(t)
                if splits(t):
                    split_low(t - FIRST_SPLIT, q)
                if has(t, 2):
                    rstd1(t + 2)

            nc.gpsimd.memset(zeros[:, :], 0.0).then_inc(sm["zeros_ready"], 1)
            rstd1(0)

            def before_0():
                pool.wait_ge(sm["w_out"], 16 * W_OUT)

            def before_1():
                pool.wait_ge(sm["mask_in"], 16 * W_MASK)
                pool.wait_ge(sm["consts_v"], 8)

            attention_iterations(pool, body, TILES + 3, before_0, before_1)
            pool.wait_ge(sm["const_in"], 16 * W_CONST)

            pool.wait_ge(sm["zeroed"], 16 * (W_PARTS // 2 - 1))
            pool.wait_ge(sm["xT_mm"], TILES)
            nc.gpsimd.tensor_copy(x_send[:, :, :, D:D + 1].rearrange("p t r o -> p t (r o)"), out_rows[:, :, :]
                                  ).then_inc(sm["out_rows_ready"], 1)
            pool.wait_ge(sm["out_rows_ready"], 1)
            pool.wait_ge(sm["pos_ready"], 1)
            alone(pool, sm["pool_passed"])
            for t in range(TILES):
                pool.wait_ge(sm["rows_ready"], 2 * (t + 1))
                for r in range(2):
                    nc.gpsimd.indirect_dma_start(
                        out=xs_d[:, :], out_offset=bass.IndirectOffsetOnAxis(ap=pos[:, t, r:r + 1], axis=0),
                        in_=x_send[:, t, r, :], in_offset=None).then_inc(sm["sent"], 16)

            def scatter_out(i, q):
                pool.wait_ge(sm["out_row_ready"], i + 1)
                pool.wait_ge(sm["e_y_ready"], i + 1)
                alone(pool, sm["pool_passed"])
                nc.gpsimd.indirect_dma_start(
                    out=y_d[:, :], out_offset=bass.IndirectOffsetOnAxis(ap=out_row[:, q:q + 1], axis=0),
                    in_=e_y[:, q, :], in_offset=None).then_inc(sm[f"ys_out{q}"], 16)

            for i in range(4):
                scatter_out(i, i)
            with pool.Fori(1, SLOT_TILES // 4) as quad:
                i = 4 * quad
                for q in range(4):
                    scatter_out(i + q, q)

        @block.tensor
        def _(pe):
            T = nc.tensor

            def transpose_x(t):
                pe.wait_ge(sm["ln1_done"], t + 1)
                for k in range(KC):
                    mm = T.transpose(ps[:, A0, k * P:(k + 1) * P], xn1[:, k * P:(k + 1) * P], ident[:, :])
                mm.then_inc(sm["xn1T_mm"], 1)

            def project_kv(t):
                pe.wait_ge(sm["xn1T_ready"], t + 1)
                for k in range(KC):
                    mm = T.matmul(ps[:, A2, :], xn1T[:, k, :], wkv[:, k, :], start=(k == 0), stop=(k == KC - 1))
                mm.then_inc(sm["kv_mm"], 1)

            def project_q(t):
                for c in range(KC):
                    for k in range(KC):
                        mm = T.matmul(ps[:, A0, (KC + c) * P:(KC + c + 1) * P], wq[:, k, c * P:(c + 1) * P], xn1T[:, k, :],
                                      start=(k == 0), stop=(k == KC - 1))
                mm.then_inc(sm["q_mm"], 1)

            def key_value(t):
                pe.wait_ge(sm["kf_ready"], t + 1)
                pe.wait_ge(sm["v_ready"], t + 1)
                wait(pe, sm["x1_ready"], t)
                alone(pe, sm["pe_passed"])
                for s in range(SEQS):
                    rows = slice(s * S, (s + 1) * S)
                    for c in range(2):
                        for j in range(4):
                            g = c * 4 + j
                            mm = T.matmul(ps[32 * j:32 * j + 32, (A2, A1)[s], c * 33:c * 33 + 33],
                                          kf[rows, g * 32:g * 32 + 32], vo[rows, g, :], start=True, stop=True)
                mm.then_inc(sm["kvs_mm"], 1)

            def query_kv(t):
                pe.wait_ge(sm["kvs_ready"], t + 1)
                pe.wait_ge(sm["qf_ready"], t + 1)
                for c in range(2):
                    for s in range(SEQS):
                        mm = T.matmul(ps[s * S:(s + 1) * S, A1, c * (P + HALF):(c + 1) * (P + HALF)],
                                      qf[:, c, s * S:(s + 1) * S], kv_bd[:, s, c, :], start=True, stop=True)
                mm.then_inc(sm["numden_mm"], 1)

            def transpose_o(t):
                pe.wait_ge(sm["o_ready"], t + 1)
                for k in range(KC):
                    mm = T.transpose(ps[:, A1, k * P:(k + 1) * P], o[:, k * P:(k + 1) * P], ident[:, :])
                mm.then_inc(sm["oT_mm"], 1)

            def project_attn(t):
                pe.wait_ge(sm["oT_ready"], t + 1)
                for k in range(KC):
                    mm = T.matmul(ps[:, A1, 0:D], oT[:, k, :], wo[:, k, :], start=(k == 0), stop=(k == KC - 1))
                mm.then_inc(sm["attn_mm"], 1)

            def transpose_xc(t):
                pe.wait_ge(sm["ctx_in"], 16 * (t + 1))
                pe.wait_ge(sm["q1_ready"], 2 * (t + 2 if has(t, 1) else t + 1))
                for k in range(KC):
                    T.transpose(ps[:, A0, (KC + k) * P:(KC + k + 1) * P], ctx_sb[:, k * P:(k + 1) * P], ident[:, :])
                pe.wait_ge(sm["ln2_done"], t + 1)
                for k in range(KC):
                    mm = T.transpose(ps[:, A0, k * P:(k + 1) * P], xn2[:, k * P:(k + 1) * P], ident[:, :])
                mm.then_inc(sm["xcT_mm"], 1)

            def project_ctx(t):
                pe.wait_ge(sm["xcT_ready"], t + 1)
                wait(pe, sm["sc_ready"], t)
                for c in range(2):
                    for k in range(KC):
                        T.matmul(ps[:, B2, c * P:(c + 1) * P],
                                 xwk_rep[:, k, 2 * c:2 * c + 2, :, :].rearrange("p g h d -> p (g h d)"),
                                 xcT[:, KC + k, :], start=(k == 0), stop=(k == KC - 1))
                for s in range(SEQS):
                    for r in range(2):
                        for k in range(KC):
                            mm = T.matmul(ps[r * S:(r + 1) * S, B2, 256 + s * S:256 + (s + 1) * S],
                                          xcT[:, KC + k, s * S:(s + 1) * S], xwv[:, k, :],
                                          start=(k == 0), stop=(k == KC - 1))
                mm.then_inc(sm["ckv_mm"], 1)

            def project_q2(t):
                wait(pe, sm["xn3T_ready"], t - 2)
                for c in range(KC):
                    for k in range(KC):
                        mm = T.matmul(ps[:, B3, c * P:(c + 1) * P], xwq[:, k, c * P:(c + 1) * P], xcT[:, k, :],
                                      start=(k == 0), stop=(k == KC - 1))
                mm.then_inc(sm["q2_mm"], 1)

            def scores(t, c):
                if c == 0:
                    pe.wait_ge(sm["q2T_ready"], t + 1)
                    pe.wait_ge(sm["kbd_ready"], t + 1)
                    pe.wait_ge(sm["vbd_ready"], t + 1)
                    wait(pe, sm["prT_ready"], 2 * t)
                    wait(pe, sm["logits_ready"], t - 2)
                    alone(pe, sm["pe_passed"])
                for j in range(4):
                    q = slice(32 * j, 32 * j + 32)
                    for s in range(SEQS):
                        mm = T.matmul(ps[s * S:(s + 1) * S, B0 + j, c * P:(c + 1) * P],
                                      q2T[q, c, s * S:(s + 1) * S], k_bd[q, c, :, s * S:(s + 1) * S],
                                      start=True, stop=True)
                if c == 1:
                    mm.then_inc(sm["scores_mm"], 1)

            def transpose_probs(t):
                pe.wait_ge(sm["exp_ready"], t + 1)
                for b in range(8):
                    mm = T.transpose(ps[:, B0 + b // 4, (b % 4) * P:(b % 4 + 1) * P], pr[:, b * P:(b + 1) * P],
                                     ident[:, :])
                mm.then_inc(sm["prT_mm"], 1)

            def probs_values(t, q):
                pe.wait_ge(sm["prT_ready"], 2 * (t + 1))
                wait(pe, sm["x2_ready"], t)
                alone(pe, sm["pe_passed"])
                for c in range(2):
                    for j in range(4):
                        for s in range(SEQS):
                            col = (c * 4 + j) * 2 * (DH + 1)
                            mm = T.matmul(ps[s * S:(s + 1) * S, A3, col:col + 2 * (DH + 1)],
                                          prT[:, 2 * j + c, s * S:(s + 1) * S],
                                          v_bd[:, q, s * GROUPS + 2 * c + j // 2, :, :].rearrange("p h e -> p (h e)"),
                                          start=True, stop=True)
                mm.then_inc(sm["pv_mm"], 1)

            def transpose_o2(t):
                pe.wait_ge(sm["o2_ready"], t + 1)
                for k in range(KC):
                    mm = T.transpose(ps[:, A3, k * P:(k + 1) * P], o2[:, k * P:(k + 1) * P], ident[:, :])
                mm.then_inc(sm["o2T_mm"], 1)

            def project_cross(t):
                pe.wait_ge(sm["o2T_ready"], t + 1)
                for k in range(KC):
                    mm = T.matmul(ps[:, A3, 0:D], o2T[:, k, :], xwo[:, k, :], start=(k == 0), stop=(k == KC - 1))
                mm.then_inc(sm["xo_mm"], 1)

            def transpose_x3(t):
                pe.wait_ge(sm["ln3_done"], t + 1)
                pe.wait_ge(sm["sc_ready"], min(t + 3, TILES) if isinstance(t, int) else t + 3)
                for k in range(KC):
                    mm = T.transpose(ps[:, B3, k * P:(k + 1) * P], xn3[:, 0, k * P:(k + 1) * P], ident[:, :])
                mm.then_inc(sm["xT_mm"], 1)

            def router(t):
                pe.wait_ge(sm["xn3T_ready"], t + 1)
                if isinstance(t, int):
                    wait(pe, sm["logits_ready"], t)
                pe.wait_ge(sm["vbd_ready"], min(t + 4, TILES) if isinstance(t, int) else t + 4)
                for k in range(KC):
                    mm = T.matmul(ps[:, B2, 0:ROUTE], xn3T[:, k, :], w_route[:, k, :], start=(k == 0), stop=(k == KC - 1))
                mm.then_inc(sm["route_mm"], 1)

            def keep_warm(bank, n):
                for _ in range(n):
                    T.matmul(ps[:, bank, 0:D], zeros[:, 0:P], zeros[:, 0:D], start=True, stop=True)

            def stay_warm(t):
                if isinstance(t, int) and t > TILES:
                    keep_warm(A2, 2)

            def body(t, q):
                if has(t, -4):
                    stay_warm(t)
                    transpose_x3(t - 4)
                if has(t, -1):
                    project_ctx(t - 1)
                if has(t, 0):
                    query_kv(t)
                if has(t, 1):
                    transpose_x(t + 1)
                if has(t, -1):
                    stay_warm(t)
                    project_q2(t - 1)
                if has(t, 0):
                    transpose_o(t)
                if has(t, 1):
                    project_kv(t + 1)
                if has(t, -4):
                    stay_warm(t)
                    router(t - 4)
                if has(t, -2):
                    stay_warm(t)
                    transpose_probs(t - 2)
                if has(t, 0):
                    project_attn(t)
                if has(t, 1):
                    project_q(t + 1)
                if has(t, -2):
                    stay_warm(t)
                    probs_values(t - 2, q)
                if has(t, -1):
                    stay_warm(t)
                    scores(t - 1, 0)
                if has(t, -2):
                    stay_warm(t)
                    transpose_o2(t - 2)
                if has(t, -1):
                    scores(t - 1, 1)
                if has(t, 1):
                    key_value(t + 1)
                if has(t, 0):
                    transpose_xc(t)
                if has(t, -2):
                    stay_warm(t)
                    project_cross(t - 2)

            def before_0():
                pe.wait_ge(sm["w_out"], 16 * W_OUT)

            def before_1():
                pe.wait_ge(sm["w_cross"], 16 * W_CROSS)
                pe.wait_ge(sm["const_in"], 16 * W_CONST)
                pe.wait_ge(sm["consts_v"], 8)

            pe.wait_ge(sm["zeros_ready"], 1)
            keep_warm(B3, WARM_UP)
            pe.wait_ge(sm["ident_in"], 16)
            pe.wait_ge(sm["w_self"], 16 * W_SELF)
            attention_iterations(pe, body, TILES + 4, before_0, before_1)

            def product(out_ap, hi, lo, rows, cols, first, last):
                for lhs, rhs, st, en in ((hi, w_hi, first, False), (hi, w_lo, False, False), (lo, w_hi, False, last)):
                    mm = T.matmul(out_ap, lhs, rhs[rows, cols], start=st, stop=en)
                return mm

            pe.wait_ge(sm["w_lo_ready"], W_PARTS)
            pe.wait_ge(sm["x2_ready"], TILES)
            pe.wait_ge(sm["logits_ready"], TILES)

            def ranks():
                pe.wait_ge(sm["hotb_ready"], 1)
                for r in range(2):
                    T.matmul(ps[:, LG, 0:NE * TILES], before_b[:, :], hot_b[:, r, :], start=(r == 0), stop=(r == 1))
                for r in range(2):
                    mm = T.matmul(ps[:, LG, NE * TILES:2 * NE * TILES], ones_b[:, :], hot_b[:, r, :], start=(r == 0), stop=(r == 1))
                mm.then_inc(sm["rank_mm"], 1)

            def transpose_sx(t, p):
                pe.wait_ge(sm["s_x_ready"], t + 1)
                wait(pe, sm["s_xl_ready"], t)
                for k in range(KC):
                    mm = T.transpose(ps[:, TX, k * P:(k + 1) * P], xn3[:, p, k * P:(k + 1) * P], ident[:, :])
                mm.then_inc(sm["s_xT_mm"], 1)

            def shared_gate_up(t, p):
                pe.wait_ge(sm["s_xl_ready"], t + 1)
                wait(pe, sm["s_h_ready"], t - 1)
                for bank, base, done in ((GT, W_SHGATE, "s_gate_mm"), (UP, W_SHUP, "s_up_mm")):
                    for k in range(KC):
                        mm = product(ps[:, bank + p, 0:HS], xh[:, p, k, :], xl[:, p, k, :], slice(0, P),
                                     slice(base + k * HS, base + (k + 1) * HS), k == 0, k == KC - 1)
                    mm.then_inc(sm[done], 1)

            def transpose_sh(t, p):
                pe.wait_ge(sm["s_h_ready"], t + 1)
                wait(pe, sm["s_hl_ready"], t)
                T.transpose(ps[:, HT, 0:P], s_h[:, p, 0:P], ident[:, :])
                T.transpose(ps[:, HT, P:2 * P], s_h[:, p, P:2 * P], ident[:, :])
                T.transpose(ps[0:HS_LAST, HT, 2 * P:3 * P], s_h[:, p, 2 * P:HS], ident[:, :]).then_inc(sm["hT_mm"], 1)

            def shared_down(t, p):
                pe.wait_ge(sm["s_hl_ready"], t + 1)
                wait(pe, sm["x3_ready"], t)
                for c in range(3):
                    rows = slice(0, P if c < 2 else HS_LAST)
                    mm = product(ps[:, DN, 0:D], s_hh[rows, p, c, :], s_hl[rows, p, c, :], rows,
                                 slice(W_SHDOWN + c * D, W_SHDOWN + (c + 1) * D), c == 0, c == 2)
                mm.then_inc(sm["s_down_mm"], 1)

            def shared(t, p, prev, prev2, nxt):
                shared_gate_up(t, p)
                if nxt:
                    transpose_sx(t + 1, 1 - p)
                if prev:
                    transpose_sh(t - 1, 1 - p)
                if prev2:
                    shared_down(t - 2, p)

            transpose_sx(0, 0)
            shared(0, 0, False, False, True)
            shared_gate_up(1, 1)
            ranks()
            transpose_sx(2, 0)
            transpose_sh(0, 0)
            with pe.Fori(1, TILES // 2 - 1) as pair:
                t = 2 * pair
                shared(t, 0, True, True, True)
                shared(t + 1, 1, True, True, True)
            shared(TILES - 2, 0, True, True, True)
            shared(TILES - 1, 1, True, True, False)

            def expert_of(i):
                return pe.value_load(slot_ei[0:1, i:i + 1], min_val=0, max_val=NE - 1)

            def transpose_slots(i, q):
                p = q % 2
                pe.wait_ge(sm[f"xs_in{q}"], 4 * (i - q) + 16)
                wait(pe, sm["e_xl_ready"], i - 1)
                for k in range(KC):
                    mm = T.transpose(ps[:, EX + p, k * P:(k + 1) * P], xs[:, q, k * P:(k + 1) * P], ident[:, :])
                mm.then_inc(sm["e_xT_mm"], 1)

            def gate_up(i, p, e):
                pe.wait_ge(sm["e_xl_ready"], i + 1)
                wait(pe, sm["e_h_ready"], i - 1)
                for k in range(KC):
                    mm = product(ps[:, EG + p, 0:2 * H], xh[:, p, k, :], xl[:, p, k, :], slice(0, P),
                                 bass.ds(e * (KC * 2 * H) + (W_GU + k * 2 * H), 2 * H), k == 0, k == KC - 1)
                mm.then_inc(sm["gu_mm"], 1)

            def transpose_h(i, p):
                pe.wait_ge(sm["e_h_ready"], i + 1)
                wait(pe, sm["e_hl_ready"], i - 1)
                for c in range(2):
                    mm = T.transpose(ps[0:HC, EH + p, c * P:(c + 1) * P], e_h[:, p, c * HC:(c + 1) * HC], ident[:, :])
                mm.then_inc(sm["e_hT_mm"], 1)

            def expert_down(i, p, e):
                pe.wait_ge(sm["e_hl_ready"], i + 1)
                wait(pe, sm["e_y_ready"], i - 1)
                for c in range(2):
                    mm = product(ps[:, ED + p, 0:D], e_hh[:, p, c, :], e_hl[:, p, c, :], slice(0, HC),
                                 bass.ds(e * (2 * D) + (W_DOWN + c * D), D), c == 0, c == 1)
                mm.then_inc(sm["e_down_mm"], 1)

            pe.wait_ge(sm["slots_ready"], 1)
            transpose_slots(0, 0)
            pe.wait_ge(sm["s_h_ready"], TILES - 1)
            transpose_slots(1, 1)
            shared_down(TILES - 2, 0)
            transpose_sh(TILES - 1, 1)
            expert = {}
            for i in range(SLOT_TILES + 2):
                p = i % 2
                if i < SLOT_TILES:
                    expert[i] = expert_of(i)
                    gate_up(i, p, expert[i])
                if i == 0:
                    shared_down(TILES - 1, 1)
                if i == 2:
                    pe.wait_ge(sm["x3_ready"], TILES)
                if 1 <= i <= SLOT_TILES:
                    transpose_h(i - 1, 1 - p)
                if i + 2 < SLOT_TILES:
                    transpose_slots(i + 2, (i + 2) % 4)
                if i >= 2:
                    expert_down(i - 2, p, expert[i - 2])

        @block.scalar
        def _(act):
            A = nc.scalar
            def k_exp(t):
                act.wait_ge(sm["k1_ready"], t + 1)
                wait(act, sm["kf_ready"], t)
                A.activation(ke[:, :], k1[:, :], ACT.Exp, bias=minus_one[:, :]).then_inc(sm["ke_ready"], 1)

            def q_exp(t):
                act.wait_ge(sm["q_mm"], t + 1)
                wait(act, sm["qf_ready"], t)
                for c in range(KC):
                    A.activation(q1[:, c, :], ps[:, A0, (KC + c) * P:(KC + c + 1) * P], ACT.Identity,
                                 bias=bq1[:, c:c + 1]).then_inc(sm["q1_ready"], 1)
                act.wait_ge(sm["q1_ready"], 2 * (t + 1))
                A.activation(qe[:, :, :], q1[:, :, :], ACT.Exp, bias=minus_one[:, :]).then_inc(sm["qe_ready"], 1)

            def copy_xcT(t):
                act.wait_ge(sm["xcT_mm"], t + 1)
                wait(act, sm["q2_mm"], t)
                A.activation(xcT[:, :, :].rearrange("p c t -> p (c t)"), ps[:, A0, :], ACT.Copy).then_inc(sm["xcT_ready"], 1)

            def copy_prT(t):
                act.wait_ge(sm["prT_mm"], t + 1)
                wait(act, sm["pv_mm"], t)
                for b in range(2):
                    A.activation(prT[:, 4 * b:4 * b + 4, :].rearrange("p c t -> p (c t)"), ps[:, B0 + b, :],
                                 ACT.Copy).then_inc(sm["prT_ready"], 1)

            def scale_q2(t):
                act.wait_ge(sm["q2_mm"], t + 1)
                wait(act, sm["scores_mm"], t)
                A.activation(q2T[:, :, :].rearrange("p c t -> p (c t)"), ps[:, B3, 0:D], ACT.Copy,
                             scale=DH ** -0.5).then_inc(sm["q2T_ready"], 1)

            def copy_oT(t):
                act.wait_ge(sm["oT_mm"], t + 1)
                wait(act, sm["attn_mm"], t)
                A.activation(oT[:, :, :].rearrange("p c t -> p (c t)"), ps[:, A1, 0:D], ACT.Copy).then_inc(sm["oT_ready"], 1)

            def copy_o2T(t):
                act.wait_ge(sm["o2T_mm"], t + 1)
                wait(act, sm["xo_mm"], t)
                A.activation(o2T[:, :, :].rearrange("p c t -> p (c t)"), ps[:, A3, 0:D], ACT.Copy).then_inc(sm["o2T_ready"], 1)

            def copy_xn1T(t):
                act.wait_ge(sm["xn1T_mm"], t + 1)
                wait(act, sm["q_mm"], t)
                A.activation(xn1T[:, :, :].rearrange("p c t -> p (c t)"), ps[:, A0, 0:D], ACT.Copy).then_inc(sm["xn1T_ready"], 1)

            def score_exp(t):
                act.wait_ge(sm["sub_ready"], t + 1)
                wait(act, sm["prT_mm"], t)
                A.activation(pr[:, :], sc[:, :], ACT.Exp).then_inc(sm["exp_ready"], 1)

            def split_high(c, half):
                act.wait_ge(sm[f"w_part{half}"], 8 * (c - half) + 16)
                A.activation(w_hi[:, bass.ds(c * W_PART, W_PART)], w_stage[:, half, :], ACT.Copy).then_inc(sm["w_hi_ready"], 1)

            def normalise3(t, out_ap):
                return A.activation(out_ap, x_all[:, bass.ds(t, 1), :].rearrange("p t d -> p (t d)"), ACT.Identity,
                                    bias=nb3[:, bass.ds(t, 1)], scale=rs3[:, bass.ds(t, 1)])

            def copy_xn3T(t):
                act.wait_ge(sm["xT_mm"], t + 1)
                wait(act, sm["route_mm"], t)
                A.activation(xn3T[:, :, :].rearrange("p c t -> p (c t)"), ps[:, B3, 0:D], ACT.Copy).then_inc(sm["xn3T_ready"], 1)

            def ln3_norm(t):
                act.wait_ge(sm["ln3_nb"], t + 1)
                wait(act, sm["xT_mm"], t)
                normalise3(t, xn3[:, 0, :]).then_inc(sm["ln3_done"], 1)

            def k_block(t):
                act.wait_ge(sm["ckv_mm"], t + 1)
                wait(act, sm["scores_mm"], t)
                for h in range(2):
                    last = A.activation(k_bd[:, :, h, :], ps[:, B2, 0:D].rearrange("p (c t) -> p c t", c=2), ACT.Copy,
                                        scale=row_head[:, h:h + 1])
                last.then_inc(sm["kbd_ready"], 1)

            def v_block(t, q):
                wait(act, sm["pv_mm"], t - 1)
                vv = ps[:, B2, 256:384].rearrange("p (g e) -> p g e", e=DH)
                for h in range(2):
                    last = A.activation(v_bd[:, q, :, h, 0:DH], vv, ACT.Copy, scale=row_half[:, h:h + 1])
                last.then_inc(sm["vbd_ready"], 1)

            def body(t, q):
                if has(t, -4):
                    copy_xn3T(t - 4)
                if has(t, 1):
                    copy_xn1T(t + 1)
                if has(t, -1):
                    k_block(t - 1)
                    v_block(t - 1, 1 - q)
                if has(t, -2):
                    score_exp(t - 2)
                if has(t, -1):
                    scale_q2(t - 1)
                if has(t, 0):
                    copy_oT(t)
                if splits(t):
                    split_high(t - FIRST_SPLIT, q)
                if has(t, 1):
                    k_exp(t + 1)
                if has(t, -2):
                    copy_prT(t - 2)
                if has(t, 1):
                    q_exp(t + 1)
                if has(t, -3):
                    ln3_norm(t - 3)
                if has(t, -2):
                    copy_o2T(t - 2)
                if has(t, 0):
                    copy_xcT(t)

            act.wait_ge(sm["consts_v"], 2)
            A.activation(early[:, :], minus_one[:, :], ACT.Exp).then_inc(sm["early_exp"], 1)
            act.wait_ge(sm["consts_v"], 4)
            def before_0():
                pass

            def before_1():
                act.wait_ge(sm["mask_in"], 16 * W_MASK)
                act.wait_ge(sm["consts_v"], 8)

            attention_iterations(act, body, TILES + 4, before_0, before_1)

            def shared_x(t, p):
                wait(act, sm["s_xT_mm"], t - 1)
                if not isinstance(t, int):
                    alone(act, sm["act_passed"])
                normalise3(t, xn3[:, p, :]).then_inc(sm["s_x_ready"], 1)

            def send_rows(t):
                for r in range(2):
                    normalise3(t, x_send[:, bass.ds(t, 1), r, 0:D].rearrange("p t d -> p (t d)")).then_inc(sm["rows_ready"], 1)

            def shared_x_high(t, p):
                act.wait_ge(sm["s_xT_mm"], t + 1)
                wait(act, sm["s_up_mm"], t - 1)
                A.activation(xh[:, p, :, :].rearrange("p c t -> p (c t)"), ps[:, TX, 0:D], ACT.Copy).then_inc(sm["s_xh_ready"], 1)

            def shared_tanh(t, p):
                act.wait_ge(sm["s_gate_mm"], t + 1)
                wait(act, sm["s_gg_ready"], t)
                A.activation(s_th[:, :], ps[:, GT + p, 0:HS], ACT.Tanh, scale=0.5).then_inc(sm["s_th_ready"], 1)

            def sh_high(t, p):
                act.wait_ge(sm["hT_mm"], t + 1)
                wait(act, sm["s_down_mm"], t - 1)
                A.activation(s_hh[:, p, 0:2, :].rearrange("p c t -> p (c t)"), ps[:, HT, 0:2 * P], ACT.Copy)
                A.activation(s_hh[0:HS_LAST, p, 2, :], ps[0:HS_LAST, HT, 2 * P:3 * P], ACT.Copy).then_inc(sm["s_hh_ready"], 1)

            def shared(t, p, prev, nxt, nxt2, nxt3):
                shared_tanh(t, p)
                if nxt:
                    shared_x_high(t + 1, 1 - p)
                if prev:
                    sh_high(t - 1, 1 - p)
                if nxt2:
                    shared_x(t + 2, p)
                if nxt3:
                    send_rows(t + 3)

            act.wait_ge(sm["xT_mm"], TILES)
            shared_x(0, 0)
            shared_x(1, 1)
            act.wait_ge(sm["route_mm"], TILES)
            shared_x_high(0, 0)
            act.wait_ge(sm["logits_ready"], TILES)
            send_rows(0)
            A.activation(sgt[:, :], lg[:, :, NE:NE + 1].rearrange("p t o -> p (t o)"), ACT.Tanh, scale=0.5).then_inc(sm["sgt_ready"], 1)
            act.wait_ge(sm["lgs_ready"], 1)
            A.activation(pe8[:, :, :], lgs[:, :, :], ACT.Exp).then_inc(sm["pe8_ready"], 1)
            send_rows(1)
            send_rows(2)
            shared(0, 0, False, True, True, True)
            shared(1, 1, True, True, True, True)
            with act.Fori(1, TILES // 2 - 2) as pair:
                t = 2 * pair
                shared(t, 0, True, True, True, True)
                shared(t + 1, 1, True, True, True, True)
            shared(TILES - 4, 0, True, True, True, True)
            shared(TILES - 3, 1, True, True, True, False)
            shared(TILES - 2, 0, True, True, False, False)
            shared(TILES - 1, 1, True, False, False, False)

            def slots_high(i, p):
                act.wait_ge(sm["e_xT_mm"], i + 1)
                A.activation(xh[:, p, :, :].rearrange("p c t -> p (c t)"), ps[:, EX + p, 0:D], ACT.Copy).then_inc(sm["e_xh_ready"], 1)

            def expert_tanh(i, p):
                act.wait_ge(sm["gu_mm"], i + 1)
                wait(act, sm["e_gg_ready"], i - 1)
                A.activation(e_th[:, p, :], ps[:, EG + p, 0:H], ACT.Tanh, scale=0.5).then_inc(sm["e_th_ready"], 1)

            def h_high(i, p):
                act.wait_ge(sm["e_hT_mm"], i + 1)
                wait(act, sm["e_down_mm"], i - 1)
                A.activation(e_hh[:, p, :, :].rearrange("p c t -> p (c t)"), ps[0:HC, EH + p, 0:2 * P], ACT.Copy).then_inc(sm["e_hh_ready"], 1)

            def copy_y(i, q):
                act.wait_ge(sm["e_down_mm"], i + 1)
                wait(act, sm[f"ys_out{q}"], 4 * (i - q))
                A.activation(e_y[:, q, :], ps[:, ED + q % 2, 0:D], ACT.Copy).then_inc(sm["e_y_ready"], 1)

            def experts(i, q, prev, prev2, nxt2):
                p = q % 2
                expert_tanh(i, p)
                if prev:
                    h_high(i - 1, 1 - p)
                if nxt2:
                    slots_high(i + 2, p)
                if prev2:
                    copy_y(i - 2, (q + 2) % 4)

            slots_high(0, 0)
            slots_high(1, 1)
            sh_high(TILES - 1, 1)
            for i in range(8):
                experts(i, i % 4, i >= 1, i >= 2, True)
            with act.Fori(2, SLOT_TILES // 4 - 1) as quad:
                i = 4 * quad
                for q in range(4):
                    experts(i + q, q, True, True, True)
            for q in range(4):
                experts(SLOT_TILES - 4 + q, q, True, True, q < 2)
            h_high(SLOT_TILES - 1, 1)
            copy_y(SLOT_TILES - 2, 2)
            copy_y(SLOT_TILES - 1, 3)

            def store_out(t, q):
                act.wait_ge(sm["y_ready"], t + 1)
                act.dma_start(out_d[bass.ds(t * P, P), :], y2[:, q, :]).then_inc(sm[f"stored{q}"], 16)

            with act.Fori(0, TILES // 4) as quad:
                t = 4 * quad
                for q in range(4):
                    store_out(t + q, q)

        @block.vector
        def _(v):
            V = nc.vector

            def xt(t):
                return x_all[:, bass.ds(t, 1), :].rearrange("p t d -> p (t d)")

            V.memset(minus_one[:, :], -1.0).then_inc(sm["consts_v"], 1)
            V.memset(vo[:, :, 32:33], 1.0).then_inc(sm["consts_v"], 1)

            def ln1_stats(t):
                wait(v, sm["ln1_rs"], t)
                wait(v, sm["ln1_done"], t)
                alone(v, sm["dve_passed"])
                V.bn_stats(st1[:, :], xt(t)).then_inc(sm["ln1_st"], 1)
                v.wait_ge(sm["ln1_st"], t + 1)
                alone(v, sm["dve_passed"])
                V.bn_aggr(mv1[:, :], st1[:, :]).then_inc(sm["ln1_mv"], 1)

            def ln1_norm(t):
                v.wait_ge(sm["ln1_rs"], t + 1)
                wait(v, sm["xn1T_mm"], t)
                V.tensor_scalar(xn1[:, :], xt(t), mv1[:, 0:1], rs1[:, :], ALU.subtract, ALU.mult).then_inc(sm["ln1_done"], 1)

            def k_v_bias(t):
                v.wait_ge(sm["kv_mm"], t + 1)
                wait(v, sm["kf_ready"], t)
                V.tensor_tensor(k1[:, :], ps[:, A2, 0:D], bkv[:, 0:D], ALU.add).then_inc(sm["k1_ready"], 1)
                wait(v, sm["kvs_mm"], t)
                V.tensor_tensor(vo[:, :, 0:32], ps[:, A2, D:2 * D].rearrange("p (g e) -> p g e", e=32),
                                bkv[:, D:2 * D].rearrange("p (g e) -> p g e", e=32), ALU.add).then_inc(sm["v_ready"], 1)

            def k_feature(t):
                v.wait_ge(sm["ke_ready"], t + 1)
                V.scalar_tensor_tensor(out=kf[:, :], in0=k1[:, :], scalar=1.0, in1=ke[:, :], op0=ALU.max,
                                       op1=ALU.min).then_inc(sm["kf_ready"], 1)

            def q_feature(t):
                v.wait_ge(sm["qe_ready"], t + 1)
                wait(v, sm["numden_mm"], t)
                V.scalar_tensor_tensor(out=qf[:, :, :].rearrange("p c t -> p (c t)"),
                                       in0=q1[:, :, :].rearrange("p c t -> p (c t)"), scalar=1.0,
                                       in1=qe[:, :, :].rearrange("p c t -> p (c t)"), op0=ALU.max,
                                       op1=ALU.min).then_inc(sm["qf_ready"], 1)

            def block_diagonal(t):
                v.wait_ge(sm["kvs_mm"], t + 1)
                wait(v, sm["numden_mm"], t)
                for s in range(SEQS):
                    g = ps[:, (A2, A1)[s], 0:66].rearrange("p (c o e) -> p c o e", o=1, e=33)
                    bm = spread(block_mask[:, :].rearrange("p (o j e) -> p o j e", o=1, e=32), 1, 2)
                    oh = spread(own_head[:, :].rearrange("p (o j) -> p o j", o=1), 1, 2)
                    V.tensor_tensor(kv_bd[:, s, :, 0:P].rearrange("p c (j e) -> p c j e", e=32),
                                    spread(g[:, :, :, 0:32], 2, 4), bm, ALU.mult)
                    last = V.tensor_tensor(kv_bd[:, s, :, P:P + HALF],
                                           spread(g[:, :, :, 32:33].rearrange("p c o e -> p c (o e)"), 2, HALF), oh, ALU.mult)
                last.then_inc(sm["kvs_ready"], 1)

            def divide(t):
                nd = ps[:, A1, 0:2 * (P + HALF)].rearrange("p (c n) -> p c n", c=2)
                v.wait_ge(sm["numden_mm"], t + 1)
                V.tensor_scalar(den[:, :, :], nd[:, :, P:P + HALF], DEN_EPS, None, ALU.add).then_inc(sm["den_ready"], 1)
                v.wait_ge(sm["den_ready"], t + 1)
                V.reciprocal(rden[:, :, :], den[:, :, :]).then_inc(sm["rden_ready"], 1)
                v.wait_ge(sm["rden_ready"], t + 1)
                wait(v, sm["oT_mm"], t)
                V.tensor_tensor(o[:, :].rearrange("p (c h e) -> p c h e", c=2, e=DH),
                                nd[:, :, 0:P].rearrange("p c (h e) -> p c h e", e=DH),
                                spread(rden[:, :, :].rearrange("p c (h o) -> p c h o", o=1), 3, DH),
                                ALU.mult).then_inc(sm["o_ready"], 1)

            def residual1(t):
                v.wait_ge(sm["attn_mm"], t + 1)
                v.wait_ge(sm["xbo_ready"], t + 1)
                V.tensor_tensor(xt(t), ps[:, A1, 0:D], xt(t), ALU.add).then_inc(sm["x1_ready"], 1)

            def ln2_stats(t):
                v.wait_ge(sm["x1_ready"], t + 1)
                wait(v, sm["ln2_rs"], t)
                wait(v, sm["ln2_done"], t)
                alone(v, sm["dve_passed"])
                V.bn_stats(st2[:, :], xt(t)).then_inc(sm["ln2_st"], 1)
                v.wait_ge(sm["ln2_st"], t + 1)
                alone(v, sm["dve_passed"])
                V.bn_aggr(mv2[:, :], st2[:, :]).then_inc(sm["ln2_mv"], 1)

            def ln2_norm(t):
                v.wait_ge(sm["ln2_rs"], t + 1)
                wait(v, sm["xcT_mm"], t)
                V.tensor_scalar(xn2[:, :], xt(t), mv2[:, 0:1], rs2[:, :], ALU.subtract, ALU.mult).then_inc(sm["ln2_done"], 1)

            def score_add(t):
                v.wait_ge(sm["scores_mm"], t + 1)
                v.wait_ge(sm["bias_ready"], t + 1)
                wait(v, sm["exp_ready"], t)
                V.tensor_tensor(sc[:, :].rearrange("p (j c) -> p j c", j=4), ps[:, B0:B3 + 1, 0:256],
                                bias_t[:, :].rearrange("p (j c) -> p j c", j=4), ALU.add).then_inc(sm["sc_ready"], 1)

            def score_max(t):
                v.wait_ge(sm["sc_ready"], t + 1)
                wait(v, sm["sub_ready"], t)
                V.tensor_reduce(smax[:, :], sc[:, :].rearrange("p (h k) -> p h k", h=HEADS), AX.X,
                                ALU.max).then_inc(sm["smax_ready"], 1)

            def scale_values(t):
                nd = ps[:, A3, 0:HEADS * (DH + 1)].rearrange("p (h e) -> p h e", e=DH + 1)
                v.wait_ge(sm["pv_mm"], t + 1)
                V.reciprocal(rsum[:, :], nd[:, :, DH:DH + 1].rearrange("p h o -> p (h o)")).then_inc(sm["rsum_ready"], 1)
                v.wait_ge(sm["rsum_ready"], t + 1)
                wait(v, sm["o2T_mm"], t)
                V.tensor_tensor(o2[:, :].rearrange("p (h e) -> p h e", e=DH), nd[:, :, 0:DH],
                                spread(rsum[:, :].rearrange("p (h o) -> p h o", o=1), 2, DH), ALU.mult).then_inc(sm["o2_ready"], 1)

            def residual2(t):
                v.wait_ge(sm["xo_mm"], t + 1)
                V.tensor_tensor(xt(t), ps[:, A3, 0:D], xt(t), ALU.add).then_inc(sm["x2_ready"], 1)

            def ln3_stats(t):
                v.wait_ge(sm["x2_ready"], t + 1)
                alone(v, sm["dve_passed"])
                V.bn_stats(st3[:, :], xt(t)).then_inc(sm["ln3_st"], 1)
                v.wait_ge(sm["ln3_st"], t + 1)
                wait(v, sm["ln3_ve"], t)
                wait(v, sm["neg_mean_ready"], t)
                alone(v, sm["dve_passed"])
                V.bn_aggr(mv3[:, :], st3[:, :]).then_inc(sm["ln3_mv"], 1)

            def negate_mean3(t):
                v.wait_ge(sm["ln3_mv"], t + 1)
                wait(v, sm["ln3_nb"], t)
                V.tensor_scalar(neg_mean3[:, :], mv3[:, 0:1], -1.0, None, ALU.mult).then_inc(sm["neg_mean_ready"], 1)

            def keep_logits(t):
                v.wait_ge(sm["route_mm"], t + 1)
                V.tensor_copy(lg[:, bass.ds(t, 1), :].rearrange("p t e -> p (t e)"), ps[:, B2, 0:ROUTE]
                              ).then_inc(sm["logits_ready"], 1)

            def cross_constants():
                v.wait_ge(sm["w_cross"], 16 * W_CROSS)
                v.wait_ge(sm["mask_in"], 16 * W_MASK)
                V.tensor_copy(xwk_rep[:, :, :, :, :].rearrange("p k g h d -> p (k g) h d"),
                              spread(xwk[:, :, :].rearrange("p k (g o d) -> p (k g) o d", g=GROUPS, o=1), 2, HEADS // GROUPS)
                              ).then_inc(sm["consts_v"], 1)
                for h in range(2):
                    V.tensor_copy(v_bd[:, :, :, h, DH:DH + 1].rearrange("p q g o -> p (q g) o"),
                                  spread(row_half[:, h:h + 1].rearrange("p (g o) -> p g o", o=1), 1, 2 * SEQS * GROUPS)
                                  ).then_inc(sm["consts_v"], 1)
                V.tensor_scalar(key_off[:, :, :], mask_u8[:, :, :], -1.0, BIG, ALU.add, ALU.mult).then_inc(sm["consts_v"], 1)
                v.wait_ge(sm["consts_v"], 8)

            def body(t, q):
                if has(t, 0):
                    divide(t)
                if isinstance(t, int) and t == 0:
                    cross_constants()
                if has(t, -3):
                    residual2(t - 3)
                    ln3_stats(t - 3)
                if has(t, 1):
                    k_v_bias(t + 1)
                    k_feature(t + 1)
                if has(t, -3):
                    negate_mean3(t - 3)
                if has(t, -4):
                    keep_logits(t - 4)
                if has(t, 0):
                    residual1(t)
                    ln2_stats(t)
                if has(t, -2):
                    scale_values(t - 2)
                if has(t, 0):
                    ln2_norm(t)
                if has(t, 1):
                    q_feature(t + 1)
                if has(t, 2):
                    ln1_stats(t + 2)
                if has(t, -1):
                    score_add(t - 1)
                if has(t, 1):
                    block_diagonal(t + 1)
                if has(t, -1):
                    score_max(t - 1)
                if has(t, 2):
                    ln1_norm(t + 2)

            v.wait_ge(sm["x_first"], 16)
            ln1_stats(0)
            ln1_norm(0)
            v.wait_ge(sm["w_self"], 16 * W_SELF)
            V.tensor_scalar(bkv[:, 0:D], bkv[:, 0:D], 1.0, None, ALU.add).then_inc(sm["consts_v"], 1)
            V.tensor_scalar(bq1[:, :], bq1[:, :], 1.0, None, ALU.add).then_inc(sm["consts_v"], 1)
            v.wait_ge(sm["heads_in"], 32)
            v.wait_ge(sm["consts_v"], 4)

            def before_0():
                v.wait_ge(sm["x_rest"], 16)

            def before_1():
                pass

            attention_iterations(v, body, TILES + 4, before_0, before_1)

            v.wait_ge(sm["const_in"], 16 * W_CONST)
            V.tensor_copy(before_b[:, :], before[:, :]).then_inc(sm["consts_v"], 1)
            V.memset(ones_b[:, :], 1.0).then_inc(sm["consts_v"], 1)
            V.memset(ones8[:, :], 1.0).then_inc(sm["consts_v"], 1)
            v.wait_ge(sm["consts_v"], 11)
            v.wait_ge(sm["x2_ready"], TILES)

            def shared_x_low(t, p):
                v.wait_ge(sm["s_xh_ready"], t + 1)
                V.tensor_tensor(xl[:, p, :, :].rearrange("p c t -> p (c t)"), ps[:, TX, 0:D],
                                xh[:, p, :, :].rearrange("p c t -> p (c t)").bitcast(F32), ALU.subtract).then_inc(sm["s_xl_ready"], 1)

            step = [0]

            def chained(ins):
                step[0] += 1
                ins.then_inc(sm["routing"], 1)
                v.wait_ge(sm["routing"], step[0])

            def by_expert(ap):
                return spread(ap.rearrange("p (t o) -> p t o", o=1), 2, NE)

            def by_tile(ap):
                return spread(ap.rearrange("p (o e) -> p o e", o=1), 1, TILES)

            def shared_h(t, p):
                v.wait_ge(sm["s_th_ready"], t + 1)
                V.scalar_tensor_tensor(out=s_gg[:, :], in0=s_th[:, :], scalar=1.0, in1=ps[:, GT + p, 0:HS],
                                       op0=ALU.add, op1=ALU.mult).then_inc(sm["s_gg_ready"], 1)
                v.wait_ge(sm["s_gg_ready"], t + 1)
                v.wait_ge(sm["s_up_mm"], t + 1)
                wait(v, sm["hT_mm"], t - 1)
                V.scalar_tensor_tensor(out=s_h[:, p, :], in0=s_gg[:, :], scalar=sg4[:, bass.ds(t, 1)], in1=ps[:, UP + p, 0:HS],
                                       op0=ALU.mult, op1=ALU.mult).then_inc(sm["s_h_ready"], 1)

            def sh_low(t, p):
                v.wait_ge(sm["s_hh_ready"], t + 1)
                V.tensor_tensor(s_hl[:, p, 0:2, :].rearrange("p c t -> p (c t)"), ps[:, HT, 0:2 * P],
                                s_hh[:, p, 0:2, :].rearrange("p c t -> p (c t)").bitcast(F32), ALU.subtract)
                V.tensor_tensor(s_hl[0:HS_LAST, p, 2, :], ps[0:HS_LAST, HT, 2 * P:3 * P],
                                s_hh[0:HS_LAST, p, 2, :].bitcast(F32), ALU.subtract).then_inc(sm["s_hl_ready"], 1)

            def residual3(t):
                v.wait_ge(sm["s_down_mm"], t + 1)
                V.tensor_tensor(xt(t), ps[:, DN, 0:D], xt(t), ALU.add).then_inc(sm["x3_ready"], 1)

            def shared(t, p, prev, prev2, nxt):
                shared_h(t, p)
                if nxt:
                    shared_x_low(t + 1, 1 - p)
                if prev:
                    sh_low(t - 1, 1 - p)
                if prev2:
                    residual3(t - 2)

            v.wait_ge(sm["route_mm"], TILES)
            shared_x_low(0, 0)
            v.wait_ge(sm["logits_ready"], TILES)
            chained(V.tensor_reduce(nmx[:, :], lg[:, :, 0:NE], AX.X, ALU.max))
            V.tensor_tensor(lgs[:, :, :], lg[:, :, 0:NE], by_expert(nmx[:, :]), ALU.subtract).then_inc(sm["lgs_ready"], 1)
            v.wait_ge(sm["sgt_ready"], 1)
            V.tensor_scalar(sg4[:, :], sgt[:, :], 1.0, 0.25, ALU.add, ALU.mult).then_inc(sm["sg4_ready"], 1)
            v.wait_ge(sm["pe8_ready"], 1)
            chained(V.tensor_reduce(psum8[:, :], pe8[:, :, :], AX.X, ALU.add))
            chained(V.reciprocal(prec8[:, :], psum8[:, :]))
            chained(V.tensor_tensor(prob[:, :, :], pe8[:, :, :], by_expert(prec8[:, :]), ALU.mult))
            for r, pr_r in enumerate((prob, prob2)):
                chained(V.tensor_reduce(top[:, r, :], pr_r[:, :, :], AX.X, ALU.max))
                chained(V.tensor_tensor(is_top[:, :, :], pr_r[:, :, :], by_expert(top[:, r, :]), ALU.is_equal))
                chained(V.tensor_tensor(is_top[:, :, :], is_top[:, :, :], by_tile(rev8[:, :]), ALU.mult))
                chained(V.tensor_reduce(top_e[:, :], is_top[:, :, :], AX.X, ALU.max))
                chained(V.tensor_tensor(hot[:, r, :, :], by_expert(top_e[:, :]), by_tile(rev8[:, :]), ALU.is_equal))
                if r == 0:
                    v.wait_ge(sm["sg4_ready"], 1)
                    shared(0, 0, False, False, True)
                    chained(V.scalar_tensor_tensor(out=prob2[:, :, :], in0=hot[:, 0, :, :], scalar=-2.0, in1=prob[:, :, :],
                                                   op0=ALU.mult, op1=ALU.add))
            V.tensor_copy(hot_b[:, :, :], hot[:, :, :, :].rearrange("p r t e -> p r (t e)")).then_inc(sm["hotb_ready"], 1)
            chained(V.tensor_tensor(tsum[:, :], top[:, 0, :], top[:, 1, :], ALU.add))
            chained(V.reciprocal(trec[:, :], tsum[:, :]))
            chained(V.tensor_tensor(w_choice[:, :, :], top[:, :, :], spread(trec[:, :].rearrange("p (o t) -> p o t", o=1), 1, 2),
                                    ALU.mult))
            shared(1, 1, True, False, True)
            v.wait_ge(sm["rank_mm"], 1)
            chained(V.tensor_copy(in_tile[:, :, :], ps[:, LG, NE * TILES:2 * NE * TILES].rearrange("p (t e) -> p e t", e=NE)))
            chained(V.tensor_tensor_scan(upto[:, :, :].rearrange("p e t -> p (e t)"), not_first[:, :, :].rearrange("p e t -> p (e t)"),
                                         in_tile[:, :, :].rearrange("p e t -> p (e t)"), 0.0, ALU.mult, ALU.add))
            chained(V.tensor_scalar(cnt_i[:, :], upto[:, :, TILES - 1:TILES].rearrange("p e o -> p (e o)"), float(P - 1), None, ALU.add))
            chained(V.tensor_scalar(til_i[:, :], cnt_i[:, :], 7, None, ALU.logical_shift_right))
            chained(V.tensor_copy(til[:, :], til_i[:, :]))
            chained(V.tensor_tensor_scan(cum[:, :], ones8[:, :], til[:, :], 0.0, ALU.mult, ALU.add))
            chained(V.tensor_tensor(first[:, :], cum[:, :], til[:, :], ALU.subtract))
            chained(V.tensor_tensor(upto[:, :, :], upto[:, :, :], in_tile[:, :, :], ALU.subtract))
            chained(V.scalar_tensor_tensor(out=rowf[:, :, :], in0=by_tile(first[:, :]), scalar=float(P),
                                           in1=upto[:, :, :].rearrange("p e t -> p t e"), op0=ALU.mult, op1=ALU.add))
            chained(V.tensor_tensor(rowf[:, :, :], rowf[:, :, :], ps[:, LG, 0:NE * TILES].rearrange("p (t e) -> p t e", e=NE), ALU.add))
            for r in range(2):
                chained(V.tensor_tensor(row_x[:, r, :, :], hot[:, r, :, :], rowf[:, :, :], ALU.mult))
            shared(2, 0, True, True, True)
            chained(V.tensor_reduce(posf[:, :, :], row_x[:, :, :, :], AX.X, ALU.add))
            V.tensor_copy(pos[:, :, :], posf[:, :, :].rearrange("p r t -> p t r")).then_inc(sm["pos_ready"], 1)

            def slot_table():
                slots_x = spread(iota_slot[:, :].rearrange("p (i o) -> p i o", o=1), 2, NE)
                chained(V.tensor_tensor(ge[:, :, :], slots_x, spread(cum[0:1, :].rearrange("p (o e) -> p o e", o=1), 1, SLOT_TILES),
                                        ALU.is_ge))
                chained(V.tensor_reduce(slot_e[:, :], ge[:, :, :], AX.X, ALU.add))
                V.tensor_scalar(slot_ei[:, :], slot_e[:, :], float(NE - 1), None, ALU.min).then_inc(sm["slots_ready"], 1)

            slot_table()
            shared(3, 1, True, True, True)
            with v.Fori(2, TILES // 2 - 1) as pair:
                t = 2 * pair
                shared(t, 0, True, True, True)
                shared(t + 1, 1, True, True, True)
            shared(TILES - 2, 0, True, True, True)
            shared(TILES - 1, 1, True, True, False)

            def slots_low(i, p):
                v.wait_ge(sm["e_xh_ready"], i + 1)
                V.tensor_tensor(xl[:, p, :, :].rearrange("p c t -> p (c t)"), ps[:, EX + p, 0:D],
                                xh[:, p, :, :].rearrange("p c t -> p (c t)").bitcast(F32), ALU.subtract).then_inc(sm["e_xl_ready"], 1)

            def expert_h(i, p):
                v.wait_ge(sm["e_th_ready"], i + 1)
                V.scalar_tensor_tensor(out=e_gg[:, p, :], in0=e_th[:, p, :], scalar=1.0, in1=ps[:, EG + p, 0:H],
                                       op0=ALU.add, op1=ALU.mult).then_inc(sm["e_gg_ready"], 1)
                v.wait_ge(sm["e_gg_ready"], i + 1)
                wait(v, sm["e_hT_mm"], i - 1)
                V.scalar_tensor_tensor(out=e_h[:, p, :], in0=e_gg[:, p, :], scalar=0.5, in1=ps[:, EG + p, H:2 * H],
                                       op0=ALU.mult, op1=ALU.mult).then_inc(sm["e_h_ready"], 1)

            def h_low(i, p):
                v.wait_ge(sm["e_hh_ready"], i + 1)
                V.tensor_tensor(e_hl[:, p, :, :].rearrange("p c t -> p (c t)"), ps[0:HC, EH + p, 0:2 * P],
                                e_hh[:, p, :, :].rearrange("p c t -> p (c t)").bitcast(F32), ALU.subtract).then_inc(sm["e_hl_ready"], 1)

            def rows_out(i, q):
                v.wait_ge(sm[f"xs_in{q}"], 4 * (i - q) + 16)
                wait(v, sm[f"ys_out{q}"], 4 * (i - q))
                V.tensor_tensor(out_row[:, q:q + 1], xs[:, q, D:D + 1], spare_rows[:, bass.ds(i, 1)], ALU.max
                                ).then_inc(sm["out_row_ready"], 1)

            def experts(i, q, prev, nxt2):
                p = q % 2
                rows_out(i, q)
                expert_h(i, p)
                if prev:
                    h_low(i - 1, 1 - p)
                if nxt2:
                    slots_low(i + 2, p)

            slots_low(0, 0)
            slots_low(1, 1)
            residual3(TILES - 2)
            sh_low(TILES - 1, 1)
            experts(0, 0, False, True)
            residual3(TILES - 1)
            for i in range(1, 4):
                experts(i, i, True, True)
            with v.Fori(1, SLOT_TILES // 4 - 1) as quad:
                i = 4 * quad
                for q in range(4):
                    experts(i + q, q, True, True)
            for q in range(4):
                experts(SLOT_TILES - 4 + q, q, True, q < 2)
            h_low(SLOT_TILES - 1, 1)

            def combine(t, q):
                p = q % 2
                v.wait_ge(sm[f"y_in{q}"], 4 * (t - q) + 16)
                V.scalar_tensor_tensor(out=y1[:, p, :], in0=yg[:, q, 0, :], scalar=w_choice[:, 0, bass.ds(t, 1)], in1=xt(t),
                                       op0=ALU.mult, op1=ALU.add).then_inc(sm["y1_ready"], 1)
                v.wait_ge(sm["y1_ready"], t + 1)
                wait(v, sm[f"stored{q}"], 4 * (t - q))
                V.scalar_tensor_tensor(out=y2[:, q, :], in0=yg[:, q, 1, :], scalar=w_choice[:, 1, bass.ds(t, 1)], in1=y1[:, p, :],
                                       op0=ALU.mult, op1=ALU.add).then_inc(sm["y_ready"], 1)

            for t in range(4):
                combine(t, t)
            with v.Fori(1, TILES // 4) as quad:
                t = 4 * quad
                for q in range(4):
                    combine(t + q, q)


def kernel(**inputs):
    import concourse.bacc as _bacc
    from concourse import mybir as _mybir
    from concourse.bass_utils import run_bass_kernel_spmd as _run

    i = {k: np.asarray(v) for k, v in inputs.items()}

    def chunks(w, c=KC):
        return np.ascontiguousarray(w.reshape(c, w.shape[0] // c, w.shape[1]).transpose(1, 0, 2))

    def experts(w, c):
        return np.ascontiguousarray(w.reshape(NE, c, w.shape[1] // c, w.shape[2]).transpose(2, 0, 1, 3))

    pos = np.arange(P)
    slopes = (2.0 ** (-8.0 / HEADS * np.arange(1, HEADS + 1))).astype(np.float32)
    order = [c * 8 + j * 2 + h for j in range(4) for c in range(2) for h in range(2)]
    rel = (np.arange(S)[None, :] - (pos % S)[:, None]).astype(np.float32)
    alibi = slopes[order][None, :, None] * rel[:, None, :]
    w_ffn = np.zeros((P, W_ALL), np.float32)
    w_ffn[:, W_GU:W_DOWN] = experts(np.concatenate([i["L0_ffn_w_gate"], i["L0_ffn_w_up"]], 2), KC).reshape(P, -1)
    w_ffn[:HC, W_DOWN:W_SHGATE] = experts(i["L0_ffn_w_down"], 2).reshape(HC, -1)
    w_ffn[:, W_SHGATE:W_SHUP] = chunks(i["L0_ffn_shw_gate"]).reshape(P, -1)
    w_ffn[:, W_SHUP:W_SHDOWN] = chunks(i["L0_ffn_shw_up"]).reshape(P, -1)
    w_ffn[:, W_SHDOWN:W_SHDOWN + 2 * D] = chunks(i["L0_ffn_shw_down"][:2 * P]).reshape(P, -1)
    w_ffn[:HS_LAST, W_SHDOWN + 2 * D:W_END] = i["L0_ffn_shw_down"][2 * P:]
    arrays = {
        "x": i["x"], "ctx": i["ctx_2048"], "mask": i["mask_BxS2_bf1"].view(np.uint8),
        "ident": np.eye(P, dtype=np.float32),
        "own_head": (pos[:, None] // DH == np.arange(HALF)[None, :]).astype(np.float32),
        "block_mask": (pos[:, None] // DH == pos[None, :] // DH).astype(np.float32),
        "row_head": ((pos[:, None] % 32) // DH == np.arange(2)[None, :]).astype(np.float32),
        "row_half": (pos[:, None] // S == np.arange(2)[None, :]).astype(np.float32),
        "alibi": np.ascontiguousarray(alibi.reshape(P, HEADS * S)),
        "out_rows": (2 * (np.arange(TILES)[None, :, None] * P + pos[:, None, None]) + np.arange(2) + SPARE).astype(np.float32),
        "spare_rows": (np.arange(SLOT_TILES)[None, :] * P + pos[:, None]).astype(np.float32),
        "rev8": np.tile(NE - np.arange(NE, dtype=np.float32), (P, 1)),
        "not_first": np.tile((np.arange(NE * TILES) % TILES > 0).astype(np.float32), (P, 1)),
        "iota_slot": np.arange(SLOT_TILES, dtype=np.float32)[None],
        "before": (pos[:, None] < pos[None, :]).astype(np.float32),
        "wq": chunks(i["L0_attn_wq"].T), "wkv": chunks(np.concatenate([i["L0_attn_wk"].T, i["L0_attn_wv"].T], 1)),
        "wo": chunks(i["L0_attn_wo"].T),
        "bq": np.ascontiguousarray(i["L0_attn_bq"].reshape(KC, P).T),
        "bkv": np.concatenate([i["L0_attn_bk"], i["L0_attn_bv"]]), "bo": i["L0_attn_bo"],
        "xwq": chunks(i["L0_xattn_Wq"]), "xwk": chunks(i["L0_xattn_Wk"]), "xwv": chunks(i["L0_xattn_Wv"]),
        "xwo": chunks(i["L0_xattn_Wo"]),
        "w_route": chunks(np.concatenate([i["L0_ffn_gate_w"].T, i["L0_ffn_shgate_w"][:, None]], 1)),
        "w_ffn": w_ffn,
    }
    nc = _bacc.Bacc("TRN2", target_bir_lowering=False, num_devices=1)
    args, feeds = {}, {}
    for name, arr in arrays.items():
        feeds[f"in_{name}_dram"] = arr
        args[name] = nc.dram_tensor(f"in_{name}_dram", arr.shape, _mybir.dt.from_np(arr.dtype), kind="ExternalInput").ap()
    out = nc.dram_tensor("out_0_dram", (B, S, D), F32, kind="ExternalOutput").ap()
    build(nc, args, out)
    r = _run(nc, [feeds], core_ids=[0])
    return r.results[0]["out_0_dram"]
```
